# Optimizing a Trainium2 kernel written in Bass

```python
import numpy as np
import jax
import jax.numpy as jnp

def _softmax(x, axis=-1):
    return jax.nn.softmax(x, axis=axis)

def _gelu(x):
    return jax.nn.gelu(x, approximate=True)

def _silu(x):
    return jax.nn.silu(x)

def _sigmoid(x):
    return jax.nn.sigmoid(x)

def _layernorm(x, axis=-1, eps=1e-05):
    m = jnp.mean(x, axis=axis, keepdims=True)
    v = jnp.var(x, axis=axis, keepdims=True)
    return (x - m) / jnp.sqrt(v + eps)

def _scatter_add(tgt, idx, src, axis=0):
    return tgt.at[idx].add(src)

def _segment_sum(src, seg, n):
    return jax.ops.segment_sum(src, seg, n)
kernel_name = 'mk_gps_d1_gnn_r8_47b6bc'

def setup_inputs(seed: int=0):
    np.random.seed(seed)
    _w = jnp.asarray

    def _rec_inputs():
        import jax
        import jax.numpy as jnp
        _gk = jax.random.key(seed)
        x = -0.0003713 + 1 * jax.random.normal(jax.random.fold_in(_gk, 1), (12500, 256), jnp.float32)
        _s = jax.random.randint(jax.random.fold_in(_gk, 2), (100000,), 0, 12500, jnp.int32)
        _d = jax.random.randint(jax.random.fold_in(_gk, 3), (100000,), 0, 12500, jnp.int32)
        _loop = jnp.arange(12500, dtype=jnp.int32)
        src = jnp.concatenate([_s, _d, _loop])
        dst = jnp.concatenate([_d, _s, _loop])
        _o = jnp.argsort(dst, stable=True)
        src = src[_o]
        dst = dst[_o]
        return (x, src, dst)
    x, src, dst = _rec_inputs()

    def _L0_gnn_setup():
        import jax, jax.numpy as jnp
        import numpy as np
        NEG_SLOPE = 0.2
        EPS = 1e-08
        N, E, IN_F, OUT_F, H = (6250, 100000, 256, 32, 8)
        key = jax.random.key(seed)
        k1, k2, k3, k4, k5 = jax.random.split(key, 5)
        x = jax.random.normal(k1, (N, IN_F), dtype=jnp.float32)
        edge_index = jax.random.randint(k2, (2, E), 0, N, dtype=jnp.int32)
        bw = float(np.sqrt(6.0 / (IN_F + OUT_F)))
        W = jax.random.uniform(k3, (H, IN_F, OUT_F), minval=-bw, maxval=bw, dtype=jnp.float32)
        ba = float(np.sqrt(6.0 / (OUT_F + 1)))
        a_src = jax.random.uniform(k4, (H, OUT_F), minval=-ba, maxval=ba, dtype=jnp.float32)
        a_dst = jax.random.uniform(k5, (H, OUT_F), minval=-ba, maxval=ba, dtype=jnp.float32)
        return {'x': x, 'edge_index': edge_index, 'W': W, 'a_src': a_src, 'a_dst': a_dst}
    _L0_gnn_all = _L0_gnn_setup()
    _L0_gnn_in = {k: v for k, v in _L0_gnn_all.items() if k in ('W', 'a_src', 'a_dst')}
    del _L0_gnn_all

    def _L0_mix_setup():
        import jax, jax.numpy as jnp
        import numpy as np
        DIM = 256
        HEADS = 4
        HEAD_DIM = DIM // HEADS
        MLP_HIDDEN = DIM * 3
        B, N = (8, 512)
        EPS = 1e-05

        def _layernorm(x, g, b):
            mu = jnp.mean(x, axis=-1, keepdims=True)
            var = jnp.mean(jnp.square(x - mu), axis=-1, keepdims=True)
            return (x - mu) * jax.lax.rsqrt(var + EPS) * g + b
        key = jax.random.key(seed)
        ks = jax.random.split(key, 8)
        s = 0.02
        return {'x': jax.random.normal(ks[0], (B, N, DIM), dtype=jnp.float32), 'w_qkv': jax.random.normal(ks[1], (DIM, 3 * DIM), dtype=jnp.float32) * s, 'b_qkv': jnp.zeros((3 * DIM,), dtype=jnp.float32), 'norm_g': jnp.ones((DIM,), dtype=jnp.float32), 'norm_b': jnp.zeros((DIM,), dtype=jnp.float32), 'w_fc1': jax.random.normal(ks[2], (DIM, MLP_HIDDEN), dtype=jnp.float32) * s, 'b_fc1': jnp.zeros((MLP_HIDDEN,), dtype=jnp.float32), 'w_fc2': jax.random.normal(ks[3], (MLP_HIDDEN, DIM), dtype=jnp.float32) * s, 'b_fc2': jnp.zeros((DIM,), dtype=jnp.float32)}
    _L0_mix_all = _L0_mix_setup()
    _L0_mix_in = {k: v for k, v in _L0_mix_all.items() if k in ('w_qkv', 'b_qkv', 'norm_g', 'norm_b', 'w_fc1', 'b_fc1', 'w_fc2', 'b_fc2')}
    del _L0_mix_all

    def _L0_ffn_setup():
        import jax, jax.numpy as jnp
        import numpy as np
        B, T, D, H, E = (16, 512, 256, 512, 8)
        key = jax.random.key(seed)
        ks = jax.random.split(key, 5)
        x = jax.random.normal(ks[0], (B, T, D), dtype=jnp.float32)
        gate_w = jax.random.normal(ks[1], (D, E), dtype=jnp.float32) * 0.02
        gate_b = jnp.zeros((E,), dtype=jnp.float32)
        W1 = jax.random.normal(ks[2], (E, D, H), dtype=jnp.float32) * 0.02
        b1 = jnp.zeros((E, H), dtype=jnp.float32)
        W2 = jax.random.normal(ks[3], (E, H, D), dtype=jnp.float32) * 0.02
        b2 = jnp.zeros((E, D), dtype=jnp.float32)
        return {'x': x, 'gate_w': gate_w, 'gate_b': gate_b, 'W1': W1, 'b1': b1, 'W2': W2, 'b2': b2}
    _L0_ffn_all = _L0_ffn_setup()
    _L0_ffn_in = {k: v for k, v in _L0_ffn_all.items() if k in ('gate_w', 'gate_b', 'W1', 'b1', 'W2', 'b2')}
    del _L0_ffn_all
    return {'x': x, 'src': src, 'dst': dst, 'L0_gnn_W': _L0_gnn_in['W'], 'L0_gnn_a_src': _L0_gnn_in['a_src'], 'L0_gnn_a_dst': _L0_gnn_in['a_dst'], 'L0_mix_w_qkv': _L0_mix_in['w_qkv'], 'L0_mix_b_qkv': _L0_mix_in['b_qkv'], 'L0_mix_norm_g': _L0_mix_in['norm_g'], 'L0_mix_norm_b': _L0_mix_in['norm_b'], 'L0_mix_w_fc1': _L0_mix_in['w_fc1'], 'L0_mix_b_fc1': _L0_mix_in['b_fc1'], 'L0_mix_w_fc2': _L0_mix_in['w_fc2'], 'L0_mix_b_fc2': _L0_mix_in['b_fc2'], 'L0_ffn_gate_w': _L0_ffn_in['gate_w'], 'L0_ffn_gate_b': _L0_ffn_in['gate_b'], 'L0_ffn_W1': _L0_ffn_in['W1'], 'L0_ffn_b1': _L0_ffn_in['b1'], 'L0_ffn_W2': _L0_ffn_in['W2'], 'L0_ffn_b2': _L0_ffn_in['b2']}

def reference(x, src, dst, L0_gnn_W, L0_gnn_a_src, L0_gnn_a_dst, L0_mix_w_qkv, L0_mix_b_qkv, L0_mix_norm_g, L0_mix_norm_b, L0_mix_w_fc1, L0_mix_b_fc1, L0_mix_w_fc2, L0_mix_b_fc2, L0_ffn_gate_w, L0_ffn_gate_b, L0_ffn_W1, L0_ffn_b1, L0_ffn_W2, L0_ffn_b2):
    import jax
    import jax.numpy as jnp

    def _L0_gnn_ref(x, edge_index, W, a_src, a_dst):
        import jax, jax.numpy as jnp
        import numpy as np
        NEG_SLOPE = 0.2
        EPS = 1e-08
        N, E, IN_F, OUT_F, H = (6250, 100000, 256, 32, 8)
        num_nodes = x.shape[0]
        src, dst = (edge_index[0], edge_index[1])
        h = jnp.einsum('ni,hif->hnf', x, W)
        s_src = jnp.einsum('hnf,hf->hn', h, a_src)
        s_dst = jnp.einsum('hnf,hf->hn', h, a_dst)
        ea = (s_src[:, src] + s_dst[:, dst]).T
        ea = jnp.where(ea > 0, ea, NEG_SLOPE * ea)
        m = jax.ops.segment_max(ea, dst, num_segments=num_nodes)
        ea = jnp.exp(ea - m[dst])
        s = jax.ops.segment_sum(ea, dst, num_segments=num_nodes)
        ea = ea / (s[dst] + EPS)
        hn = jnp.transpose(h, (1, 0, 2))
        wf = hn[src] * ea[:, :, None]
        out = jax.ops.segment_sum(wf, dst, num_segments=num_nodes)
        return out.reshape(num_nodes, -1)

    def _L0_mix_ref(x, w_qkv, b_qkv, norm_g, norm_b, w_fc1, b_fc1, w_fc2, b_fc2):
        import jax, jax.numpy as jnp
        import numpy as np
        DIM = 256
        HEADS = 4
        HEAD_DIM = DIM // HEADS
        MLP_HIDDEN = DIM * 3
        B, N = (8, 512)
        EPS = 1e-05

        def _layernorm(x, g, b):
            mu = jnp.mean(x, axis=-1, keepdims=True)
            var = jnp.mean(jnp.square(x - mu), axis=-1, keepdims=True)
            return (x - mu) * jax.lax.rsqrt(var + EPS) * g + b
        Bx, Nx, C = x.shape
        scale = HEAD_DIM ** (-0.5)
        qkv = (x @ w_qkv + b_qkv).reshape(Bx, Nx, 3, HEADS, HEAD_DIM)
        qkv = jnp.transpose(qkv, (2, 0, 3, 1, 4))
        q, k, v = (qkv[0], qkv[1], qkv[2])
        k = k * scale
        attn = jnp.einsum('bhnd,bhne->bhde', k, v)
        attn = jax.nn.softmax(attn, axis=-1)
        xf = jnp.einsum('bhde,bhne->bhnd', attn, q)
        xf = jnp.transpose(xf, (0, 2, 1, 3)).reshape(Bx, Nx, C)
        x = x + xf
        h = _layernorm(x, norm_g, norm_b)
        h = jax.nn.gelu(h @ w_fc1 + b_fc1, approximate=False) @ w_fc2 + b_fc2
        return x + h

    def _L0_ffn_ref(x, gate_w, gate_b, W1, b1, W2, b2):
        import jax, jax.numpy as jnp
        import numpy as np
        B, T, D, H, E = (16, 512, 256, 512, 8)
        Bb, Tt, Dd = x.shape
        Ee = gate_w.shape[1]
        xf = x.reshape(-1, Dd)
        N = xf.shape[0]
        logits = xf @ gate_w + gate_b
        probs = jax.nn.softmax(logits, axis=-1)
        top2_vals, top2_idx = jax.lax.top_k(probs, 2)
        cw = jnp.zeros((N, Ee), dtype=xf.dtype).at[jnp.arange(N)[:, None], top2_idx].add(top2_vals)

        def step(acc, params):
            w1, bb1, w2, bb2, we = params
            h = jax.nn.gelu(xf @ w1 + bb1, approximate=False)
            y = h @ w2 + bb2
            return (acc + we[:, None] * y, None)
        out, _ = jax.lax.scan(step, jnp.zeros_like(xf), (W1, b1, W2, b2, cw.T))
        return out.reshape(Bb, Tt, Dd)
    edge_index = jnp.stack([src, dst])
    xn = _layernorm(x, axis=-1)
    x = x + _L0_gnn_ref(xn, edge_index, L0_gnn_W, L0_gnn_a_src, L0_gnn_a_dst) + _L0_mix_ref(xn[None], L0_mix_w_qkv, L0_mix_b_qkv, L0_mix_norm_g, L0_mix_norm_b, L0_mix_w_fc1, L0_mix_b_fc1, L0_mix_w_fc2, L0_mix_b_fc2)[0]
    x = x + _L0_ffn_ref(_layernorm(x, axis=-1)[None], L0_ffn_gate_w, L0_ffn_gate_b, L0_ffn_W1, L0_ffn_b1, L0_ffn_W2, L0_ffn_b2)[0]
    return x

_drawn_inputs = setup_inputs


def setup_inputs(seed=0):
    import zlib

    import numpy as np

    out = dict(_drawn_inputs(seed))
    spreads = {'L0_mix_b_qkv': (0.0, 0.1),
     'L0_mix_norm_g': (1.0, 0.6),
     'L0_mix_norm_b': (0.0, 0.8),
     'L0_mix_b_fc1': (0.0, 0.584),
     'L0_mix_b_fc2': (0.0, 0.1),
     'L0_ffn_gate_b': (0.0, 0.8),
     'L0_ffn_b1': (0.0, 0.8),
     'L0_ffn_b2': (0.0, 0.667)}
    factors = {'L0_ffn_gate_w': 4.28, 'L0_ffn_W1': 6.075, 'L0_ffn_W2': 5.688}
    for name, (base, spread) in spreads.items():
        noise = np.random.default_rng([zlib.crc32(name.encode()), seed]).standard_normal(out[name].shape)
        drawn = base * np.exp(spread * noise) if base else spread * noise
        out[name] = jnp.asarray(drawn.astype(out[name].dtype))
    for name, factor in factors.items():
        out[name] = (out[name] * factor).astype(out[name].dtype)
    return out
```

```python
import numpy as np

import concourse.bass as bass
from concourse import mybir

F32 = mybir.dt.float32
I32 = mybir.dt.int32
ALU = mybir.AluOpType
ACT = mybir.ActivationFunctionType
AX = mybir.AxisListType.X

P = 128
BIG = 1.0e30
LN_EPS = 1e-5
SEG_EPS = 1e-8
SLOPE = 0.2

N_NODES = 12500
N_EDGES = 212500
D = 256
KD = D // P
TILES = -(-N_NODES // P)
N_PAD = TILES * P
ST = 4
SUPERS = [(s, min(ST, TILES - s)) for s in range(0, TILES, ST)]
GH, GF = 8, 32
ROW = D + 2 * GH
CB = 16
GROUPS = -(-N_EDGES // (P * CB))
BLOCKS = -(-GROUPS * CB // P)
CHUNKS = BLOCKS * P
NEAR = 32
FAR = CHUNKS * NEAR
FRAGS = FAR + N_NODES + 1 + P
NOT_WIDE = FRAGS - (P - NEAR)
MIX_HEADS, MIX_HD = 4, 64
MLP = 768
MT = MLP // P
EXPERTS, HID = 8, 512
HT = HID // P


class Lane:

    def __init__(self, nc, engine, name):
        self.engine, self.sem, self.count, self.seen = engine, nc.alloc_semaphore(name), 0, {}

    def wait(self, *tokens):
        for t in tokens:
            if t is None:
                continue
            if isinstance(t, list):
                self.wait(*t)
                continue
            sem, value, key = t
            if self.seen.get(key, 0) < value:
                self.engine.wait_ge(sem, value)
                self.seen[key] = value

    def run(self, issue, *tokens):
        self.wait(*tokens)
        issue(self.engine).then_inc(self.sem, 1)
        self.count += 1
        return (self.sem, self.count, id(self))

    def last(self):
        return (self.sem, self.count, id(self)) if self.count else None


class Slot:

    def __init__(self, nc, name):
        self.sem, self.count = nc.alloc_semaphore(name), 0

    def dma(self, lane, issue, *tokens):
        lane.wait(*tokens)
        issue(lane.engine).then_inc(self.sem, 16)
        self.count += 16
        return (self.sem, self.count, id(self))

    def last(self):
        return (self.sem, self.count, id(self)) if self.count else None


class Core:
    def __init__(self, nc):
        self.nc = nc
        self.pe = Lane(nc, nc.tensor, "pe_done")
        self.dve = Lane(nc, nc.vector, "dve_done")
        self.act = Lane(nc, nc.scalar, "act_done")
        self.pool = Lane(nc, nc.gpsimd, "pool_done")
        self.sp = Lane(nc, nc.sync, "sp_done")
        self.slots = []
        self.banks = [nc.alloc_psum_tensor(f"bank{i}", [P, 512], F32) for i in range(8)]

    def slot(self, name):
        self.slots.append(Slot(self.nc, name))
        return self.slots[-1]

    def fence(self):
        done = [l.last() for l in (self.pe, self.dve, self.act, self.pool)] + [s.last() for s in self.slots]
        for lane in (self.pe, self.dve, self.act, self.pool, self.sp):
            lane.wait(*done)


def rsqrt(c, var, out, tmp, ready):
    v = c.dve
    t = v.run(lambda e: e.tensor_single_scalar(tmp.bitcast(I32), var.bitcast(I32), 1, ALU.logical_shift_right), ready)
    t = v.run(lambda e: e.tensor_scalar(out.bitcast(I32), tmp.bitcast(I32), -1.0, float(0x5F3759DF), ALU.mult, ALU.add), t)
    for _ in range(3):
        t = v.run(lambda e: e.tensor_tensor(tmp, out, out, ALU.mult), t)
        t = v.run(lambda e: e.tensor_tensor(tmp, tmp, var, ALU.mult), t)
        t = v.run(lambda e: e.tensor_scalar(tmp, tmp, -0.5, 1.5, ALU.mult, ALU.add), t)
        t = v.run(lambda e: e.tensor_tensor(out, out, tmp, ALU.mult), t)
    return t


def layernorm(c, x, out, stats, n, ready, free):
    v = c.dve
    v.wait(*ready)
    t = None
    for i in range(n):
        t = v.run(lambda e, i=i: e.bn_stats(stats[:, i, 0:6], x[:, i, :]))
    t = v.run(lambda e: e.engine_nop(), t) if False else t
    for i in range(n):
        t = v.run(lambda e, i=i: e.bn_aggr(stats[:, i, 6:8], stats[:, i, 0:6]), t)
    var = stats[:, 0:n, 8]
    t = v.run(lambda e: e.tensor_scalar(var, stats[:, 0:n, 7], LN_EPS, None, ALU.add), t)
    t = rsqrt(c, var, stats[:, 0:n, 9], stats[:, 0:n, 10], t)
    v.wait(*free)
    for i in range(n):
        t = v.run(lambda e, i=i: e.tensor_scalar(out[:, i, 0:D], x[:, i, :], stats[:, i, 6:7], stats[:, i, 9:10],
                                                 ALU.subtract, ALU.mult), t)
    return t


def turn(c, src, dst, n, banks, ready, bank_free, dst_free):
    outs = []
    for k in range(KD):
        c.pe.wait(ready, bank_free[k])
        for i in range(n):
            t = c.pe.run(lambda e, i=i: e.transpose(banks[k][:, i * P:(i + 1) * P], src[:, i, k * P:(k + 1) * P],
                                                    c.ident[:, :]))
        o = c.act.run(lambda e: e.activation(dst[:, k, 0:n * P], banks[k][:, 0:n * P], ACT.Copy), t, dst_free)
        bank_free[k] = o
        outs.append(o)
    return outs


def constants(c):
    nc = c.nc
    c.ident = nc.alloc_sbuf_tensor("ident", [P, P], F32)
    c.ramp = nc.alloc_sbuf_tensor("ramp", [P, P], F32)
    c.ones = nc.alloc_sbuf_tensor("ones", [P, P], F32)
    c.headsel = nc.alloc_sbuf_tensor("headsel", [GH, D], F32)
    p = c.pool
    t = p.run(lambda e: e.memset(c.ident[:, :], 0.0))
    t = p.run(lambda e: e.affine_select(out=c.ident[:, :], in_=c.ident[:, :], compare_op=ALU.not_equal, fill=1.0,
                                        base=0, pattern=[[-1, P]], channel_multiplier=1), t)
    p.run(lambda e: e.iota(c.ramp[:, :], pattern=[[1, P]], base=0, channel_multiplier=0,
                           allow_small_or_imprecise_dtypes=True))
    p.run(lambda e: e.memset(c.ones[:, :], 1.0))
    t = p.run(lambda e: e.memset(c.headsel[:, :], 0.0))
    v = c.headsel[:, :].rearrange("p (h f) -> p h f", f=GF)
    p.run(lambda e: e.affine_select(out=v, in_=v, compare_op=ALU.not_equal, fill=1.0, base=0,
                                    pattern=[[-1, GH], [0, GF]], channel_multiplier=1), t)


def nodes_stage(c, x, frag, table, xn_d, xnt_d, gnn_w, a_src, a_dst, gram):
    nc = c.nc
    A = nc.alloc_sbuf_tensor
    wcat = A("wcat", [P, KD, ROW], F32)
    avec = A("avec", [P, 2, D], F32)
    wtmp = A("wtmp", [P, D], F32)
    xs = [A(f"xs{b}", [P, ST, D], F32) for b in range(2)]
    xn = [A(f"xn{b}", [P, ST, D + 1], F32) for b in range(2)]
    xt = [A(f"xt{b}", [P, KD, ST * P], F32) for b in range(2)]
    hr = [A(f"hr{b}", [P, ST, ROW], F32) for b in range(2)]
    st = A("st_a", [P, ST, 16], F32)
    s_w, s_x = c.slot("a_w"), [c.slot(f"a_x{b}") for b in range(2)]
    s_xn, s_xt, s_h = ([c.slot(f"a_{n}{b}") for b in range(2)] for n in ("xn", "xt", "h"))

    for k in range(KD):
        w = s_w.dma(c.sp, lambda e: e.dma_start(wcat[:, k, 0:D].rearrange("p (h f) -> p h f", f=GF),
                                                gnn_w[:, k * P:(k + 1) * P, :].rearrange("h i f -> i h f")))
    for j, a in enumerate((a_src, a_dst)):
        w = s_w.dma(c.sp, lambda e: e.dma_start(avec[:, j, :], a.rearrange("h f -> (h f)").partition_broadcast(P)))
    t = w
    for k in range(KD):
        for j in range(2):
            t = c.dve.run(lambda e: e.tensor_tensor(wtmp[:, :], wcat[:, k, 0:D], avec[:, j, :], ALU.mult), t)
            t = c.dve.run(lambda e: e.tensor_reduce(wcat[:, k, D + GH * j:D + GH * (j + 1)],
                                                    wtmp[:, :].rearrange("p (h f) -> p h f", f=GF), AX, ALU.add), t)
    scores_ready = t
    for b in range(2):
        c.dve.run(lambda e: e.memset(xn[b][:, :, D:D + 1], 1.0))
    zero = A("zero", [P, ROW], F32)
    t = c.dve.run(lambda e: e.memset(zero[:, :], 0.0))
    s_z = c.slot("a_zero")
    for r in range(FAR, FRAGS, P):
        n = min(P, FRAGS - r)
        s_z.dma(c.sp, lambda e: e.dma_start(frag[r:r + n, :], zero[0:n, :]), t)

    load, xs_free = [None, None], [None, None]
    tp_free, h_free = [None, None], [None, None]
    xn_used, xt_used, h_out = [None, None], [None, None], [None, None]
    gram_banks = (c.banks[4], c.banks[5])
    g_done = None

    def fetch(k):
        s, n = SUPERS[k]
        b = k % 2
        load[b] = s_x[b].dma(c.sp, lambda e: e.dma_start(
            xs[b][:, 0:n, :], x[s * P:(s + n) * P, :].rearrange("(t p) d -> p t d", p=P)), xs_free[b])

    fetch(0)
    hcount = 0
    for k, (s, n) in enumerate(SUPERS):
        b = k % 2
        if k + 1 < len(SUPERS):
            fetch(k + 1)
        normed = layernorm(c, xs[b], xn[b], st, n, [load[b]], [xn_used[b], s_xn[b].last()])
        xs_free[b] = normed
        s_xn[b].dma(c.sp, lambda e: e.dma_start(
            xn_d[s * P:(s + n) * P, :].rearrange("(t p) d -> p t d", p=P), xn[b][:, 0:n, 0:D]), normed)
        turned = turn(c, xn[b], xt[b], n, c.banks[0:2], normed, tp_free, [xt_used[b], s_xt[b].last()])
        s_xt[b].dma(c.sp, lambda e: e.dma_start(
            xnt_d.rearrange("(k p) n -> p k n", p=P)[:, :, s * P:(s + n) * P], xt[b][:, :, 0:n * P]), turned)
        for i in range(n):
            hb = hcount % 2
            bank = c.banks[2 + hb]
            c.pe.wait(turned, scores_ready, h_free[hb])
            for kk in range(KD):
                t = c.pe.run(lambda e: e.matmul(bank[:, 0:ROW], xt[b][:, kk, i * P:(i + 1) * P], wcat[:, kk, :],
                                                start=(kk == 0), stop=(kk == KD - 1)))
            h_free[hb] = c.act.run(lambda e: e.activation(hr[b][:, i, :], bank[:, 0:ROW], ACT.Copy), t, s_h[b].last())
            hcount += 1
        xt_used[b] = t
        s_h[b].dma(c.sp, lambda e: e.dma_start(
            table[s * P:(s + n) * P, :].rearrange("(t p) d -> p t d", p=P), hr[b][:, 0:n, :]), h_free[hb])
        for i in range(n):
            for m in range(KD):
                g_done = c.pe.run(lambda e: e.matmul(
                    gram_banks[m][:, 0:D + 1], xn[b][:, i, m * P:(m + 1) * P], xn[b][:, i, :],
                    start=(s + i == 0), stop=(s + i == TILES - 1)))
        xn_used[b] = g_done
    for m in range(KD):
        c.dve.run(lambda e: e.tensor_copy(gram[:, m, :], gram_banks[m][:, 0:D + 1]), g_done)


def mix_weights_stage(c, gram, wqkv, bqkv, wqa, bqa):
    nc = c.nc
    A = nc.alloc_sbuf_tensor
    w = A("wqkv_s", [P, KD, 3 * D], F32)
    brow = A("bqkv_row", [1, 3 * D], F32)
    bqc = A("bq_col", [P, KD], F32)
    u = A("mix_u", [P, KD, D], F32)
    srow = A("mix_srow", [1, D], F32)
    rrow = A("mix_rrow", [1, D], F32)
    att = A("mix_att", [P, KD, P], F32)
    attt = A("mix_attt", [P, KD, P], F32)
    wqt = A("mix_wqt", [P, KD, D], F32)
    red = A("mix_red", [P, 8], F32)
    s = c.slot("mix_in")
    s.dma(c.sp, lambda e: e.dma_start(w[:, :, :], wqkv.rearrange("(k p) n -> p k n", p=P)))
    s.dma(c.sp, lambda e: e.dma_start(brow[:, :], bqkv.unsqueeze(0)))
    ready = s.dma(c.sp, lambda e: e.dma_start(bqc[:, :], bqkv[0:D].rearrange("(k p) -> p k", p=P)))
    pe, v, bk = c.pe, c.dve, c.banks
    pe.wait(ready)
    for m in range(KD):
        t = pe.run(lambda e: e.transpose(bk[0][0:1, m * P:(m + 1) * P], gram[:, m, D:D + 1], c.ident[:, :]))
    t = v.run(lambda e: e.tensor_copy(srow[:, :], bk[0][0:1, 0:D]), t)
    for m in range(KD):
        pe.wait(t)
        for k in range(KD):
            pe.run(lambda e: e.matmul(bk[1 + m][:, 0:D], gram[:, k, m * P:(m + 1) * P], w[:, k, 2 * D:3 * D],
                                      start=(k == 0), stop=False))
        q = pe.run(lambda e: e.matmul(bk[1 + m][:, 0:D], srow[0:1, m * P:(m + 1) * P], brow[0:1, 2 * D:3 * D],
                                      start=False, stop=True))
        v.run(lambda e: e.tensor_copy(u[:, m, :], bk[1 + m][:, 0:D]), q)
    for k in range(KD):
        q = pe.run(lambda e: e.matmul(bk[3][0:1, 0:D], gram[:, k, D:D + 1], w[:, k, 2 * D:3 * D],
                                      start=(k == 0), stop=(k == KD - 1)))
    t = v.run(lambda e: e.scalar_tensor_tensor(out=rrow[:, :], in0=brow[0:1, 2 * D:3 * D], scalar=float(N_NODES),
                                               in1=bk[3][0:1, 0:D], op0=ALU.mult, op1=ALU.add), q)
    t0 = v.run(lambda e: e.memset(att[:, :, :], 0.0))
    for m in range(KD):
        pe.wait(t)
        for k in range(KD):
            pe.run(lambda e: e.matmul(bk[4 + m][:, 0:D], w[:, k, D + m * P:D + (m + 1) * P], u[:, k, :],
                                      start=(k == 0), stop=False))
        q = pe.run(lambda e: e.matmul(bk[4 + m][:, 0:D], brow[0:1, D + m * P:D + (m + 1) * P], rrow[:, :],
                                      start=False, stop=True))
        scale = float(MIX_HD) ** -0.5
        for hh in range(2):
            r = slice(hh * MIX_HD, (hh + 1) * MIX_HD)
            col = (2 * m + hh) * MIX_HD
            sc = bk[4 + m][r, col:col + MIX_HD]
            o = att[r, m, hh * MIX_HD:(hh + 1) * MIX_HD]
            x = v.run(lambda e: e.tensor_reduce(red[r, 0:1], sc, AX, ALU.max), q, t0)
            x = v.run(lambda e: e.tensor_scalar(red[r, 1:2], red[r, 0:1], -scale, None, ALU.mult), x)
            x = c.act.run(lambda e: e.activation(o, sc, ACT.Exp, bias=red[r, 1:2], scale=scale), x)
            x = v.run(lambda e: e.tensor_reduce(red[r, 2:3], o, AX, ALU.add), x)
            x = v.run(lambda e: e.reciprocal(red[r, 3:4], red[r, 2:3]), x)
            x = v.run(lambda e: e.tensor_scalar(o, o, red[r, 3:4], None, ALU.mult), x)
    for m in range(KD):
        q = pe.run(lambda e: e.transpose(bk[6][:, m * P:(m + 1) * P], att[:, m, :], c.ident[:, :]), x)
    x = v.run(lambda e: e.tensor_copy(attt[:, :, :], bk[6][:, 0:D].rearrange("p (m e) -> p m e", m=KD)), q)
    for m in range(KD):
        for i in range(KD):
            q = pe.run(lambda e: e.transpose(bk[7][:, m * D + i * P:m * D + (i + 1) * P], w[:, i, m * P:(m + 1) * P],
                                             c.ident[:, :]))
    x = v.run(lambda e: e.tensor_copy(wqt[:, :, :], bk[7][:, :].rearrange("p (m i) -> p m i", m=KD)), q)
    pe.wait(x)
    for i in range(KD):
        for m in range(KD):
            q = pe.run(lambda e: e.matmul(bk[i][:, m * P:(m + 1) * P], wqt[:, m, i * P:(i + 1) * P], attt[:, m, :],
                                          start=True, stop=True))
        v.run(lambda e: e.tensor_copy(wqa[:, i, :], bk[i][:, 0:D]), q)
    for m in range(KD):
        q = pe.run(lambda e: e.matmul(bk[2][0:1, m * P:(m + 1) * P], bqc[:, m:m + 1], attt[:, m, :],
                                      start=True, stop=True))
    v.run(lambda e: e.tensor_copy(bqa[:, :], bk[2][0:1, 0:D]), q)


def fragment_rows(c, q, node, out, n, ready):
    A = c.nc.alloc_sbuf_tensor
    qi, loc, ch, far, sel = (A(f"fr{n}_{i}", [P, n], dt) for i, dt in enumerate((I32, I32, I32, F32, F32)))
    v = c.dve
    t = v.run(lambda e: e.tensor_copy(qi[:, :], q[:, 0:n]), ready)
    t1 = v.run(lambda e: e.tensor_scalar(loc[:, :], qi[:, :], P - 1, None, ALU.bitwise_and), t)
    t = v.run(lambda e: e.tensor_scalar(ch[:, :], qi[:, :], 7, 5, ALU.logical_shift_right, ALU.logical_shift_left), t)
    t = v.run(lambda e: e.tensor_tensor(q[:, 0:n], ch[:, :], loc[:, :], ALU.add), t, t1)
    t2 = v.run(lambda e: e.tensor_scalar(sel[:, :], loc[:, :], float(NEAR), None, ALU.is_ge), t1)
    t = v.run(lambda e: e.scalar_tensor_tensor(out=far[:, :], in0=node, scalar=float(FAR), in1=q[:, 0:n], op0=ALU.add,
                                               op1=ALU.subtract), t)
    t = v.run(lambda e: e.tensor_tensor(far[:, :], far[:, :], sel[:, :], ALU.mult), t, t2)
    return v.run(lambda e: e.tensor_tensor(out[:, :], far[:, :], q[:, 0:n], ALU.add), t)


def index_stage(c, dst, src, table, rows_d, sdst_d, g):
    nc = c.nc
    A = nc.alloc_sbuf_tensor
    di = A("dst_i", [P, BLOCKS, P], I32)
    si = A("src_i", [P, BLOCKS, P], I32)
    fl = A("dfl_f", [P, 2, BLOCKS], F32)
    fli = A("dfl_i", [P, 2, BLOCKS], I32)
    tmp = [A(f"ix_tmp{b}", [P, P], F32) for b in range(2)]
    junk = A("ix_rows", [P, 2 * BLOCKS, ROW], F32)
    sd = A("ix_sd", [P, 2, BLOCKS, GH], F32)
    sdg = A("ix_sdg", [GROUPS, 2, P], F32)
    dkey = A("ix_key", [P, CHUNKS], F32)
    cnum = A("ix_cnum", [P, CHUNKS], F32)
    wide = A("ix_cmp", [P, CHUNKS], F32)
    nid = A("ix_nid", [P, TILES], F32)
    nf = A("ix_nf", [P, TILES], F32)
    cn = A("ix_cn", [P, BLOCKS], F32)
    s1, s2, s3, s4, s5 = (c.slot(f"ix_{i}") for i in range(5))
    v, pe = c.dve, c.pe
    s1.dma(c.sp, lambda e: e.dma_start(di[:, :, :], dst.rearrange("(b c) e -> c b e", c=P)))
    t = s1.dma(c.sp, lambda e: e.dma_start(si[:, :, :], src.rearrange("(b c) e -> c b e", c=P)))
    for j, col in ((0, 0), (1, P - 1)):
        v.run(lambda e: e.tensor_copy(fl[:, j, :], di[:, :, col]), t)
        f = v.run(lambda e: e.tensor_copy(fli[:, j, :], di[:, :, col]), t)
    w = s2.dma(c.sp, lambda e: e.dma_start(rows_d.rearrange("j (b c) -> c j b", c=P), fl[:, :, :]), f)
    for j, to in ((0, g["dfb"]), (1, g["dlb"])):
        w2 = s3.dma(c.sp, lambda e: e.dma_start(to[:, :], rows_d[j].partition_broadcast(P)), w)
    free = [None, None]
    n = 0
    for b in range(BLOCKS):
        for what in range(2):
            u = n % 2
            if what == 0:
                t = v.run(lambda e: e.tensor_scalar(tmp[u][:, :], di[:, b, :], fl[:, 0, b:b + 1], None, ALU.subtract),
                          f, free[u])
            else:
                t = v.run(lambda e: e.tensor_copy(tmp[u][:, :], si[:, b, :]), free[u])
            t = pe.run(lambda e: e.transpose(c.banks[u][:, 0:P], tmp[u][:, :], c.ident[:, :]), t)
            to = (g["loc"], g["srcix"])[what]
            free[u] = v.run(lambda e: e.tensor_copy(to[:, b * P:(b + 1) * P], c.banks[u][:, 0:P]), t)
            n += 1
    for j in range(2):
        for b in range(BLOCKS):
            t = s4.dma(c.pool, lambda e: e.indirect_dma_start(
                out=junk[:, j * BLOCKS + b, :], out_offset=None, in_=table[:, :],
                in_offset=bass.IndirectOffsetOnAxis(ap=fli[:, j, b:b + 1], axis=0)), f)
    t = v.run(lambda e: e.tensor_copy(sd[:, :, :, :], junk[:, :, D + GH:ROW].rearrange("p (j b) h -> p j b h", j=2)), t)
    for j in range(2):
        t2 = s2.dma(c.sp, lambda e: e.dma_start(sdst_d[j].rearrange("(b c) h -> c b h", c=P), sd[:, j, :, :]), t)
    t = s5.dma(c.sp, lambda e: e.dma_start(sdg[:, :, :], sdst_d.rearrange("j (g c) h -> g j (c h)", c=CB)), t2)
    for j in range(2):
        t = pe.run(lambda e: e.transpose(c.banks[2 + j][:, 0:GROUPS], sdg[:, j, :], c.ident[0:GROUPS, 0:GROUPS]), t)
        v.run(lambda e: e.tensor_copy(g["sdedge"][:, j, :], c.banks[2 + j][:, 0:GROUPS]), t)
    t = c.pool.run(lambda e: e.iota(cn[:, :], pattern=[[P * P, BLOCKS]], base=0, channel_multiplier=P,
                                    allow_small_or_imprecise_dtypes=True))
    t = v.run(lambda e: e.tensor_tensor(cn[:, :], cn[:, :], fl[:, 1, :], ALU.add), t)
    t = v.run(lambda e: e.tensor_tensor(cn[:, :], cn[:, :], fl[:, 0, :], ALU.subtract), t)
    fragment_rows(c, cn, fl[:, 1, :], g["lastix"], BLOCKS, t)
    t = c.pool.run(lambda e: e.iota(cnum[:, :], pattern=[[P, CHUNKS]], base=0, channel_multiplier=0,
                                    allow_small_or_imprecise_dtypes=True))
    t = v.run(lambda e: e.tensor_tensor(cnum[:, :], cnum[:, :], g["dfb"][:, :], ALU.subtract), t, w2)
    v.run(lambda e: e.tensor_copy(dkey[:, 0:1], cnum[:, 0:1]), t)
    key = v.run(lambda e: e.tensor_tensor(dkey[:, 1:], cnum[:, 1:], cnum[:, 0:CHUNKS - 1], ALU.subtract), t)
    t = c.pool.run(lambda e: e.iota(nid[:, :], pattern=[[P, TILES]], base=0, channel_multiplier=1,
                                    allow_small_or_imprecise_dtypes=True))
    for i in range(TILES):
        t = v.run(lambda e: e.scalar_tensor_tensor(out=wide[:, :], in0=g["dfb"][:, :], scalar=nid[:, i:i + 1],
                                                   in1=dkey[:, :], op0=ALU.is_le, op1=ALU.mult,
                                                   accum_out=nf[:, i:i + 1]), t, key)
    t = v.run(lambda e: e.tensor_tensor(nf[:, :], nf[:, :], nid[:, :], ALU.add), t)
    fragment_rows(c, nf, nid[:, :], g["nodeix"], TILES, t)
    t = v.run(lambda e: e.tensor_tensor(wide[0:1, :], g["dlb"][0:1, :], g["dfb"][0:1, :], ALU.subtract), t)
    t = v.run(lambda e: e.tensor_scalar(wide[0:1, :], wide[0:1, :], float(NEAR), float(FRAGS), ALU.is_lt, ALU.mult), t)
    t = v.run(lambda e: e.tensor_tensor(wide[0:1, :], wide[0:1, :], g["dfb"][0:1, :], ALU.add), t)
    v.run(lambda e: e.tensor_scalar(g["far"][0:1, :], wide[0:1, :], float(N_NODES + 1), float(FAR + NEAR), ALU.min,
                                    ALU.add), t)


def edges_stage(c, dst, src, table, frag, g):
    nc = c.nc
    A = nc.alloc_sbuf_tensor
    NB = 3
    rows = [A(f"rows{b}", [P, CB, ROW], F32) for b in range(NB)]
    onehot = [A(f"onehot{b}", [P, CB, P], F32) for b in range(2)]
    fout = [A(f"fout{b}", [P, CB, ROW], F32) for b in range(2)]
    dsr = [A(f"dsr{b}", [P, 2, P], I32) for b in range(2)]
    sc_e = [A(f"sc_e{b}", [P, 2, P], F32) for b in range(2)]
    brk = A("brk", [P, P + 1], F32)
    neq = A("neq", [P, P + 1], F32)
    notself = A("notself", [P, P], F32)
    sdm, d1, d2, ea0, ea, mx1, mx, dlt, fm = (A(f"g_{n}", [P, P], F32) for n in (
        "sdm", "d1", "d2", "ea0", "ea", "mx1", "mx", "dlt", "fm"))
    wgt = A("g_w", [P, P], F32)
    we = [A(f"g_we{b}", [P, 2, P], F32) for b in range(2)]
    s_row = [c.slot(f"rows_in{b}") for b in range(NB)]
    s_ds = [c.slot(f"ds_in{b}") for b in range(2)]
    s_near = [c.slot(f"near_out{b}") for b in range(2)]
    s_far = [c.slot(f"far_out{b}") for b in range(2)]
    v, pe, act, pool, sp = c.dve, c.pe, c.act, c.pool, c.sp
    in_bank, out_bank, o_banks = c.banks[0], c.banks[1], c.banks[2:4]
    ends = v.run(lambda e: e.memset(neq[:, :], 1.0))
    gathered, rows_free = [None] * NB, [None] * NB
    ds_ready, ds_free = [None] * 2, [None] * 2
    in_free = out_free = None
    o_free, oh_free, sce_free, we_free = [None] * 2, [None] * 2, [None] * 2, [None] * 2
    fm_free = w_free = None
    far_done = None
    nmm = 0

    def gather(k):
        b = k % NB
        for j in range(CB):
            col = k * CB + j
            gathered[b] = s_row[b].dma(pool, lambda e: e.indirect_dma_start(
                out=rows[b][:, j, :], out_offset=None, in_=table[:, :],
                in_offset=bass.IndirectOffsetOnAxis(ap=g["srcix"][:, col:col + 1], axis=0)), rows_free[b])

    def edge_rows(k):
        b = k % 2
        for j, of in enumerate((dst, src)):
            rep = bass.AP(of.tensor, k * CB * P, [[P, CB], [0, GH], [1, P]])
            ds_ready[b] = s_ds[b].dma(sp, lambda e: e.dma_start(dsr[b][:, j, :], rep), ds_free[b])

    def back(a):
        return a[:, ::-1]

    gather(0)
    gather(1)
    edge_rows(0)
    for k in range(GROUPS):
        r, b = k % NB, k % 2
        if k + 2 < GROUPS:
            gather(k + 2)
        if k + 1 < GROUPS:
            edge_rows(k + 1)
        R = rows[r]
        t = act.run(lambda e: e.activation(sc_e[b][:, :, :].rearrange("p j (c h) -> p j c h", h=GH),
                                           R[:, :, D:ROW].rearrange("p c (j h) -> p j c h", h=GH), ACT.Copy),
                    gathered[r], sce_free[b])
        pe.wait(t, in_free)
        for j in range(2):
            turned = pe.run(lambda e: e.transpose(in_bank[:, j * P:(j + 1) * P], sc_e[b][:, j, :], c.ident[:, :]))
        sce_free[b] = turned
        ds = dsr[b]
        t = v.run(lambda e: e.tensor_tensor(neq[:, 1:P], ds[:, 0, 1:P], ds[:, 0, 0:P - 1], ALU.not_equal),
                  ds_ready[b], ends, fm_free)
        v.run(lambda e: e.tensor_scalar(brk[:, :], neq[:, :], -BIG, None, ALU.mult), t)
        t = v.run(lambda e: e.tensor_tensor(notself[:, :], ds[:, 0, :], ds[:, 1, :], ALU.not_equal))
        ds_free[b] = t
        t = v.run(lambda e: e.scalar_tensor_tensor(out=sdm[:, :], in0=notself[:, :], scalar=-BIG,
                                                   in1=in_bank[:, P:2 * P], op0=ALU.mult, op1=ALU.add), t, turned)
        v.run(lambda e: e.tensor_copy(sdm[:, 0:1], g["sdedge"][:, 0, k:k + 1]), t)
        t = v.run(lambda e: e.tensor_copy(sdm[:, P - 1:P], g["sdedge"][:, 1, k:k + 1]), t)
        t = v.run(lambda e: e.tensor_tensor_scan(out=d1[:, :], data0=brk[:, 0:P], data1=sdm[:, :], initial=-BIG,
                                                 op0=ALU.add, op1=ALU.max), t)
        t = v.run(lambda e: e.tensor_tensor_scan(out=back(d2), data0=back(brk[:, 1:P + 1]), data1=back(d1),
                                                 initial=-BIG, op0=ALU.add, op1=ALU.max), t)
        t = v.run(lambda e: e.tensor_tensor(ea0[:, :], d2[:, :], in_bank[:, 0:P], ALU.add), t)
        in_free = t
        t = v.run(lambda e: e.scalar_tensor_tensor(out=ea[:, :], in0=ea0[:, :], scalar=SLOPE, in1=ea0[:, :],
                                                   op0=ALU.mult, op1=ALU.max), t)
        t = v.run(lambda e: e.tensor_tensor_scan(out=mx1[:, :], data0=brk[:, 0:P], data1=ea[:, :], initial=-BIG,
                                                 op0=ALU.add, op1=ALU.max), t)
        t = v.run(lambda e: e.tensor_tensor_scan(out=back(mx), data0=back(brk[:, 1:P + 1]), data1=back(mx1),
                                                 initial=-BIG, op0=ALU.add, op1=ALU.max), t)
        t1 = v.run(lambda e: e.tensor_tensor(dlt[:, :], ea[:, :], mx[:, :], ALU.subtract), t, w_free)
        t2 = v.run(lambda e: e.tensor_tensor(fm[:, :], mx[:, :], neq[:, 0:P], ALU.mult), t, fm_free)
        w_free = act.run(lambda e: e.activation(wgt[:, :], dlt[:, :], ACT.Exp), t1, fm_free)
        pe.wait(w_free, t2, out_free)
        for j, a in enumerate((wgt, fm)):
            t = pe.run(lambda e: e.transpose(out_bank[:, j * P:(j + 1) * P], a[:, :], c.ident[:, :]))
        fm_free = t
        weights = act.run(lambda e: e.activation(we[b][:, :, :], out_bank[:, 0:2 * P].rearrange("p (j x) -> p j x", j=2),
                                                 ACT.Copy), t, we_free[b])
        out_free = weights
        act.run(lambda e: e.activation(R[:, :, D:ROW].rearrange("p c (j h) -> p j c h", h=GH),
                                       we[b][:, :, :].rearrange("p j (c h) -> p j c h", h=GH), ACT.Copy),
                weights)
        tail = act.last()
        oh = v.run(lambda e: e.tensor_tensor(onehot[b][:, :, :], c.ramp[:, :].unsqueeze(1).to_broadcast([P, CB, P]),
                                             g["loc"][:, k * CB:(k + 1) * CB].unsqueeze(2).to_broadcast([P, CB, P]),
                                             ALU.is_equal), oh_free[b])
        Q = 4
        for q in range(0, CB, Q):
            hv = R[:, q:q + Q, 0:D].rearrange("p c (h f) -> p c h f", f=GF)
            wv = we[b][:, 0, q * GH:(q + Q) * GH].rearrange("p (c h) -> p c h", h=GH)
            t = v.run(lambda e: e.tensor_tensor(hv, hv, wv.unsqueeze(3).to_broadcast([P, Q, GH, GF]), ALU.mult), weights)
            pe.wait(t, tail, oh)
            for j in range(q, q + Q):
                ob = nmm % 2
                m = pe.run(lambda e: e.matmul(o_banks[ob][:, 0:ROW], onehot[b][:, j, :], R[:, j, :],
                                              start=True, stop=True), o_free[ob])
                o_free[ob] = act.run(lambda e: e.activation(fout[b][:, j, :], o_banks[ob][:, 0:ROW], ACT.Copy),
                                     m, s_near[b].last(), s_far[b].last())
                nmm += 1
        we_free[b] = [t, tail]
        oh_free[b] = rows_free[r] = m
        near = frag[k * CB * NEAR:(k + 1) * CB * NEAR, :].rearrange("(c l) f -> l c f", l=NEAR)
        s_near[b].dma(sp, lambda e: e.dma_start(near, fout[b][0:NEAR, :, :]), o_free[ob])
        for j in range(CB):
            at = sp.engine.value_load(g["far"][0:1, k * CB + j:k * CB + j + 1], min_val=FAR + NEAR, max_val=NOT_WIDE)
            far_done = s_far[b].dma(sp, lambda e: e.dma_start(frag[bass.ds(at, P - NEAR), :], fout[b][NEAR:P, j, :],
                                                              cond=at < NOT_WIDE, bounds_check="skip_entire_dma"), o_free[ob], far_done)
        yield


def merge_stage(c, frag, g):
    nc = c.nc
    A = nc.alloc_sbuf_tensor
    first = A("mg_first", [P, BLOCKS, ROW], F32)
    last = A("mg_last", [P, BLOCKS, ROW], F32)
    hm = {n: A(f"mg_{n}", [GH, CHUNKS], F32) for n in
          ("mF", "mL", "sF", "sL", "cont", "cs", "G", "alpha", "beta", "gamma", "delta", "Cm", "tmp", "bs")}
    gs = A("mg_gs", [GH, CHUNKS + 1], F32)
    gp = A("mg_gp", [GH, CHUNKS + 1], F32)
    s_f, s_l, s_o = c.slot("mg_f"), c.slot("mg_l"), c.slot("mg_o")
    v, pe, act = c.dve, c.pe, c.act
    fl = s_f.dma(c.sp, lambda e: e.dma_start(first[:, :, :], frag[0:FAR].rearrange("(b c l) f -> l c b f", c=P, l=NEAR)[0]))
    for b in range(BLOCKS):
        ll = s_l.dma(c.pool, lambda e: e.indirect_dma_start(
            out=last[:, b, :], out_offset=None, in_=frag[:, :],
            in_offset=bass.IndirectOffsetOnAxis(ap=g["lastix"][:, b:b + 1], axis=0)))
    bank_free = [None] * 4
    n = 0
    for b in range(BLOCKS):
        for name, of, col in (("sF", first, D), ("mF", first, D + GH), ("sL", last, D), ("mL", last, D + GH)):
            q = n % 4
            t = pe.run(lambda e: e.transpose(c.banks[q][0:GH, 0:P], of[:, b, col:col + GH], c.ident[:, :]),
                       fl, ll, bank_free[q])
            bank_free[q] = v.run(lambda e: e.tensor_copy(hm[name][:, b * P:(b + 1) * P], c.banks[q][0:GH, 0:P]), t)
            n += 1
    h = {k: a[:, :] for k, a in hm.items()}
    df, dl = g["dfb"][0:GH, :], g["dlb"][0:GH, :]
    tt = lambda o, a, b, op, *w: v.run(lambda e: e.tensor_tensor(o, a, b, op), *w)
    ts = lambda o, a, s1, s2, o1, o2, *w: v.run(lambda e: e.tensor_scalar(o, a, s1, s2, o1, o2), *w)
    t = bank_free[:]
    t = v.run(lambda e: e.memset(hm["cont"][:, 0:1], 0.0), t)
    t = tt(hm["cont"][:, 1:], df[:, 1:], dl[:, 0:CHUNKS - 1], ALU.is_equal, t)
    t = tt(h["cs"], df, dl, ALU.is_equal, t)
    t = tt(h["cs"], h["cs"], h["cont"], ALU.mult, t)
    t = ts(h["tmp"], h["cs"], BIG, -BIG, ALU.mult, ALU.add, t)
    t = v.run(lambda e: e.tensor_tensor_scan(out=gp[:, 1:], data0=h["tmp"], data1=h["mL"], initial=-BIG,
                                             op0=ALU.add, op1=ALU.max), t)
    t = v.run(lambda e: e.memset(gp[:, 0:1], -BIG), t)
    G, Gp = gp[:, 1:], gp[:, 0:CHUNKS]
    t = tt(h["alpha"], Gp, G, ALU.subtract, t)
    t = ts(h["alpha"], h["alpha"], 0.0, None, ALU.min, ALU.bypass, t)
    t = act.run(lambda e: e.activation(h["alpha"], h["alpha"], ACT.Exp), t)
    t = tt(h["alpha"], h["alpha"], h["cs"], ALU.mult, t)
    t = tt(h["beta"], h["mL"], G, ALU.subtract, t)
    t = act.run(lambda e: e.activation(h["beta"], h["beta"], ACT.Exp), t)
    t = ts(h["tmp"], h["cont"], BIG, -BIG, ALU.mult, ALU.add, t)
    t = tt(h["Cm"], Gp, h["tmp"], ALU.add, t)
    t = tt(h["tmp"], h["Cm"], h["mF"], ALU.max, t)
    t = tt(h["gamma"], h["Cm"], h["tmp"], ALU.subtract, t)
    t = act.run(lambda e: e.activation(h["gamma"], h["gamma"], ACT.Exp), t)
    t = tt(h["delta"], h["mF"], h["tmp"], ALU.subtract, t)
    t = act.run(lambda e: e.activation(h["delta"], h["delta"], ACT.Exp), t)
    t = tt(h["bs"], h["beta"], h["sL"], ALU.mult, t)
    t = v.run(lambda e: e.memset(gs[:, 0:1], 0.0), t)
    t = v.run(lambda e: e.tensor_tensor_scan(out=gs[:, 1:], data0=h["alpha"], data1=h["bs"], initial=0.0,
                                             op0=ALU.mult, op1=ALU.add), t)
    t = tt(h["tmp"], h["gamma"], gs[:, 0:CHUNKS], ALU.mult, t)
    t = tt(h["sF"], h["sF"], h["delta"], ALU.mult, t)
    t = tt(h["sF"], h["sF"], h["tmp"], ALU.add, t)
    merged = t
    fT = A("mg_fT", [P, CHUNKS], F32)
    lT = A("mg_lT", [P, CHUNKS], F32)
    run = A("mg_run", [P, CHUNKS + 1], F32)
    W = 416
    bank_free = [None] * 8
    for half in range(KD):
        n = 0
        for b in range(BLOCKS):
            for of, to in ((first, fT), (last, lT)):
                q = n % 4
                t = pe.run(lambda e: e.transpose(c.banks[q][:, 0:P], of[:, b, half * P:(half + 1) * P], c.ident[:, :]),
                           bank_free[q], merged)
                bank_free[q] = v.run(lambda e: e.tensor_copy(to[:, b * P:(b + 1) * P], c.banks[q][:, 0:P]), t)
                n += 1
        t = v.run(lambda e: e.memset(run[:, 0:1], 0.0), bank_free[0:4])
        for w in range(0, CHUNKS, W):
            sl = slice(w, w + W)
            for q, name in enumerate(("alpha", "beta", "gamma", "delta")):
                x = pe.run(lambda e: e.matmul(c.banks[4 + q][:, 0:W], c.headsel[:, half * P:(half + 1) * P],
                                              hm[name][:, sl], start=True, stop=True), merged, bank_free[4 + q])
            al, be, ga, de = (c.banks[4 + q][:, 0:W] for q in range(4))
            t = tt(lT[:, sl], lT[:, sl], be, ALU.mult, t, x, bank_free[0:4])
            t = v.run(lambda e: e.tensor_tensor_scan(out=run[:, w + 1:w + W + 1], data0=al, data1=lT[:, sl],
                                                     initial=run[:, w:w + 1], op0=ALU.mult, op1=ALU.add), t)
            t = tt(lT[:, sl], run[:, sl], ga, ALU.mult, t)
            t = tt(fT[:, sl], fT[:, sl], de, ALU.mult, t)
            for q in range(4):
                bank_free[4 + q] = t
            t = tt(fT[:, sl], fT[:, sl], lT[:, sl], ALU.add, t)
        for b in range(BLOCKS):
            q = b % 4
            x = pe.run(lambda e: e.transpose(c.banks[q][:, 0:P], fT[:, b * P:(b + 1) * P], c.ident[:, :]),
                       t, bank_free[q])
            bank_free[q] = v.run(lambda e: e.tensor_copy(first[:, b, half * P:(half + 1) * P], c.banks[q][:, 0:P]), x)
    for b in range(BLOCKS):
        q = b % 4
        x = pe.run(lambda e: e.transpose(c.banks[q][:, 0:GH], hm["sF"][:, b * P:(b + 1) * P], c.ident[0:GH, 0:GH]),
                   merged, bank_free[q])
        bank_free[q] = v.run(lambda e: e.tensor_copy(first[:, b, D:D + GH], c.banks[q][:, 0:GH]), x)
    s_o.dma(c.sp, lambda e: e.dma_start(frag[0:FAR].rearrange("(b c l) f -> l c b f", c=P, l=NEAR)[0], first[:, :, :]),
            bank_free[0:4])


def mlp_stage(c, x, xn_d, xnt_d, xm_d, wqa, bqa, w_fc1, b_fc1, w_fc2, b_fc2, norm_g, norm_b):
    nc = c.nc
    A = nc.alloc_sbuf_tensor
    w1 = A("fc1_w", [P, KD, MLP], F32)
    w2 = A("fc2_w", [P, MT, D], F32)
    gcol = A("fc_gcol", [P, 2, KD], F32)
    b1 = A("fc1_b", [P, MT], F32)
    b2 = A("fc2_b", [1, D], F32)
    xt = A("m_xt", [P, KD, ST * P], F32)
    xn = A("m_xn", [P, ST, D], F32)
    xs = A("m_xs", [P, ST, D], F32)
    x2 = A("m_x2", [P, ST, D], F32)
    hn = xn
    hnt = A("m_hnt", [P, KD, ST * P], F32)
    hid = A("m_hid", [P, MT, ST * P], F32)
    st = A("m_st", [P, ST, 16], F32)
    s_w, s_xt, s_xn, s_xs, s_o = (c.slot(f"m_{n}") for n in ("w", "xt", "xn", "xs", "o"))
    v, pe, act, sp = c.dve, c.pe, c.act, c.sp
    s_w.dma(sp, lambda e: e.dma_start(w1[:, :, :], w_fc1.rearrange("(k p) n -> p k n", p=P)))
    s_w.dma(sp, lambda e: e.dma_start(w2[:, :, :], w_fc2.rearrange("(k p) n -> p k n", p=P)))
    s_w.dma(sp, lambda e: e.dma_start(gcol[:, 0, :], norm_g.rearrange("(k p) -> p k", p=P)))
    s_w.dma(sp, lambda e: e.dma_start(gcol[:, 1, :], norm_b.rearrange("(k p) -> p k", p=P)))
    s_w.dma(sp, lambda e: e.dma_start(b1[:, :], b_fc1.rearrange("(k p) -> p k", p=P)))
    w = s_w.dma(sp, lambda e: e.dma_start(b2[:, :], b_fc2.unsqueeze(0)))
    bank_t, bank_h, bank_y = c.banks[4:6], c.banks[6], c.banks[7]
    pe.wait(w)
    for m in range(MT):
        for k in range(KD):
            t = pe.run(lambda e: e.matmul(bank_h[:, m:m + 1], w1[:, k, m * P:(m + 1) * P], gcol[:, 1, k:k + 1],
                                          start=(k == 0), stop=(k == KD - 1)))
    t = v.run(lambda e: e.tensor_tensor(b1[:, :], b1[:, :], bank_h[:, 0:MT], ALU.add), t)
    for k in range(KD):
        t = v.run(lambda e: e.tensor_scalar(w1[:, k, :], w1[:, k, :], gcol[:, 0, k:k + 1], None, ALU.mult), t)
    wready = t
    tp_free = [t, t]
    h_free = y_free = t
    xt_used = xn_used = xs_used = hnt_used = hid_used = None
    for s, n in SUPERS:
        rows = slice(s * P, (s + n) * P)
        a = s_xt.dma(sp, lambda e: e.dma_start(xt[:, :, 0:n * P], xnt_d.rearrange("(k p) n -> p k n", p=P)[:, :, rows]), xt_used)
        b = s_xn.dma(sp, lambda e: e.dma_start(xn[:, 0:n, :], xn_d[rows].rearrange("(t p) d -> p t d", p=P)), xn_used)
        d = s_xs.dma(sp, lambda e: e.dma_start(xs[:, 0:n, :], x[rows].rearrange("(t p) d -> p t d", p=P)), xs_used)
        for i in range(0, n, 2):
            pe.wait(a, y_free)
            for j in range(2):
                for k in range(KD):
                    pe.run(lambda e: e.matmul(bank_y[:, j * D:(j + 1) * D], xt[:, k, (i + j) * P:(i + j + 1) * P], wqa[:, k, :],
                                              start=(k == 0), stop=False))
                t = pe.run(lambda e: e.matmul(bank_y[:, j * D:(j + 1) * D], c.ones[0:1, :], bqa[:, :], start=False, stop=True))
            y_free = v.run(lambda e: e.tensor_tensor(x2[:, i:i + 2, :], bank_y[:, :].rearrange("p (t d) -> p t d", t=2),
                                                     xn[:, i:i + 2, :], ALU.add), t, b, s_o.last())
        xt_used = t
        yield
        normed = layernorm(c, x2, hn, st, n, [y_free], [])
        turned = turn(c, hn, hnt, n, bank_t, normed, tp_free, hnt_used)
        xn_used = pe.last()
        yield
        for m in range(MT):
            pe.wait(turned, wready, h_free)
            for k in range(KD):
                t = pe.run(lambda e: e.matmul(bank_h[:, 0:n * P], w1[:, k, m * P:(m + 1) * P], hnt[:, k, 0:n * P],
                                              start=(k == 0), stop=(k == KD - 1)))
            h_free = act.run(lambda e: e.activation(hid[:, m, 0:n * P], bank_h[:, 0:n * P], ACT.Gelu, bias=b1[:, m:m + 1]),
                             t, hid_used)
        hnt_used = t
        yield
        for i in range(0, n, 2):
            pe.wait(h_free, y_free)
            for j in range(2):
                for m in range(MT):
                    pe.run(lambda e: e.matmul(bank_y[:, j * D:(j + 1) * D], hid[:, m, (i + j) * P:(i + j + 1) * P], w2[:, m, :],
                                              start=(m == 0), stop=False))
                t = pe.run(lambda e: e.matmul(bank_y[:, j * D:(j + 1) * D], c.ones[0:1, :], b2[:, :], start=False, stop=True))
            y_free = v.run(lambda e: e.tensor_tensor(x2[:, i:i + 2, :], bank_y[:, :].rearrange("p (t d) -> p t d", t=2),
                                                     x2[:, i:i + 2, :], ALU.add), t)
        hid_used = t
        t = v.run(lambda e: e.tensor_tensor(x2[:, 0:n, :], x2[:, 0:n, :], xs[:, 0:n, :], ALU.add), y_free, d)
        xs_used = t
        s_o.dma(sp, lambda e: e.dma_start(xm_d[rows].rearrange("(t p) d -> p t d", p=P), x2[:, 0:n, :]), t)
        yield


def experts_stage(c, xm_d, frag, g, out, gate_w, gate_b, ew1, eb1, ew2, eb2):
    nc = c.nc
    A = nc.alloc_sbuf_tensor
    w1 = A("e_w1", [P, EXPERTS, KD, HID], F32)
    w2 = A("e_w2", [P, EXPERTS, HT, D], F32)
    b1 = A("e_b1", [P, EXPERTS, HT], F32)
    b2 = A("e_b2", [EXPERTS, D], F32)
    gw = A("e_gw", [P, KD, EXPERTS], F32)
    gb = A("e_gb", [1, EXPERTS], F32)
    x1 = [A(f"e_x1{b}", [P, ST, D], F32) for b in range(2)]
    fr = [A(f"e_fr{b}", [P, ST, ROW], F32) for b in range(2)]
    rs = A("e_rs", [P, ST, GH], F32)
    hn = A("e_hn", [P, ST, D], F32)
    hnt = A("e_hnt", [P, KD, ST * P], F32)
    hid = [A(f"e_hid{b}", [P, HT, ST * P], F32) for b in range(2)]
    acc = A("e_acc", [P, ST, D], F32)
    st = A("e_st", [P, ST, 16], F32)
    lg = A("e_lg", [P, ST, EXPERTS], F32)
    pr = A("e_pr", [P, ST, EXPERTS], F32)
    m8 = A("e_m8", [P, ST, 8], F32)
    gt = A("e_gt", [P, ST, EXPERTS], F32)
    eq = A("e_eq", [P, ST, EXPERTS], F32)
    cum = A("e_cum", [P, ST, EXPERTS], F32)
    cw = A("e_cw", [P, ST, EXPERTS], F32)
    cwt = A("e_cwt", [EXPERTS, ST * P], F32)
    s1 = A("e_s1", [P, ST, 4], F32)
    s_w, s_o = c.slot("e_w"), c.slot("e_o")
    s_x, s_f = [c.slot(f"e_x{b}") for b in range(2)], [c.slot(f"e_f{b}") for b in range(2)]
    v, pe, act, sp, pool = c.dve, c.pe, c.act, c.sp, c.pool
    for to, of in ((w1[:, :, :, :].rearrange("p e k n -> p (e k) n"), ew1.rearrange("e (k p) n -> p (e k) n", p=P)),
                   (w2[:, :, :, :].rearrange("p e k n -> p (e k) n"), ew2.rearrange("e (k p) n -> p (e k) n", p=P)),
                   (b1[:, :, :].rearrange("p e k -> p (e k)"), eb1.rearrange("e (k p) -> p (e k)", p=P)),
                   (b2[:, :], eb2), (gw[:, :, :], gate_w.rearrange("(k p) n -> p k n", p=P)),
                   (gb[:, :], gate_b.unsqueeze(0))):
        w = s_w.dma(sp, lambda e: e.dma_start(to, of))
    bank_t, bank_h, bank_y, bank_g = c.banks[0:2], c.banks[2:4], c.banks[4:6], c.banks[6:8]
    tp_free, h_free, y_free, g_free = [None] * 2, [None] * 2, [None] * 2, [None] * 2
    xin, fin, x_used = [None] * 2, [None] * 2, [None] * 2
    hid_used = [None] * 2
    hnt_used = gate_used = None
    nh = ny = 0

    def fetch(k):
        s, n = SUPERS[k]
        b = k % 2
        xin[b] = s_x[b].dma(sp, lambda e: e.dma_start(
            x1[b][:, 0:n, :], xm_d[s * P:(s + n) * P].rearrange("(t p) d -> p t d", p=P)), x_used[b], s_o.last())
        for i in range(n):
            fin[b] = s_f[b].dma(pool, lambda e: e.indirect_dma_start(
                out=fr[b][:, i, :], out_offset=None, in_=frag[:, :],
                in_offset=bass.IndirectOffsetOnAxis(ap=g["nodeix"][:, s + i:s + i + 1], axis=0)), x_used[b])

    fetch(0)
    for k, (s, n) in enumerate(SUPERS):
        b = k % 2
        if k + 1 < len(SUPERS):
            fetch(k + 1)
        X, Fr = x1[b], fr[b]
        t = v.run(lambda e: e.tensor_scalar(rs[:, 0:n, :], Fr[:, 0:n, D:D + GH], SEG_EPS, None, ALU.add), fin[b])
        t = v.run(lambda e: e.reciprocal(rs[:, 0:n, :], rs[:, 0:n, :]), t)
        fv = Fr[:, 0:n, 0:D].rearrange("p t (h f) -> p t h f", f=GF)
        t = v.run(lambda e: e.tensor_tensor(fv, fv, rs[:, 0:n, :].unsqueeze(3).to_broadcast([P, n, GH, GF]), ALU.mult), t)
        t = v.run(lambda e: e.tensor_tensor(X[:, 0:n, :], X[:, 0:n, :], Fr[:, 0:n, 0:D], ALU.add), t, xin[b])
        normed = layernorm(c, X, hn, st, n, [t], [pe.last()])
        turned = turn(c, hn, hnt, n, bank_t, normed, tp_free, hnt_used)
        pe.wait(w, turned, g_free[0])
        for i in range(n):
            o = bank_g[0][:, i * EXPERTS:(i + 1) * EXPERTS]
            for kk in range(KD):
                pe.run(lambda e: e.matmul(o, hnt[:, kk, i * P:(i + 1) * P], gw[:, kk, :], start=(kk == 0), stop=False))
            t = pe.run(lambda e: e.matmul(o, c.ones[0:1, :], gb[:, :], start=False, stop=True))
        t = v.run(lambda e: e.tensor_copy(lg[:, 0:n, :], bank_g[0][:, 0:n * EXPERTS].rearrange("p (t e) -> p t e", t=n)), t)
        g_free[0] = t
        wide = lambda a: a.to_broadcast([P, n, EXPERTS])
        t = v.run(lambda e: e.tensor_reduce(s1[:, 0:n, 0], lg[:, 0:n, :], AX, ALU.max), t)
        t = v.run(lambda e: e.tensor_tensor(lg[:, 0:n, :], lg[:, 0:n, :], wide(s1[:, 0:n, 0:1]), ALU.subtract), t)
        t = act.run(lambda e: e.activation(pr[:, 0:n, :], lg[:, 0:n, :], ACT.Exp), t)
        t = v.run(lambda e: e.tensor_reduce(s1[:, 0:n, 1], pr[:, 0:n, :], AX, ALU.add), t)
        t = v.run(lambda e: e.reciprocal(s1[:, 0:n, 2], s1[:, 0:n, 1]), t)
        t = v.run(lambda e: e.tensor_tensor(pr[:, 0:n, :], pr[:, 0:n, :], wide(s1[:, 0:n, 2:3]), ALU.mult), t)
        for i in range(n):
            x = v.run(lambda e: e.max(m8[:, i, :], pr[:, i, :]), t)
        t = v.run(lambda e: e.tensor_tensor(gt[:, 0:n, :], pr[:, 0:n, :], wide(m8[:, 0:n, 1:2]), ALU.is_gt), x)
        t = v.run(lambda e: e.tensor_tensor(eq[:, 0:n, :], pr[:, 0:n, :], wide(m8[:, 0:n, 1:2]), ALU.is_equal), t)
        t = v.run(lambda e: e.tensor_reduce(s1[:, 0:n, 3], gt[:, 0:n, :], AX, ALU.add), t)
        for i in range(n):
            x = v.run(lambda e: e.tensor_tensor_scan(out=cum[:, i, :], data0=c.ones[:, 0:EXPERTS], data1=eq[:, i, :],
                                                     initial=s1[:, i, 3:4], op0=ALU.mult, op1=ALU.add), t)
        t = v.run(lambda e: e.tensor_scalar(cum[:, 0:n, :], cum[:, 0:n, :], 2.0, None, ALU.is_le), x)
        t = v.run(lambda e: e.tensor_tensor(eq[:, 0:n, :], eq[:, 0:n, :], cum[:, 0:n, :], ALU.mult), t)
        t = v.run(lambda e: e.tensor_tensor(gt[:, 0:n, :], gt[:, 0:n, :], eq[:, 0:n, :], ALU.add), t)
        cwr = v.run(lambda e: e.tensor_tensor(cw[:, 0:n, :], gt[:, 0:n, :], pr[:, 0:n, :], ALU.mult), t, gate_used)
        pe.wait(cwr, g_free[1])
        for i in range(n):
            t = pe.run(lambda e: e.transpose(bank_g[1][0:EXPERTS, i * P:(i + 1) * P], cw[:, i, :], c.ident[:, :]))
        t = v.run(lambda e: e.tensor_copy(cwt[:, 0:n * P], bank_g[1][0:EXPERTS, 0:n * P]), t)
        g_free[1] = t
        for i in range(0, n, 2):
            yb = ny % 2
            ny += 1
            pe.wait(t, y_free[yb])
            for j in range(2):
                x = pe.run(lambda e: e.matmul(bank_y[yb][:, j * D:(j + 1) * D], cwt[:, (i + j) * P:(i + j + 1) * P], b2[:, :],
                                              start=True, stop=True))
            y_free[yb] = v.run(lambda e: e.tensor_tensor(acc[:, i:i + 2, :], bank_y[yb][:, :].rearrange("p (t d) -> p t d", t=2),
                                                         X[:, i:i + 2, :], ALU.add), x, s_o.last())
        x_used[b] = v.last()
        accr = v.last()
        for ex in range(EXPERTS):
            H = hid[ex % 2]
            for m in range(HT):
                hb = nh % 2
                nh += 1
                pe.wait(h_free[hb])
                for kk in range(KD):
                    t = pe.run(lambda e: e.matmul(bank_h[hb][:, 0:n * P], w1[:, ex, kk, m * P:(m + 1) * P], hnt[:, kk, 0:n * P],
                                                  start=(kk == 0), stop=(kk == KD - 1)))
                h_free[hb] = act.run(lambda e: e.activation(H[:, m, 0:n * P], bank_h[hb][:, 0:n * P], ACT.Gelu,
                                                            bias=b1[:, ex, m:m + 1]), t, hid_used[ex % 2])
            hnt_used = t
            for i in range(0, n, 2):
                yb = ny % 2
                ny += 1
                pe.wait(h_free, y_free[yb])
                for j in range(2):
                    for m in range(HT):
                        t = pe.run(lambda e: e.matmul(bank_y[yb][:, j * D:(j + 1) * D], H[:, m, (i + j) * P:(i + j + 1) * P],
                                                      w2[:, ex, m, :], start=(m == 0), stop=(m == HT - 1)))
                for j in range(2):
                    y = v.run(lambda e: e.scalar_tensor_tensor(
                        out=acc[:, i + j, :], in0=bank_y[yb][:, j * D:(j + 1) * D], scalar=cw[:, i + j, ex:ex + 1],
                        in1=acc[:, i + j, :], op0=ALU.mult, op1=ALU.add), t, accr)
                y_free[yb] = y
            accr = y
            hid_used[ex % 2] = t
        gate_used = y
        lo, hi = s * P, min((s + n) * P, N_NODES)
        full = (hi - lo) // P
        s_o.dma(sp, lambda e: e.dma_start(out[lo:lo + full * P].rearrange("(t p) d -> p t d", p=P), acc[:, 0:full, :]), y)
        if hi - lo > full * P:
            r = hi - lo - full * P
            s_o.dma(sp, lambda e: e.dma_start(out[lo + full * P:hi], acc[0:r, full, :]), y)


def build(nc, a, out, stop=None):
    c = Core(nc)
    dram = lambda name, shape: nc.dram_tensor(name, shape, F32, kind="Internal").ap()
    table = dram("table", [N_PAD, ROW])
    xn_d = dram("xn_d", [N_PAD, D])
    xnt_d = dram("xnt_d", [D, N_PAD])
    xm_d = dram("xm_d", [N_PAD, D])
    frag = dram("frag", [FRAGS, ROW])
    rows_d = dram("rows_d", [2, CHUNKS])
    sdst_d = dram("sdst_d", [2, CHUNKS, GH])
    A = nc.alloc_sbuf_tensor
    constants(c)
    gram = A("gram", [P, KD, D + 1], F32)
    wqa, bqa = A("wqa", [P, KD, D], F32), A("bqa", [1, D], F32)
    g = {"dfb": A("dfb", [P, CHUNKS], F32), "dlb": A("dlb", [P, CHUNKS], F32), "loc": A("loc", [P, CHUNKS], F32),
         "srcix": A("srcix", [P, CHUNKS], I32), "sdedge": A("sdedge", [P, 2, GROUPS], F32),
         "lastix": A("lastix", [P, BLOCKS], I32), "nodeix": A("nodeix", [P, TILES], I32),
         "far": A("far", [1, CHUNKS], I32)}
    c.fence()
    src, dst = (a[n].rearrange("(c e) -> c e", e=P) for n in ("src", "dst"))
    mark = nc.sbuf_base
    nodes_stage(c, a["x"], frag, table, xn_d, xnt_d, a["L0_gnn_W"], a["L0_gnn_a_src"], a["L0_gnn_a_dst"], gram)
    c.fence()
    nc.sbuf_base = mark
    mix_weights_stage(c, gram, a["L0_mix_w_qkv"], a["L0_mix_b_qkv"], wqa, bqa)
    index_stage(c, dst, src, table, rows_d, sdst_d, g)
    c.fence()
    nc.sbuf_base = mark
    edges = edges_stage(c, dst, src, table, frag, g)
    mlp = mlp_stage(c, a["x"], xn_d, xnt_d, xm_d, wqa, bqa, *(a[f"L0_mix_{n}"] for n in (
        "w_fc1", "b_fc1", "w_fc2", "b_fc2", "norm_g", "norm_b")))
    for _ in edges:
        next(mlp, None)
    for _ in mlp:
        pass
    c.fence()
    nc.sbuf_base = mark
    merge_stage(c, frag, g)
    c.fence()
    nc.sbuf_base = mark
    experts_stage(c, xm_d, frag, g, out, *(a[f"L0_ffn_{n}"] for n in ("gate_w", "gate_b", "W1", "b1", "W2", "b2")))
    c.fence()


_INS = ["x", "src", "dst", "L0_gnn_W", "L0_gnn_a_src", "L0_gnn_a_dst", "L0_mix_w_qkv", "L0_mix_b_qkv",
        "L0_mix_norm_g", "L0_mix_norm_b", "L0_mix_w_fc1", "L0_mix_b_fc1", "L0_mix_w_fc2", "L0_mix_b_fc2",
        "L0_ffn_gate_w", "L0_ffn_gate_b", "L0_ffn_W1", "L0_ffn_b1", "L0_ffn_W2", "L0_ffn_b2"]


def kernel(**inputs):
    import concourse.bacc as _bacc
    from concourse.bass_utils import run_bass_kernel_spmd as _run

    nc = _bacc.Bacc("TRN2", target_bir_lowering=False, num_devices=1)
    arrays, aps = {}, {}
    pads = {"x": (N_PAD - N_NODES, 0), "src": (CHUNKS * P - N_EDGES, N_NODES), "dst": (CHUNKS * P - N_EDGES, N_NODES)}
    for name in _INS:
        v = np.ascontiguousarray(inputs[name])
        if name in pads:
            more, fill = pads[name]
            v = np.concatenate([v, np.full((more,) + v.shape[1:], fill, v.dtype)])
        arrays[f"in_{name}"] = v
        aps[name] = nc.dram_tensor(f"in_{name}", v.shape, mybir.dt.from_np(v.dtype), kind="ExternalInput").ap()
    out = nc.dram_tensor("out_0", (N_NODES, D), F32, kind="ExternalOutput").ap()
    with nc.allow_non_contiguous_dma(reason="small strided loads, once"):
        build(nc, aps, out)
    r = _run(nc, [arrays], core_ids=[0])
    return r.results[0]["out_0"]
```

```python
import numpy as np

import concourse.bass as bass
from concourse import mybir

F32 = mybir.dt.float32
I32 = mybir.dt.int32
ALU = mybir.AluOpType
ACT = mybir.ActivationFunctionType
AX = mybir.AxisListType.X

P = 128
BIG = 1.0e30
LN_EPS = 1e-5
SEG_EPS = 1e-8
SLOPE = 0.2

N_NODES = 12500
N_EDGES = 212500
D = 256
KD = D // P
TILES = -(-N_NODES // P)
N_PAD = TILES * P
ST = 4
SUPERS = [(s, min(ST, TILES - s)) for s in range(0, TILES, ST)]
GH, GF = 8, 32
ROW = D + 2 * GH
CB = 16
GROUPS = -(-N_EDGES // (P * CB))
BLOCKS = -(-GROUPS * CB // P)
CHUNKS = BLOCKS * P
NEAR = 32
FAR = CHUNKS * NEAR
FRAGS = FAR + N_NODES + 1 + P
NOT_WIDE = FRAGS - (P - NEAR)
MIX_HEADS, MIX_HD = 4, 64
MLP = 768
MT = MLP // P
EXPERTS, HID = 8, 512
HT = HID // P
REGION = N_PAD + P
SLOTS = (2 * N_PAD + EXPERTS * (P - 1)) // P


class Lane:

    def __init__(self, nc, engine, name):
        self.engine, self.sem, self.count, self.seen = engine, nc.alloc_semaphore(name), 0, {}

    def wait(self, *tokens):
        for t in tokens:
            if t is None:
                continue
            if isinstance(t, list):
                self.wait(*t)
                continue
            sem, value, key = t
            if self.seen.get(key, 0) < value:
                self.engine.wait_ge(sem, value)
                self.seen[key] = value

    def run(self, issue, *tokens):
        self.wait(*tokens)
        issue(self.engine).then_inc(self.sem, 1)
        self.count += 1
        return (self.sem, self.count, id(self))

    def last(self):
        return (self.sem, self.count, id(self)) if self.count else None


class Slot:

    def __init__(self, nc, name):
        self.sem, self.count = nc.alloc_semaphore(name), 0

    def dma(self, lane, issue, *tokens):
        lane.wait(*tokens)
        issue(lane.engine).then_inc(self.sem, 16)
        self.count += 16
        return (self.sem, self.count, id(self))

    def last(self):
        return (self.sem, self.count, id(self)) if self.count else None


class Core:
    def __init__(self, nc):
        self.nc = nc
        self.pe = Lane(nc, nc.tensor, "pe_done")
        self.dve = Lane(nc, nc.vector, "dve_done")
        self.act = Lane(nc, nc.scalar, "act_done")
        self.pool = Lane(nc, nc.gpsimd, "pool_done")
        self.sp = Lane(nc, nc.sync, "sp_done")
        self.slots = []
        self.banks = [nc.alloc_psum_tensor(f"bank{i}", [P, 512], F32) for i in range(8)]

    def slot(self, name):
        self.slots.append(Slot(self.nc, name))
        return self.slots[-1]

    def fence(self):
        done = [l.last() for l in (self.pe, self.dve, self.act, self.pool)] + [s.last() for s in self.slots]
        for lane in (self.pe, self.dve, self.act, self.pool, self.sp):
            lane.wait(*done)


def rsqrt(c, var, out, tmp, ready):
    v = c.dve
    t = v.run(lambda e: e.tensor_single_scalar(tmp.bitcast(I32), var.bitcast(I32), 1, ALU.logical_shift_right), ready)
    t = v.run(lambda e: e.tensor_scalar(out.bitcast(I32), tmp.bitcast(I32), -1.0, float(0x5F3759DF), ALU.mult, ALU.add), t)
    for _ in range(3):
        t = v.run(lambda e: e.tensor_tensor(tmp, out, out, ALU.mult), t)
        t = v.run(lambda e: e.tensor_tensor(tmp, tmp, var, ALU.mult), t)
        t = v.run(lambda e: e.tensor_scalar(tmp, tmp, -0.5, 1.5, ALU.mult, ALU.add), t)
        t = v.run(lambda e: e.tensor_tensor(out, out, tmp, ALU.mult), t)
    return t


def layernorm(c, x, out, stats, n, ready, free):
    v = c.dve
    v.wait(*ready)
    t = None
    for i in range(n):
        t = v.run(lambda e, i=i: e.bn_stats(stats[:, i, 0:6], x[:, i, :]))
    t = v.run(lambda e: e.engine_nop(), t) if False else t
    for i in range(n):
        t = v.run(lambda e, i=i: e.bn_aggr(stats[:, i, 6:8], stats[:, i, 0:6]), t)
    var = stats[:, 0:n, 8]
    t = v.run(lambda e: e.tensor_scalar(var, stats[:, 0:n, 7], LN_EPS, None, ALU.add), t)
    t = rsqrt(c, var, stats[:, 0:n, 9], stats[:, 0:n, 10], t)
    v.wait(*free)
    for i in range(n):
        t = v.run(lambda e, i=i: e.tensor_scalar(out[:, i, 0:D], x[:, i, :], stats[:, i, 6:7], stats[:, i, 9:10],
                                                 ALU.subtract, ALU.mult), t)
    return t


def turn(c, src, dst, n, banks, ready, bank_free, dst_free):
    outs = []
    for k in range(KD):
        c.pe.wait(ready, bank_free[k])
        for i in range(n):
            t = c.pe.run(lambda e, i=i: e.transpose(banks[k][:, i * P:(i + 1) * P], src[:, i, k * P:(k + 1) * P],
                                                    c.ident[:, :]))
        o = c.act.run(lambda e: e.activation(dst[:, k, 0:n * P], banks[k][:, 0:n * P], ACT.Copy), t, dst_free)
        bank_free[k] = o
        outs.append(o)
    return outs


def constants(c):
    nc = c.nc
    c.ident = nc.alloc_sbuf_tensor("ident", [P, P], F32)
    c.ramp = nc.alloc_sbuf_tensor("ramp", [P, P], F32)
    c.ones = nc.alloc_sbuf_tensor("ones", [P, P], F32)
    c.headsel = nc.alloc_sbuf_tensor("headsel", [GH, D], F32)
    p = c.pool
    t = p.run(lambda e: e.memset(c.ident[:, :], 0.0))
    t = p.run(lambda e: e.affine_select(out=c.ident[:, :], in_=c.ident[:, :], compare_op=ALU.not_equal, fill=1.0,
                                        base=0, pattern=[[-1, P]], channel_multiplier=1), t)
    p.run(lambda e: e.iota(c.ramp[:, :], pattern=[[1, P]], base=0, channel_multiplier=0,
                           allow_small_or_imprecise_dtypes=True))
    p.run(lambda e: e.memset(c.ones[:, :], 1.0))
    t = p.run(lambda e: e.memset(c.headsel[:, :], 0.0))
    v = c.headsel[:, :].rearrange("p (h f) -> p h f", f=GF)
    p.run(lambda e: e.affine_select(out=v, in_=v, compare_op=ALU.not_equal, fill=1.0, base=0,
                                    pattern=[[-1, GH], [0, GF]], channel_multiplier=1), t)


def nodes_stage(c, x, frag, table, xn_d, xnt_d, gnn_w, a_src, a_dst, gram):
    nc = c.nc
    A = nc.alloc_sbuf_tensor
    wcat = A("wcat", [P, KD, ROW], F32)
    avec = A("avec", [P, 2, D], F32)
    wtmp = A("wtmp", [P, D], F32)
    xs = [A(f"xs{b}", [P, ST, D], F32) for b in range(2)]
    xn = [A(f"xn{b}", [P, ST, D + 1], F32) for b in range(2)]
    xt = [A(f"xt{b}", [P, KD, ST * P], F32) for b in range(2)]
    hr = [A(f"hr{b}", [P, ST, ROW], F32) for b in range(2)]
    st = A("st_a", [P, ST, 16], F32)
    s_w, s_x = c.slot("a_w"), [c.slot(f"a_x{b}") for b in range(2)]
    s_xn, s_xt, s_h = ([c.slot(f"a_{n}{b}") for b in range(2)] for n in ("xn", "xt", "h"))

    for k in range(KD):
        w = s_w.dma(c.sp, lambda e: e.dma_start(wcat[:, k, 0:D].rearrange("p (h f) -> p h f", f=GF),
                                                gnn_w[:, k * P:(k + 1) * P, :].rearrange("h i f -> i h f")))
    for j, a in enumerate((a_src, a_dst)):
        w = s_w.dma(c.sp, lambda e: e.dma_start(avec[:, j, :], a.rearrange("h f -> (h f)").partition_broadcast(P)))
    t = w
    for k in range(KD):
        for j in range(2):
            t = c.dve.run(lambda e: e.tensor_tensor(wtmp[:, :], wcat[:, k, 0:D], avec[:, j, :], ALU.mult), t)
            t = c.dve.run(lambda e: e.tensor_reduce(wcat[:, k, D + GH * j:D + GH * (j + 1)],
                                                    wtmp[:, :].rearrange("p (h f) -> p h f", f=GF), AX, ALU.add), t)
    scores_ready = t
    for b in range(2):
        c.dve.run(lambda e: e.memset(xn[b][:, :, D:D + 1], 1.0))
    zero = A("zero", [P, ROW], F32)
    t = c.dve.run(lambda e: e.memset(zero[:, :], 0.0))
    s_z = c.slot("a_zero")
    for r in range(FAR, FRAGS, P):
        n = min(P, FRAGS - r)
        s_z.dma(c.sp, lambda e: e.dma_start(frag[r:r + n, :], zero[0:n, :]), t)

    load, xs_free = [None, None], [None, None]
    tp_free, h_free = [None, None], [None, None]
    xn_used, xt_used, h_out = [None, None], [None, None], [None, None]
    gram_banks = (c.banks[4], c.banks[5])
    g_done = None

    def fetch(k):
        s, n = SUPERS[k]
        b = k % 2
        load[b] = s_x[b].dma(c.sp, lambda e: e.dma_start(
            xs[b][:, 0:n, :], x[s * P:(s + n) * P, :].rearrange("(t p) d -> p t d", p=P)), xs_free[b])

    fetch(0)
    hcount = 0
    for k, (s, n) in enumerate(SUPERS):
        b = k % 2
        if k + 1 < len(SUPERS):
            fetch(k + 1)
        normed = layernorm(c, xs[b], xn[b], st, n, [load[b]], [xn_used[b], s_xn[b].last()])
        xs_free[b] = normed
        s_xn[b].dma(c.sp, lambda e: e.dma_start(
            xn_d[s * P:(s + n) * P, :].rearrange("(t p) d -> p t d", p=P), xn[b][:, 0:n, 0:D]), normed)
        turned = turn(c, xn[b], xt[b], n, c.banks[0:2], normed, tp_free, [xt_used[b], s_xt[b].last()])
        s_xt[b].dma(c.sp, lambda e: e.dma_start(
            xnt_d.rearrange("(k p) n -> p k n", p=P)[:, :, s * P:(s + n) * P], xt[b][:, :, 0:n * P]), turned)
        for i in range(n):
            hb = hcount % 2
            bank = c.banks[2 + hb]
            c.pe.wait(turned, scores_ready, h_free[hb])
            for kk in range(KD):
                t = c.pe.run(lambda e: e.matmul(bank[:, 0:ROW], xt[b][:, kk, i * P:(i + 1) * P], wcat[:, kk, :],
                                                start=(kk == 0), stop=(kk == KD - 1)))
            h_free[hb] = c.act.run(lambda e: e.activation(hr[b][:, i, :], bank[:, 0:ROW], ACT.Copy), t, s_h[b].last())
            hcount += 1
        xt_used[b] = t
        s_h[b].dma(c.sp, lambda e: e.dma_start(
            table[s * P:(s + n) * P, :].rearrange("(t p) d -> p t d", p=P), hr[b][:, 0:n, :]), h_free[hb])
        for i in range(n):
            for m in range(KD):
                g_done = c.pe.run(lambda e: e.matmul(
                    gram_banks[m][:, 0:D + 1], xn[b][:, i, m * P:(m + 1) * P], xn[b][:, i, :],
                    start=(s + i == 0), stop=(s + i == TILES - 1)))
        xn_used[b] = g_done
    for m in range(KD):
        c.dve.run(lambda e: e.tensor_copy(gram[:, m, :], gram_banks[m][:, 0:D + 1]), g_done)


def mix_weights_stage(c, gram, wqkv, bqkv, wqa, bqa):
    nc = c.nc
    A = nc.alloc_sbuf_tensor
    w = A("wqkv_s", [P, KD, 3 * D], F32)
    brow = A("bqkv_row", [1, 3 * D], F32)
    bqc = A("bq_col", [P, KD], F32)
    u = A("mix_u", [P, KD, D], F32)
    srow = A("mix_srow", [1, D], F32)
    rrow = A("mix_rrow", [1, D], F32)
    att = A("mix_att", [P, KD, P], F32)
    attt = A("mix_attt", [P, KD, P], F32)
    wqt = A("mix_wqt", [P, KD, D], F32)
    red = A("mix_red", [P, 8], F32)
    s = c.slot("mix_in")
    s.dma(c.sp, lambda e: e.dma_start(w[:, :, :], wqkv.rearrange("(k p) n -> p k n", p=P)))
    s.dma(c.sp, lambda e: e.dma_start(brow[:, :], bqkv.unsqueeze(0)))
    ready = s.dma(c.sp, lambda e: e.dma_start(bqc[:, :], bqkv[0:D].rearrange("(k p) -> p k", p=P)))
    pe, v, bk = c.pe, c.dve, c.banks
    pe.wait(ready)
    for m in range(KD):
        t = pe.run(lambda e: e.transpose(bk[0][0:1, m * P:(m + 1) * P], gram[:, m, D:D + 1], c.ident[:, :]))
    t = v.run(lambda e: e.tensor_copy(srow[:, :], bk[0][0:1, 0:D]), t)
    for m in range(KD):
        pe.wait(t)
        for k in range(KD):
            pe.run(lambda e: e.matmul(bk[1 + m][:, 0:D], gram[:, k, m * P:(m + 1) * P], w[:, k, 2 * D:3 * D],
                                      start=(k == 0), stop=False))
        q = pe.run(lambda e: e.matmul(bk[1 + m][:, 0:D], srow[0:1, m * P:(m + 1) * P], brow[0:1, 2 * D:3 * D],
                                      start=False, stop=True))
        v.run(lambda e: e.tensor_copy(u[:, m, :], bk[1 + m][:, 0:D]), q)
    for k in range(KD):
        q = pe.run(lambda e: e.matmul(bk[3][0:1, 0:D], gram[:, k, D:D + 1], w[:, k, 2 * D:3 * D],
                                      start=(k == 0), stop=(k == KD - 1)))
    t = v.run(lambda e: e.scalar_tensor_tensor(out=rrow[:, :], in0=brow[0:1, 2 * D:3 * D], scalar=float(N_NODES),
                                               in1=bk[3][0:1, 0:D], op0=ALU.mult, op1=ALU.add), q)
    t0 = v.run(lambda e: e.memset(att[:, :, :], 0.0))
    for m in range(KD):
        pe.wait(t)
        for k in range(KD):
            pe.run(lambda e: e.matmul(bk[4 + m][:, 0:D], w[:, k, D + m * P:D + (m + 1) * P], u[:, k, :],
                                      start=(k == 0), stop=False))
        q = pe.run(lambda e: e.matmul(bk[4 + m][:, 0:D], brow[0:1, D + m * P:D + (m + 1) * P], rrow[:, :],
                                      start=False, stop=True))
        scale = float(MIX_HD) ** -0.5
        for hh in range(2):
            r = slice(hh * MIX_HD, (hh + 1) * MIX_HD)
            col = (2 * m + hh) * MIX_HD
            sc = bk[4 + m][r, col:col + MIX_HD]
            o = att[r, m, hh * MIX_HD:(hh + 1) * MIX_HD]
            x = v.run(lambda e: e.tensor_reduce(red[r, 0:1], sc, AX, ALU.max), q, t0)
            x = v.run(lambda e: e.tensor_scalar(red[r, 1:2], red[r, 0:1], -scale, None, ALU.mult), x)
            x = c.act.run(lambda e: e.activation(o, sc, ACT.Exp, bias=red[r, 1:2], scale=scale), x)
            x = v.run(lambda e: e.tensor_reduce(red[r, 2:3], o, AX, ALU.add), x)
            x = v.run(lambda e: e.reciprocal(red[r, 3:4], red[r, 2:3]), x)
            x = v.run(lambda e: e.tensor_scalar(o, o, red[r, 3:4], None, ALU.mult), x)
    for m in range(KD):
        q = pe.run(lambda e: e.transpose(bk[6][:, m * P:(m + 1) * P], att[:, m, :], c.ident[:, :]), x)
    x = v.run(lambda e: e.tensor_copy(attt[:, :, :], bk[6][:, 0:D].rearrange("p (m e) -> p m e", m=KD)), q)
    for m in range(KD):
        for i in range(KD):
            q = pe.run(lambda e: e.transpose(bk[7][:, m * D + i * P:m * D + (i + 1) * P], w[:, i, m * P:(m + 1) * P],
                                             c.ident[:, :]))
    x = v.run(lambda e: e.tensor_copy(wqt[:, :, :], bk[7][:, :].rearrange("p (m i) -> p m i", m=KD)), q)
    pe.wait(x)
    for i in range(KD):
        for m in range(KD):
            q = pe.run(lambda e: e.matmul(bk[i][:, m * P:(m + 1) * P], wqt[:, m, i * P:(i + 1) * P], attt[:, m, :],
                                          start=True, stop=True))
        v.run(lambda e: e.tensor_copy(wqa[:, i, :], bk[i][:, 0:D]), q)
    for m in range(KD):
        q = pe.run(lambda e: e.matmul(bk[2][0:1, m * P:(m + 1) * P], bqc[:, m:m + 1], attt[:, m, :],
                                      start=True, stop=True))
    v.run(lambda e: e.tensor_copy(bqa[:, :], bk[2][0:1, 0:D]), q)


def fragment_rows(c, q, node, out, n, ready):
    A = c.nc.alloc_sbuf_tensor
    qi, loc, ch, far, sel = (A(f"fr{n}_{i}", [P, n], dt) for i, dt in enumerate((I32, I32, I32, F32, F32)))
    v = c.dve
    t = v.run(lambda e: e.tensor_copy(qi[:, :], q[:, 0:n]), ready)
    t1 = v.run(lambda e: e.tensor_scalar(loc[:, :], qi[:, :], P - 1, None, ALU.bitwise_and), t)
    t = v.run(lambda e: e.tensor_scalar(ch[:, :], qi[:, :], 7, 5, ALU.logical_shift_right, ALU.logical_shift_left), t)
    t = v.run(lambda e: e.tensor_tensor(q[:, 0:n], ch[:, :], loc[:, :], ALU.add), t, t1)
    t2 = v.run(lambda e: e.tensor_scalar(sel[:, :], loc[:, :], float(NEAR), None, ALU.is_ge), t1)
    t = v.run(lambda e: e.scalar_tensor_tensor(out=far[:, :], in0=node, scalar=float(FAR), in1=q[:, 0:n], op0=ALU.add,
                                               op1=ALU.subtract), t)
    t = v.run(lambda e: e.tensor_tensor(far[:, :], far[:, :], sel[:, :], ALU.mult), t, t2)
    return v.run(lambda e: e.tensor_tensor(out[:, :], far[:, :], q[:, 0:n], ALU.add), t)


def index_stage(c, dst, src, table, rows_d, sdst_d, g):
    nc = c.nc
    A = nc.alloc_sbuf_tensor
    di = A("dst_i", [P, BLOCKS, P], I32)
    si = A("src_i", [P, BLOCKS, P], I32)
    fl = A("dfl_f", [P, 2, BLOCKS], F32)
    fli = A("dfl_i", [P, 2, BLOCKS], I32)
    tmp = [A(f"ix_tmp{b}", [P, P], F32) for b in range(2)]
    junk = A("ix_rows", [P, 2 * BLOCKS, ROW], F32)
    sd = A("ix_sd", [P, 2, BLOCKS, GH], F32)
    sdg = A("ix_sdg", [GROUPS, 2, P], F32)
    dkey = A("ix_key", [P, CHUNKS], F32)
    cnum = A("ix_cnum", [P, CHUNKS], F32)
    wide = A("ix_cmp", [P, CHUNKS], F32)
    nid = A("ix_nid", [P, TILES], F32)
    nf = A("ix_nf", [P, TILES], F32)
    cn = A("ix_cn", [P, BLOCKS], F32)
    s1, s2, s3, s4, s5 = (c.slot(f"ix_{i}") for i in range(5))
    v, pe = c.dve, c.pe
    s1.dma(c.sp, lambda e: e.dma_start(di[:, :, :], dst.rearrange("(b c) e -> c b e", c=P)))
    t = s1.dma(c.sp, lambda e: e.dma_start(si[:, :, :], src.rearrange("(b c) e -> c b e", c=P)))
    for j, col in ((0, 0), (1, P - 1)):
        v.run(lambda e: e.tensor_copy(fl[:, j, :], di[:, :, col]), t)
        f = v.run(lambda e: e.tensor_copy(fli[:, j, :], di[:, :, col]), t)
    w = s2.dma(c.sp, lambda e: e.dma_start(rows_d.rearrange("j (b c) -> c j b", c=P), fl[:, :, :]), f)
    for j, to in ((0, g["dfb"]), (1, g["dlb"])):
        w2 = s3.dma(c.sp, lambda e: e.dma_start(to[:, :], rows_d[j].partition_broadcast(P)), w)
    free = [None, None]
    n = 0
    for b in range(BLOCKS):
        for what in range(2):
            u = n % 2
            if what == 0:
                t = v.run(lambda e: e.tensor_scalar(tmp[u][:, :], di[:, b, :], fl[:, 0, b:b + 1], None, ALU.subtract),
                          f, free[u])
            else:
                t = v.run(lambda e: e.tensor_copy(tmp[u][:, :], si[:, b, :]), free[u])
            t = pe.run(lambda e: e.transpose(c.banks[u][:, 0:P], tmp[u][:, :], c.ident[:, :]), t)
            to = (g["loc"], g["srcix"])[what]
            free[u] = v.run(lambda e: e.tensor_copy(to[:, b * P:(b + 1) * P], c.banks[u][:, 0:P]), t)
            n += 1
    for j in range(2):
        for b in range(BLOCKS):
            t = s4.dma(c.pool, lambda e: e.indirect_dma_start(
                out=junk[:, j * BLOCKS + b, :], out_offset=None, in_=table[:, :],
                in_offset=bass.IndirectOffsetOnAxis(ap=fli[:, j, b:b + 1], axis=0)), f)
    t = v.run(lambda e: e.tensor_copy(sd[:, :, :, :], junk[:, :, D + GH:ROW].rearrange("p (j b) h -> p j b h", j=2)), t)
    for j in range(2):
        t2 = s2.dma(c.sp, lambda e: e.dma_start(sdst_d[j].rearrange("(b c) h -> c b h", c=P), sd[:, j, :, :]), t)
    t = s5.dma(c.sp, lambda e: e.dma_start(sdg[:, :, :], sdst_d.rearrange("j (g c) h -> g j (c h)", c=CB)), t2)
    for j in range(2):
        t = pe.run(lambda e: e.transpose(c.banks[2 + j][:, 0:GROUPS], sdg[:, j, :], c.ident[0:GROUPS, 0:GROUPS]), t)
        v.run(lambda e: e.tensor_copy(g["sdedge"][:, j, :], c.banks[2 + j][:, 0:GROUPS]), t)
    t = c.pool.run(lambda e: e.iota(cn[:, :], pattern=[[P * P, BLOCKS]], base=0, channel_multiplier=P,
                                    allow_small_or_imprecise_dtypes=True))
    t = v.run(lambda e: e.tensor_tensor(cn[:, :], cn[:, :], fl[:, 1, :], ALU.add), t)
    t = v.run(lambda e: e.tensor_tensor(cn[:, :], cn[:, :], fl[:, 0, :], ALU.subtract), t)
    fragment_rows(c, cn, fl[:, 1, :], g["lastix"], BLOCKS, t)
    t = c.pool.run(lambda e: e.iota(cnum[:, :], pattern=[[P, CHUNKS]], base=0, channel_multiplier=0,
                                    allow_small_or_imprecise_dtypes=True))
    t = v.run(lambda e: e.tensor_tensor(cnum[:, :], cnum[:, :], g["dfb"][:, :], ALU.subtract), t, w2)
    v.run(lambda e: e.tensor_copy(dkey[:, 0:1], cnum[:, 0:1]), t)
    key = v.run(lambda e: e.tensor_tensor(dkey[:, 1:], cnum[:, 1:], cnum[:, 0:CHUNKS - 1], ALU.subtract), t)
    t = c.pool.run(lambda e: e.iota(nid[:, :], pattern=[[P, TILES]], base=0, channel_multiplier=1,
                                    allow_small_or_imprecise_dtypes=True))
    for i in range(TILES):
        t = v.run(lambda e: e.scalar_tensor_tensor(out=wide[:, :], in0=g["dfb"][:, :], scalar=nid[:, i:i + 1],
                                                   in1=dkey[:, :], op0=ALU.is_le, op1=ALU.mult,
                                                   accum_out=nf[:, i:i + 1]), t, key)
    t = v.run(lambda e: e.tensor_tensor(nf[:, :], nf[:, :], nid[:, :], ALU.add), t)
    fragment_rows(c, nf, nid[:, :], g["nodeix"], TILES, t)
    t = v.run(lambda e: e.tensor_tensor(wide[0:1, :], g["dlb"][0:1, :], g["dfb"][0:1, :], ALU.subtract), t)
    t = v.run(lambda e: e.tensor_scalar(wide[0:1, :], wide[0:1, :], float(NEAR), float(FRAGS), ALU.is_lt, ALU.mult), t)
    t = v.run(lambda e: e.tensor_tensor(wide[0:1, :], wide[0:1, :], g["dfb"][0:1, :], ALU.add), t)
    v.run(lambda e: e.tensor_scalar(g["far"][0:1, :], wide[0:1, :], float(N_NODES + 1), float(FAR + NEAR), ALU.min,
                                    ALU.add), t)
    t = v.run(lambda e: e.tensor_reduce(cnum[0:1, 0:GROUPS], wide[0:1, :].rearrange("p (g c) -> p g c", c=CB), AX,
                                        ALU.min), t)
    v.run(lambda e: e.tensor_scalar(g["anyfar"][0:1, :], cnum[0:1, 0:GROUPS], float(N_NODES + 1), None, ALU.is_lt), t)


def edges_stage(c, dst, src, table, frag, g):
    nc = c.nc
    A = nc.alloc_sbuf_tensor
    NB = 3
    rows = [A(f"rows{b}", [P, CB, ROW], F32) for b in range(NB)]
    onehot = [A(f"onehot{b}", [P, CB, P], F32) for b in range(2)]
    fout = [A(f"fout{b}", [P, CB, ROW], F32) for b in range(2)]
    dsr = [A(f"dsr{b}", [P, 2, P], I32) for b in range(NB)]
    sc_e = [A(f"sc_e{b}", [P, 2, P], F32) for b in range(2)]
    brk = A("brk", [P, P + 1], F32)
    neq = A("neq", [P, P + 1], F32)
    notself = A("notself", [P, P], F32)
    sdm, d1, d2, ea, fm = (A(f"g_{n}", [P, P], F32) for n in ("sdm", "d1", "d2", "ea", "fm"))
    mx1, mx = d1, d2
    wgt = A("g_w", [P, P], F32)
    we = [A(f"g_we{b}", [P, 2, P], F32) for b in range(2)]
    s_row = [c.slot(f"rows_in{b}") for b in range(NB)]
    s_ds = [c.slot(f"ds_in{b}") for b in range(NB)]
    s_near = [c.slot(f"near_out{b}") for b in range(2)]
    s_far = [c.slot(f"far_out{b}") for b in range(2)]
    v, pe, act, pool, sp = c.dve, c.pe, c.act, c.pool, c.sp
    in_bank, out_bank, o_banks = c.banks[0], c.banks[1], c.banks[2:4]
    ends = v.run(lambda e: e.memset(neq[:, :], 1.0))
    gathered, rows_free = [None] * NB, [[None] * CB for _ in range(NB)]
    ds_ready, ds_free = [None] * NB, [None] * NB
    in_free = out_free = turned = flags = weighed = fm_done = fm_free = None
    o_free, oh_free, sce_free, we_free = [None] * 2, [None] * 2, [None] * 2, [None] * 2
    oh, weights, tail = [None] * 2, [None] * 2, [None] * 2
    nmm = 0

    def gather(k):
        b = k % NB
        for j in range(CB):
            col = k * CB + j
            gathered[b] = s_row[b].dma(pool, lambda e: e.indirect_dma_start(
                out=rows[b][:, j, :], out_offset=None, in_=table[:, :],
                in_offset=bass.IndirectOffsetOnAxis(ap=g["srcix"][:, col:col + 1], axis=0)), rows_free[b][j])

    def edge_rows(k):
        b = k % NB
        for j, of in enumerate((dst, src)):
            rep = bass.AP(of.tensor, k * CB * P, [[P, CB], [0, GH], [1, P]])
            ds_ready[b] = s_ds[b].dma(sp, lambda e: e.dma_start(dsr[b][:, j, :], rep), ds_free[b])

    def back(a):
        return a[:, ::-1]

    def turn_scores(k):
        nonlocal turned
        r, b = k % NB, k % 2
        t = act.run(lambda e: e.activation(sc_e[b][:, :, :].rearrange("p j (c h) -> p j c h", h=GH),
                                           rows[r][:, :, D:ROW].rearrange("p c (j h) -> p j c h", h=GH), ACT.Copy),
                    gathered[r], sce_free[b])
        pe.wait(t, in_free)
        for j in range(2):
            turned = pe.run(lambda e: e.transpose(in_bank[:, j * P:(j + 1) * P], sc_e[b][:, j, :], c.ident[:, :]))
        sce_free[b] = turned

    def breaks(k):
        nonlocal flags, oh
        b = k % 2
        ds, d = dsr[k % NB], k % NB
        t = v.run(lambda e: e.tensor_tensor(neq[:, 1:P], ds[:, 0, 1:P], ds[:, 0, 0:P - 1], ALU.not_equal),
                  ds_ready[d], ends, fm_free)
        v.run(lambda e: e.tensor_scalar(brk[:, :], neq[:, :], -BIG, None, ALU.mult), t)
        ds_free[d] = flags = v.run(lambda e: e.tensor_tensor(notself[:, :], ds[:, 0, :], ds[:, 1, :], ALU.not_equal))
        oh[b] = v.run(lambda e: e.tensor_tensor(onehot[b][:, :, :], c.ramp[:, :].unsqueeze(1).to_broadcast([P, CB, P]),
                                                g["loc"][:, k * CB:(k + 1) * CB].unsqueeze(2).to_broadcast([P, CB, P]),
                                                ALU.is_equal), oh_free[b])

    def edge_scores(k):
        nonlocal in_free, weighed, fm_done
        t = v.run(lambda e: e.scalar_tensor_tensor(out=sdm[:, :], in0=notself[:, :], scalar=-BIG,
                                                   in1=in_bank[:, P:2 * P], op0=ALU.mult, op1=ALU.add), flags, turned)
        v.run(lambda e: e.tensor_copy(sdm[:, 0:1], g["sdedge"][:, 0, k:k + 1]), t)
        t = v.run(lambda e: e.tensor_copy(sdm[:, P - 1:P], g["sdedge"][:, 1, k:k + 1]), t)
        t = v.run(lambda e: e.tensor_tensor_scan(out=d1[:, :], data0=brk[:, 0:P], data1=sdm[:, :], initial=-BIG,
                                                 op0=ALU.add, op1=ALU.max), t)
        t = v.run(lambda e: e.tensor_tensor_scan(out=back(d2), data0=back(brk[:, 1:P + 1]), data1=back(d1),
                                                 initial=-BIG, op0=ALU.add, op1=ALU.max), t)
        t = v.run(lambda e: e.tensor_tensor(ea[:, :], d2[:, :], in_bank[:, 0:P], ALU.add), t, weighed)
        in_free = t
        t = v.run(lambda e: e.scalar_tensor_tensor(out=ea[:, :], in0=ea[:, :], scalar=SLOPE, in1=ea[:, :],
                                                   op0=ALU.mult, op1=ALU.max), t)
        t = v.run(lambda e: e.tensor_tensor_scan(out=mx1[:, :], data0=brk[:, 0:P], data1=ea[:, :], initial=-BIG,
                                                 op0=ALU.add, op1=ALU.max), t)
        t = v.run(lambda e: e.tensor_tensor_scan(out=back(mx), data0=back(brk[:, 1:P + 1]), data1=back(mx1),
                                                 initial=-BIG, op0=ALU.add, op1=ALU.max), t)
        t1 = v.run(lambda e: e.tensor_tensor(ea[:, :], ea[:, :], mx[:, :], ALU.subtract), t)
        fm_done = v.run(lambda e: e.tensor_tensor(fm[:, :], mx[:, :], neq[:, 0:P], ALU.mult), t, fm_free)
        weighed = act.run(lambda e: e.activation(wgt[:, :], ea[:, :], ACT.Exp), t1, fm_free)

    def turn_weights(k):
        nonlocal fm_free, out_free
        r, b = k % NB, k % 2
        pe.wait(weighed, fm_done, out_free)
        for j, a in enumerate((wgt, fm)):
            fm_free = pe.run(lambda e: e.transpose(out_bank[:, j * P:(j + 1) * P], a[:, :], c.ident[:, :]))
        out_free = weights[b] = act.run(lambda e: e.activation(
            we[b][:, :, :], out_bank[:, 0:2 * P].rearrange("p (j x) -> p j x", j=2), ACT.Copy), fm_free, we_free[b])
        tail[b] = act.run(lambda e: e.activation(rows[r][:, :, D:ROW].rearrange("p c (j h) -> p j c h", h=GH),
                                                 we[b][:, :, :].rearrange("p j (c h) -> p j c h", h=GH), ACT.Copy),
                          weights[b])

    def sums(k, q):
        nonlocal nmm
        r, b = k % NB, k % 2
        R, n = rows[r], CB // 4
        q *= n
        hv = R[:, q:q + n, 0:D].rearrange("p c (h f) -> p c h f", f=GF)
        wv = we[b][:, 0, q * GH:(q + n) * GH].rearrange("p (c h) -> p c h", h=GH)
        t = v.run(lambda e: e.tensor_tensor(hv, hv, wv.unsqueeze(3).to_broadcast([P, n, GH, GF]), ALU.mult), weights[b])
        pe.wait(t, tail[b], oh[b])
        for j in range(q, q + n):
            ob = nmm % 2
            rows_free[r][j] = pe.run(lambda e: e.matmul(o_banks[ob][:, 0:ROW], onehot[b][:, j, :], R[:, j, :],
                                                        start=True, stop=True), o_free[ob])
            o_free[ob] = act.run(lambda e: e.activation(fout[b][:, j, :], o_banks[ob][:, 0:ROW], ACT.Copy),
                                 rows_free[r][j], s_near[b].last(), s_far[b].last())
            nmm += 1
        we_free[b] = [t, tail[b]]
        oh_free[b] = rows_free[r][j]

    def store(k):
        b = k % 2
        ready = act.last()
        near = frag[k * CB * NEAR:(k + 1) * CB * NEAR, :].rearrange("(c l) f -> l c f", l=NEAR)
        s_near[b].dma(act, lambda e: e.dma_start(near, fout[b][0:NEAR, :, :]), ready)
        eng, far = sp.engine, s_far[b]
        is_wide = eng.value_load(g["anyfar"][0:1, k:k + 1], min_val=0, max_val=1)
        with eng.If(is_wide > 0):
            eng.wait_ge(ready[0], ready[1])
            for j in range(CB):
                at = eng.value_load(g["far"][0:1, k * CB + j:k * CB + j + 1], min_val=FAR + NEAR, max_val=NOT_WIDE)
                eng.dma_start(frag[bass.ds(at, P - NEAR), :], fout[b][NEAR:P, j, :], cond=at < NOT_WIDE,
                              bounds_check="skip_entire_dma").then_inc(far.sem, 16)
                eng.wait_ge(far.sem, far.count + 16 * (j + 1))
        with eng.Else():
            eng.sem_inc(far.sem, 16 * CB)
        far.count += 16 * CB

    gather(0)
    gather(1)
    edge_rows(0)
    edge_rows(1)
    turn_scores(0)
    breaks(0)
    edge_scores(0)
    turn_weights(0)
    for k in range(GROUPS):
        more = k + 1 < GROUPS
        if k + 2 < GROUPS:
            gather(k + 2)
            edge_rows(k + 2)
        if more:
            turn_scores(k + 1)
        sums(k, 0)
        if more:
            breaks(k + 1)
        yield
        sums(k, 1)
        if more:
            edge_scores(k + 1)
        yield
        sums(k, 2)
        if more:
            turn_weights(k + 1)
        yield
        sums(k, 3)
        store(k)
        yield


def merge_stage(c, frag, g):
    nc = c.nc
    A = nc.alloc_sbuf_tensor
    first = A("mg_first", [P, BLOCKS, ROW], F32)
    last = A("mg_last", [P, BLOCKS, ROW], F32)
    hm = {n: A(f"mg_{n}", [GH, CHUNKS], F32) for n in
          ("mF", "mL", "sF", "sL", "cont", "cs", "G", "alpha", "beta", "gamma", "delta", "Cm", "tmp", "bs")}
    gs = A("mg_gs", [GH, CHUNKS + 1], F32)
    gp = A("mg_gp", [GH, CHUNKS + 1], F32)
    s_f, s_l, s_o = c.slot("mg_f"), c.slot("mg_l"), c.slot("mg_o")
    v, pe, act = c.dve, c.pe, c.act
    fl = s_f.dma(c.sp, lambda e: e.dma_start(first[:, :, :], frag[0:FAR].rearrange("(b c l) f -> l c b f", c=P, l=NEAR)[0]))
    for b in range(BLOCKS):
        ll = s_l.dma(c.pool, lambda e: e.indirect_dma_start(
            out=last[:, b, :], out_offset=None, in_=frag[:, :],
            in_offset=bass.IndirectOffsetOnAxis(ap=g["lastix"][:, b:b + 1], axis=0)))
    bank_free = [None] * 4
    n = 0
    for b in range(BLOCKS):
        for name, of, col in (("sF", first, D), ("mF", first, D + GH), ("sL", last, D), ("mL", last, D + GH)):
            q = n % 4
            t = pe.run(lambda e: e.transpose(c.banks[q][0:GH, 0:P], of[:, b, col:col + GH], c.ident[:, :]),
                       fl, ll, bank_free[q])
            bank_free[q] = v.run(lambda e: e.tensor_copy(hm[name][:, b * P:(b + 1) * P], c.banks[q][0:GH, 0:P]), t)
            n += 1
    h = {k: a[:, :] for k, a in hm.items()}
    df, dl = g["dfb"][0:GH, :], g["dlb"][0:GH, :]
    tt = lambda o, a, b, op, *w: v.run(lambda e: e.tensor_tensor(o, a, b, op), *w)
    ts = lambda o, a, s1, s2, o1, o2, *w: v.run(lambda e: e.tensor_scalar(o, a, s1, s2, o1, o2), *w)
    t = bank_free[:]
    t = v.run(lambda e: e.memset(hm["cont"][:, 0:1], 0.0), t)
    t = tt(hm["cont"][:, 1:], df[:, 1:], dl[:, 0:CHUNKS - 1], ALU.is_equal, t)
    t = tt(h["cs"], df, dl, ALU.is_equal, t)
    t = tt(h["cs"], h["cs"], h["cont"], ALU.mult, t)
    t = ts(h["tmp"], h["cs"], BIG, -BIG, ALU.mult, ALU.add, t)
    t = v.run(lambda e: e.tensor_tensor_scan(out=gp[:, 1:], data0=h["tmp"], data1=h["mL"], initial=-BIG,
                                             op0=ALU.add, op1=ALU.max), t)
    t = v.run(lambda e: e.memset(gp[:, 0:1], -BIG), t)
    G, Gp = gp[:, 1:], gp[:, 0:CHUNKS]
    t = tt(h["alpha"], Gp, G, ALU.subtract, t)
    t = ts(h["alpha"], h["alpha"], 0.0, None, ALU.min, ALU.bypass, t)
    t = act.run(lambda e: e.activation(h["alpha"], h["alpha"], ACT.Exp), t)
    t = tt(h["alpha"], h["alpha"], h["cs"], ALU.mult, t)
    t = tt(h["beta"], h["mL"], G, ALU.subtract, t)
    t = act.run(lambda e: e.activation(h["beta"], h["beta"], ACT.Exp), t)
    t = ts(h["tmp"], h["cont"], BIG, -BIG, ALU.mult, ALU.add, t)
    t = tt(h["Cm"], Gp, h["tmp"], ALU.add, t)
    t = tt(h["tmp"], h["Cm"], h["mF"], ALU.max, t)
    t = tt(h["gamma"], h["Cm"], h["tmp"], ALU.subtract, t)
    t = act.run(lambda e: e.activation(h["gamma"], h["gamma"], ACT.Exp), t)
    t = tt(h["delta"], h["mF"], h["tmp"], ALU.subtract, t)
    t = act.run(lambda e: e.activation(h["delta"], h["delta"], ACT.Exp), t)
    t = tt(h["bs"], h["beta"], h["sL"], ALU.mult, t)
    t = v.run(lambda e: e.memset(gs[:, 0:1], 0.0), t)
    t = v.run(lambda e: e.tensor_tensor_scan(out=gs[:, 1:], data0=h["alpha"], data1=h["bs"], initial=0.0,
                                             op0=ALU.mult, op1=ALU.add), t)
    t = tt(h["tmp"], h["gamma"], gs[:, 0:CHUNKS], ALU.mult, t)
    t = tt(h["sF"], h["sF"], h["delta"], ALU.mult, t)
    t = tt(h["sF"], h["sF"], h["tmp"], ALU.add, t)
    merged = t
    fT = A("mg_fT", [P, CHUNKS], F32)
    lT = A("mg_lT", [P, CHUNKS], F32)
    run = A("mg_run", [P, CHUNKS + 1], F32)
    W = 416
    bank_free = [None] * 8
    for half in range(KD):
        n = 0
        for b in range(BLOCKS):
            for of, to in ((first, fT), (last, lT)):
                q = n % 4
                t = pe.run(lambda e: e.transpose(c.banks[q][:, 0:P], of[:, b, half * P:(half + 1) * P], c.ident[:, :]),
                           bank_free[q], merged)
                bank_free[q] = v.run(lambda e: e.tensor_copy(to[:, b * P:(b + 1) * P], c.banks[q][:, 0:P]), t)
                n += 1
        t = v.run(lambda e: e.memset(run[:, 0:1], 0.0), bank_free[0:4])
        for w in range(0, CHUNKS, W):
            sl = slice(w, w + W)
            for q, name in enumerate(("alpha", "beta", "gamma", "delta")):
                x = pe.run(lambda e: e.matmul(c.banks[4 + q][:, 0:W], c.headsel[:, half * P:(half + 1) * P],
                                              hm[name][:, sl], start=True, stop=True), merged, bank_free[4 + q])
            al, be, ga, de = (c.banks[4 + q][:, 0:W] for q in range(4))
            t = tt(lT[:, sl], lT[:, sl], be, ALU.mult, t, x, bank_free[0:4])
            t = v.run(lambda e: e.tensor_tensor_scan(out=run[:, w + 1:w + W + 1], data0=al, data1=lT[:, sl],
                                                     initial=run[:, w:w + 1], op0=ALU.mult, op1=ALU.add), t)
            t = tt(lT[:, sl], run[:, sl], ga, ALU.mult, t)
            t = tt(fT[:, sl], fT[:, sl], de, ALU.mult, t)
            for q in range(4):
                bank_free[4 + q] = t
            t = tt(fT[:, sl], fT[:, sl], lT[:, sl], ALU.add, t)
        for b in range(BLOCKS):
            q = b % 4
            x = pe.run(lambda e: e.transpose(c.banks[q][:, 0:P], fT[:, b * P:(b + 1) * P], c.ident[:, :]),
                       t, bank_free[q])
            bank_free[q] = v.run(lambda e: e.tensor_copy(first[:, b, half * P:(half + 1) * P], c.banks[q][:, 0:P]), x)
    for b in range(BLOCKS):
        q = b % 4
        x = pe.run(lambda e: e.transpose(c.banks[q][:, 0:GH], hm["sF"][:, b * P:(b + 1) * P], c.ident[0:GH, 0:GH]),
                   merged, bank_free[q])
        bank_free[q] = v.run(lambda e: e.tensor_copy(first[:, b, D:D + GH], c.banks[q][:, 0:GH]), x)
    s_o.dma(c.sp, lambda e: e.dma_start(frag[0:FAR].rearrange("(b c l) f -> l c b f", c=P, l=NEAR)[0], first[:, :, :]),
            bank_free[0:4])


def mlp_stage(c, x, xn_d, xnt_d, xm_d, wqa, bqa, w_fc1, b_fc1, w_fc2, b_fc2, norm_g, norm_b):
    nc = c.nc
    A = nc.alloc_sbuf_tensor
    w1 = A("fc1_w", [P, KD, MLP], F32)
    w2 = A("fc2_w", [P, MT, D], F32)
    gcol = A("fc_gcol", [P, 2, KD], F32)
    b1 = A("fc1_b", [P, MT], F32)
    b2 = A("fc2_b", [1, D], F32)
    xts = [A(f"m_xt{b}", [P, KD, ST * P], F32) for b in range(2)]
    xns = [A(f"m_xn{b}", [P, ST, D], F32) for b in range(2)]
    xs = A("m_xs", [P, ST, D], F32)
    x2 = A("m_x2", [P, ST, D], F32)
    hnt = A("m_hnt", [P, KD, ST * P], F32)
    hid = A("m_hid", [P, MT, ST * P], F32)
    st = A("m_st", [P, ST, 16], F32)
    s_w, s_xs, s_o = (c.slot(f"m_{n}") for n in ("w", "xs", "o"))
    s_xt, s_xn = ([c.slot(f"m_{n}{b}") for b in range(2)] for n in ("xt", "xn"))
    v, pe, act, sp = c.dve, c.pe, c.act, c.sp
    s_w.dma(sp, lambda e: e.dma_start(w1[:, :, :], w_fc1.rearrange("(k p) n -> p k n", p=P)))
    s_w.dma(sp, lambda e: e.dma_start(w2[:, :, :], w_fc2.rearrange("(k p) n -> p k n", p=P)))
    s_w.dma(sp, lambda e: e.dma_start(gcol[:, 0, :], norm_g.rearrange("(k p) -> p k", p=P)))
    s_w.dma(sp, lambda e: e.dma_start(gcol[:, 1, :], norm_b.rearrange("(k p) -> p k", p=P)))
    s_w.dma(sp, lambda e: e.dma_start(b1[:, :], b_fc1.rearrange("(k p) -> p k", p=P)))
    w = s_w.dma(sp, lambda e: e.dma_start(b2[:, :], b_fc2.unsqueeze(0)))
    bank_t, bank_h, bank_y = c.banks[4:6], c.banks[6], c.banks[7]
    pe.wait(w)
    for m in range(MT):
        for k in range(KD):
            t = pe.run(lambda e: e.matmul(bank_h[:, m:m + 1], w1[:, k, m * P:(m + 1) * P], gcol[:, 1, k:k + 1],
                                          start=(k == 0), stop=(k == KD - 1)))
    t = v.run(lambda e: e.tensor_tensor(b1[:, :], b1[:, :], bank_h[:, 0:MT], ALU.add), t)
    for k in range(KD):
        t = v.run(lambda e: e.tensor_scalar(w1[:, k, :], w1[:, k, :], gcol[:, 0, k:k + 1], None, ALU.mult), t)
    wready = t
    tp_free = [t, t]
    h_free = y_free = t
    xs_used = hnt_used = hid_used = None
    xt_in, xn_in, xt_used, xn_used = [None] * 2, [None] * 2, [None] * 2, [None] * 2

    def fetch(k):
        s, n = SUPERS[k]
        b = k % 2
        rows = slice(s * P, (s + n) * P)
        xt_in[b] = s_xt[b].dma(sp, lambda e: e.dma_start(
            xts[b][:, :, 0:n * P], xnt_d.rearrange("(k p) n -> p k n", p=P)[:, :, rows]), xt_used[b])
        xn_in[b] = s_xn[b].dma(sp, lambda e: e.dma_start(
            xns[b][:, 0:n, :], xn_d[rows].rearrange("(t p) d -> p t d", p=P)), xn_used[b])

    fetch(0)
    for si, (s, n) in enumerate(SUPERS):
        u = si % 2
        rows = slice(s * P, (s + n) * P)
        d = s_xs.dma(sp, lambda e: e.dma_start(xs[:, 0:n, :], x[rows].rearrange("(t p) d -> p t d", p=P)), xs_used)
        if si + 1 < len(SUPERS):
            fetch(si + 1)
        xt, xn, a, b = xts[u], xns[u], xt_in[u], xn_in[u]
        hn = xn
        for i in range(0, n, 2):
            pe.wait(a, y_free)
            for j in range(2):
                for k in range(KD):
                    pe.run(lambda e: e.matmul(bank_y[:, j * D:(j + 1) * D], xt[:, k, (i + j) * P:(i + j + 1) * P], wqa[:, k, :],
                                              start=(k == 0), stop=False))
                t = pe.run(lambda e: e.matmul(bank_y[:, j * D:(j + 1) * D], c.ones[0:1, :], bqa[:, :], start=False, stop=True))
            y_free = v.run(lambda e: e.tensor_tensor(x2[:, i:i + 2, :], bank_y[:, :].rearrange("p (t d) -> p t d", t=2),
                                                     xn[:, i:i + 2, :], ALU.add), t, b, s_o.last())
            yield
        xt_used[u] = t
        normed = layernorm(c, x2, hn, st, n, [y_free], [])
        turned = turn(c, hn, hnt, n, bank_t, normed, tp_free, hnt_used)
        xn_used[u] = pe.last()
        yield
        for m in range(MT):
            pe.wait(turned, wready, h_free)
            for k in range(KD):
                t = pe.run(lambda e: e.matmul(bank_h[:, 0:n * P], w1[:, k, m * P:(m + 1) * P], hnt[:, k, 0:n * P],
                                              start=(k == 0), stop=(k == KD - 1)))
            h_free = act.run(lambda e: e.activation(hid[:, m, 0:n * P], bank_h[:, 0:n * P], ACT.Gelu, bias=b1[:, m:m + 1]),
                             t, hid_used)
            yield
        hnt_used = t
        for i in range(0, n, 2):
            pe.wait(h_free, y_free)
            for j in range(2):
                for m in range(MT):
                    pe.run(lambda e: e.matmul(bank_y[:, j * D:(j + 1) * D], hid[:, m, (i + j) * P:(i + j + 1) * P], w2[:, m, :],
                                              start=(m == 0), stop=False))
                t = pe.run(lambda e: e.matmul(bank_y[:, j * D:(j + 1) * D], c.ones[0:1, :], b2[:, :], start=False, stop=True))
            y_free = v.run(lambda e: e.tensor_tensor(x2[:, i:i + 2, :], bank_y[:, :].rearrange("p (t d) -> p t d", t=2),
                                                     x2[:, i:i + 2, :], ALU.add), t)
            yield
        hid_used = t
        t = v.run(lambda e: e.tensor_tensor(x2[:, 0:n, :], x2[:, 0:n, :], xs[:, 0:n, :], ALU.add), y_free, d)
        xs_used = t
        s_o.dma(sp, lambda e: e.dma_start(xm_d[rows].rearrange("(t p) d -> p t d", p=P), x2[:, 0:n, :]), t)
        yield


def route_stage(c, xm_d, frag, g, sorted_d, x1, gate_w, gate_b, r):
    nc = c.nc
    A = nc.alloc_sbuf_tensor
    gw = A("e_gw", [P, KD, EXPERTS], F32)
    gb = A("e_gb", [1, EXPERTS], F32)
    fr = [A(f"e_fr{b}", [P, ST, ROW], F32) for b in range(2)]
    rs = A("e_rs", [P, ST, GH], F32)
    hn = [A(f"e_hn{b}", [P, ST, D], F32) for b in range(2)]
    hnt = A("e_hnt", [P, KD, ST * P], F32)
    st = A("e_st", [P, ST, 16], F32)
    lg, pr, key, pos, tmp = (A(f"e_{n}", [P, ST, EXPERTS], F32) for n in ("lg", "pr", "key", "pos", "tmp"))
    sel = A("e_sel", [P, 2, ST, EXPERTS], F32)
    both = A("e_both", [P, ST, EXPERTS], F32)
    s1 = A("e_s1", [P, ST, 3], F32)
    posf = A("e_posf", [P, 2, ST], F32)
    before = A("e_before", [P, P], F32)
    rev = A("e_rev", [P, EXPERTS], F32)
    region = A("e_region", [P, EXPERTS], F32)
    carry = r["count"]
    s_w, s_x = c.slot("e_w"), [c.slot(f"e_x{b}") for b in range(2)]
    s_f, s_g = [c.slot(f"e_f{b}") for b in range(2)], [c.slot(f"e_g{b}") for b in range(2)]
    v, pe, act, sp, pool = c.dve, c.pe, c.act, c.sp, c.pool
    for to, of in ((gw[:, :, :], gate_w.rearrange("(k p) n -> p k n", p=P)), (gb[:, :], gate_b.unsqueeze(0))):
        w = s_w.dma(sp, lambda e: e.dma_start(to, of))
    t = pool.run(lambda e: e.memset(before[:, :], 1.0))
    pool.run(lambda e: e.affine_select(out=before[:, :], in_=before[:, :], compare_op=ALU.is_gt, fill=0.0, base=0,
                                       pattern=[[1, P]], channel_multiplier=-1), t)
    pool.run(lambda e: e.iota(rev[:, :], pattern=[[-1, EXPERTS]], base=EXPERTS, channel_multiplier=0,
                              allow_small_or_imprecise_dtypes=True))
    consts = pool.run(lambda e: e.iota(region[:, :], pattern=[[REGION, EXPERTS]], base=0, channel_multiplier=0,
                                       allow_small_or_imprecise_dtypes=True))
    carried = v.run(lambda e: e.memset(carry[:, :], 0.0))
    bank_t, bank_g = c.banks[0:2], c.banks[6:8]
    tp_free, g_free = [None] * 2, [None] * 2
    xin, fin, fr_used, hn_used = [None] * 2, [None] * 2, [None] * 2, [None] * 2
    hnt_used = None

    def fetch(k):
        s, n = SUPERS[k]
        b = k % 2
        xin[b] = s_x[b].dma(sp, lambda e: e.dma_start(
            x1[:, s:s + n, :], xm_d[s * P:(s + n) * P].rearrange("(t p) d -> p t d", p=P)), s_x[b].last())
        for i in range(n):
            fin[b] = s_f[b].dma(pool, lambda e: e.indirect_dma_start(
                out=fr[b][:, i, :], out_offset=None, in_=frag[:, :],
                in_offset=bass.IndirectOffsetOnAxis(ap=g["nodeix"][:, s + i:s + i + 1], axis=0)), fr_used[b])

    def send(k, ready):
        s, n = SUPERS[k]
        b = k % 2
        for i in range(n):
            for j in range(2):
                s_g[b].dma(pool, lambda e: e.indirect_dma_start(
                    out=sorted_d[:, :], out_offset=bass.IndirectOffsetOnAxis(ap=r["row"][:, j, s + i:s + i + 1], axis=0),
                    in_=hn[b][:, i, :], in_offset=None), ready)

    fetch(0)
    for k, (s, n) in enumerate(SUPERS):
        b = k % 2
        if k + 1 < len(SUPERS):
            fetch(k + 1)
        Fr, hn_k = fr[b], hn[b]
        X = x1[:, s:s + n, :]
        t = v.run(lambda e: e.tensor_scalar(rs[:, 0:n, :], Fr[:, 0:n, D:D + GH], SEG_EPS, None, ALU.add), fin[b])
        t = v.run(lambda e: e.reciprocal(rs[:, 0:n, :], rs[:, 0:n, :]), t)
        fv = Fr[:, 0:n, 0:D].rearrange("p t (h f) -> p t h f", f=GF)
        t = v.run(lambda e: e.tensor_tensor(fv, fv, rs[:, 0:n, :].unsqueeze(3).to_broadcast([P, n, GH, GF]), ALU.mult), t)
        t = v.run(lambda e: e.tensor_tensor(X, X, Fr[:, 0:n, 0:D], ALU.add), t, xin[b])
        fr_used[b] = t
        normed = layernorm(c, X, hn_k, st, n, [t], [hn_used[b], s_g[b].last()])
        turned = turn(c, hn_k, hnt, n, bank_t, normed, tp_free, hnt_used)
        hn_used[b] = pe.last()
        pe.wait(w, turned, g_free[0])
        for i in range(n):
            o = bank_g[0][:, i * EXPERTS:(i + 1) * EXPERTS]
            for kk in range(KD):
                pe.run(lambda e: e.matmul(o, hnt[:, kk, i * P:(i + 1) * P], gw[:, kk, :], start=(kk == 0), stop=False))
            t = pe.run(lambda e: e.matmul(o, c.ones[0:1, :], gb[:, :], start=False, stop=True))
        hnt_used = t
        L, Pr, K, T = (a[:, 0:n, :] for a in (lg, pr, key, tmp))
        t = v.run(lambda e: e.tensor_copy(L, bank_g[0][:, 0:n * EXPERTS].rearrange("p (t e) -> p t e", t=n)), t)
        g_free[0] = t
        wide = lambda a: a.to_broadcast([P, n, EXPERTS])
        over_tiles = lambda a: a.unsqueeze(1).to_broadcast([P, n, EXPERTS])
        t = v.run(lambda e: e.tensor_reduce(s1[:, 0:n, 0], L, AX, ALU.max), t)
        t = v.run(lambda e: e.tensor_tensor(L, L, wide(s1[:, 0:n, 0:1]), ALU.subtract), t)
        t = act.run(lambda e: e.activation(Pr, L, ACT.Exp), t)
        t = v.run(lambda e: e.tensor_reduce(s1[:, 0:n, 1], Pr, AX, ALU.add), t)
        t = v.run(lambda e: e.reciprocal(s1[:, 0:n, 2], s1[:, 0:n, 1]), t)
        t = v.run(lambda e: e.tensor_tensor(Pr, Pr, wide(s1[:, 0:n, 2:3]), ALU.mult), t)
        for j in range(2):
            top, rank = r["weight"][:, j, s:s + n], r["rev"][:, j, s:s + n]
            S = sel[:, j, 0:n, :]
            t = v.run(lambda e: e.tensor_reduce(top, Pr, AX, ALU.max), t)
            t = v.run(lambda e: e.tensor_tensor(K, Pr, wide(top.unsqueeze(2)), ALU.is_equal), t)
            t = v.run(lambda e: e.tensor_tensor(K, K, over_tiles(rev[:, :]), ALU.mult), t, consts)
            t = v.run(lambda e: e.tensor_reduce(rank, K, AX, ALU.max), t)
            t = v.run(lambda e: e.tensor_tensor(S, K, wide(rank.unsqueeze(2)), ALU.is_equal), t)
            if j == 0:
                t = v.run(lambda e: e.scalar_tensor_tensor(out=Pr, in0=S, scalar=-2.0, in1=Pr, op0=ALU.mult, op1=ALU.add), t)
        t = v.run(lambda e: e.tensor_tensor(both[:, 0:n, :], sel[:, 0, 0:n, :], sel[:, 1, 0:n, :], ALU.add), t)
        B = both[:, 0:n, :].rearrange("p t e -> p (t e)")
        pe.wait(t, g_free[1])
        pe.run(lambda e: e.matmul(bank_g[1][:, 0:n * EXPERTS], before[:, :], B, start=True, stop=True))
        t = pe.run(lambda e: e.matmul(bank_g[1][:, P:P + n * EXPERTS], c.ones[:, :], B, start=True, stop=True))
        for i in range(n):
            t = v.run(lambda e: e.tensor_tensor(pos[:, i, :], bank_g[1][:, i * EXPERTS:(i + 1) * EXPERTS], carry[:, :],
                                                ALU.add), t, carried)
            t = carried = v.run(lambda e: e.tensor_tensor(carry[:, :], carry[:, :],
                                                          bank_g[1][:, P + i * EXPERTS:P + (i + 1) * EXPERTS], ALU.add), t)
        g_free[1] = t
        t = v.run(lambda e: e.tensor_tensor(pos[:, 0:n, :], pos[:, 0:n, :], over_tiles(region[:, :]), ALU.add), t)
        for j in range(2):
            t = v.run(lambda e: e.tensor_tensor(T, pos[:, 0:n, :], sel[:, j, 0:n, :], ALU.mult), t)
            t = v.run(lambda e: e.tensor_reduce(posf[:, j, 0:n], T, AX, ALU.add), t)
        t = v.run(lambda e: e.tensor_copy(r["row"][:, :, s:s + n], posf[:, :, 0:n]), t)
        send(k, t)


def plan_stage(c, r, sorted_d):
    nc = c.nc
    A = nc.alloc_sbuf_tensor
    v, pool = c.dve, c.pool
    ci = A("pl_ci", [P, EXPERTS], I32)
    tiles, ends, starts = (A(f"pl_{n}", [P, EXPERTS], F32) for n in ("tiles", "ends", "starts"))
    region, shift = A("pl_region", [P, EXPERTS], F32), A("pl_shift", [P, EXPERTS], F32)
    step = A("pl_step", [P, EXPERTS], F32)
    endrow = A("pl_endrow", [1, EXPERTS], I32)
    num = A("pl_num", [1, SLOTS], F32)
    ge, row, ex = (A(f"pl_{n}", [1, SLOTS], F32) for n in ("ge", "row", "ex"))
    hit = A("pl_hit", [P, 2, TILES], F32)
    res = A("pl_res", [P, 2, TILES], F32)
    zero = A("pl_zero", [P, D], F32)
    s_z = c.slot("pl_z")
    z = v.run(lambda e: e.memset(zero[:, :], 0.0))
    s_z.dma(c.sp, lambda e: e.dma_start(sorted_d[EXPERTS * REGION:, :], zero[:, :]), z)
    t1 = pool.run(lambda e: e.iota(region[:, :], pattern=[[REGION, EXPERTS]], base=0, channel_multiplier=0,
                                   allow_small_or_imprecise_dtypes=True))
    t1 = pool.run(lambda e: e.iota(num[:, :], pattern=[[1, SLOTS]], base=0, channel_multiplier=0,
                                   allow_small_or_imprecise_dtypes=True))
    t = v.run(lambda e: e.tensor_scalar(ci[:, :], r["count"][:, :], float(P - 1), None, ALU.add), z)
    t = v.run(lambda e: e.tensor_single_scalar(ci[:, :], ci[:, :], 7, ALU.logical_shift_right), t)
    t = v.run(lambda e: e.tensor_copy(tiles[:, :], ci[:, :]), t)
    t = v.run(lambda e: e.tensor_tensor_scan(out=ends[:, :], data0=c.ones[:, 0:EXPERTS], data1=tiles[:, :], initial=0.0,
                                             op0=ALU.mult, op1=ALU.add), t)
    t = v.run(lambda e: e.tensor_tensor(starts[:, :], ends[:, :], tiles[:, :], ALU.subtract), t)
    t = v.run(lambda e: e.scalar_tensor_tensor(out=shift[:, :], in0=starts[:, :], scalar=float(P), in1=region[:, :],
                                               op0=ALU.mult, op1=ALU.subtract), t, t1)
    v.run(lambda e: e.tensor_copy(step[:, 0:1], shift[:, 0:1]), t)
    t = v.run(lambda e: e.tensor_tensor(step[:, 1:], shift[:, 1:], shift[:, 0:EXPERTS - 1], ALU.subtract), t)
    e1 = v.run(lambda e: e.memset(ex[:, :], 0.0))
    t = v.run(lambda e: e.tensor_scalar(row[:, :], num[:, :], float(P), None, ALU.mult), t)
    for k in range(1, EXPERTS):
        q = v.run(lambda e: e.tensor_scalar(ge[:, :], num[:, :], starts[0:1, k:k + 1], None, ALU.is_ge), t, e1)
        e1 = v.run(lambda e: e.tensor_tensor(ex[:, :], ex[:, :], ge[:, :], ALU.add), q)
        q = v.run(lambda e: e.tensor_scalar(ge[:, :], ge[:, :], step[0:1, k:k + 1], None, ALU.mult), e1)
        t = v.run(lambda e: e.tensor_tensor(row[:, :], row[:, :], ge[:, :], ALU.subtract), q)
    v.run(lambda e: e.tensor_copy(r["expert"][:, :], ex[:, :]), e1)
    zrow = float(EXPERTS * REGION)
    q = v.run(lambda e: e.tensor_scalar(ge[:, :], num[:, :], ends[0:1, EXPERTS - 1:EXPERTS], None, ALU.is_lt), t)
    t = v.run(lambda e: e.tensor_scalar(row[:, :], row[:, :], -zrow, None, ALU.add), t)
    t = v.run(lambda e: e.tensor_tensor(row[:, :], row[:, :], ge[:, :], ALU.mult), t, q)
    t = v.run(lambda e: e.tensor_scalar(r["tile_row"][:, :], row[:, :], zrow, None, ALU.add), t)
    t = v.run(lambda e: e.tensor_tensor(endrow[:, :], region[0:1, :], r["count"][0:1, :], ALU.add), t)
    c.sp.wait(t, *[x.last() for x in c.slots])
    for k in range(EXPERTS):
        at = c.sp.engine.value_load(endrow[0:1, k:k + 1], min_val=k * REGION, max_val=(k + 1) * REGION - P)
        s_z.dma(c.sp, lambda e: e.dma_start(sorted_d[bass.ds(at, P), :], zero[:, :]))
    t = v.run(lambda e: e.tensor_copy(res[:, :, :], r["row"][:, :, :]), t)
    for k in range(EXPERTS):
        q = v.run(lambda e: e.tensor_scalar(hit[:, :, :], r["rev"][:, :, :], float(EXPERTS - k), None, ALU.is_equal), t)
        t = v.run(lambda e: e.scalar_tensor_tensor(out=res[:, :, :], in0=hit[:, :, :], scalar=shift[:, k:k + 1],
                                                   in1=res[:, :, :], op0=ALU.mult, op1=ALU.add), q)
    v.run(lambda e: e.tensor_copy(r["result"][:, :, :], res[:, :, :]), t)


def experts_stage(c, r, sorted_d, result_d, w1, w2, eb1, eb2, weights):
    nc = c.nc
    A = nc.alloc_sbuf_tensor
    b1 = A("x_b1", [P, EXPERTS, HID], F32)
    b2 = A("x_b2", [P, EXPERTS, D], F32)
    NB = 2
    gin = [A(f"x_in{b}", [P, D], F32) for b in range(NB)]
    gt = [A(f"x_int{b}", [P, D], F32) for b in range(2)]
    hb = [A(f"x_h{b}", [P, HID], F32) for b in range(2)]
    ht = [A(f"x_ht{b}", [P, HID], F32) for b in range(2)]
    y = [A(f"x_y{b}", [P, D], F32) for b in range(2)]
    s_b, s_in, s_y = c.slot("x_b"), [c.slot(f"x_in{b}") for b in range(NB)], [c.slot(f"x_y{b}") for b in range(2)]
    v, pe, act, sp = c.dve, c.pe, c.act, c.sp
    s_b.dma(sp, lambda e: e.dma_start(b1[:, :, :].rearrange("p e n -> p (e n)"),
                                      eb1.rearrange("e n -> (e n)").partition_broadcast(P)))
    bias = s_b.dma(sp, lambda e: e.dma_start(b2[:, :, :].rearrange("p e n -> p (e n)"),
                                             eb2.rearrange("e n -> (e n)").partition_broadcast(P)))
    in_bank, h_bank, t_bank, y_bank = c.banks[0:2], c.banks[2:4], c.banks[4:6], c.banks[6:8]
    loaded, gin_free = [None] * NB, [None] * NB
    in_turned, in_ready, fc1_done, fc2_done = {}, {}, {}, {}
    h_ready, h_turned, ht_ready, y_read = {}, {}, {}, {}
    pre_read = {}
    last = SLOTS - 1

    def fetch(j):
        b = j % NB
        at = sp.engine.value_load(r["tile_row"][0:1, j:j + 1], min_val=0, max_val=EXPERTS * REGION)
        loaded[b] = s_in[b].dma(sp, lambda e: e.dma_start(gin[b][:, :], sorted_d[bass.ds(at, P), :]), in_turned.get(j - NB))

    def turn_in(j):
        u = j % 2
        pe.wait(loaded[j % NB], in_ready.get(j - 2))
        for k in range(KD):
            in_turned[j] = pe.run(lambda e: e.transpose(in_bank[u][:, k * P:(k + 1) * P], gin[j % NB][:, k * P:(k + 1) * P],
                                                        c.ident[:, :]))
        in_ready[j] = act.run(lambda e: e.activation(gt[u][:, :], in_bank[u][:, 0:D], ACT.Copy), in_turned[j],
                              fc1_done.get(j - 2))

    def first(j):
        u = j % 2
        ex = pe.engine.value_load(r["expert"][0:1, j:j + 1], min_val=0, max_val=EXPERTS - 1)
        pe.wait(in_ready[j], weights, pre_read.get(j - 2))
        for k in range(KD):
            fc1_done[j] = pe.run(lambda e: e.matmul(h_bank[u][:, :], gt[u][:, k * P:(k + 1) * P],
                                                    w1[:, bass.ds(ex * KD + k, 1), :], start=(k == 0), stop=(k == KD - 1)))
        exv = v.engine.value_load(r["expert"][0:1, j:j + 1], min_val=0, max_val=EXPERTS - 1)
        pre_read[j] = v.run(lambda e: e.tensor_tensor(hb[u][:, :], h_bank[u][:, :],
                                                      b1[:, bass.ds(exv, 1), :].rearrange("p a n -> p (a n)"), ALU.add),
                            fc1_done[j], bias, h_turned.get(j - 2))
        h_ready[j] = act.run(lambda e: e.activation(hb[u][:, :], hb[u][:, :], ACT.Gelu), pre_read[j])

    def turn_h(j):
        u = j % 2
        pe.wait(h_ready[j], ht_ready.get(j - 2))
        for m in range(HT):
            h_turned[j] = pe.run(lambda e: e.transpose(t_bank[u][:, m * P:(m + 1) * P], hb[u][:, m * P:(m + 1) * P],
                                                       c.ident[:, :]))
        ht_ready[j] = act.run(lambda e: e.activation(ht[u][:, :], t_bank[u][:, :], ACT.Copy), h_turned[j],
                              fc2_done.get(j - 2))

    def second(j):
        u = j % 2
        ex = pe.engine.value_load(r["expert"][0:1, j:j + 1], min_val=0, max_val=EXPERTS - 1)
        pe.wait(ht_ready[j], y_read.get(j - 2))
        for m in range(HT):
            fc2_done[j] = pe.run(lambda e: e.matmul(y_bank[u][:, 0:D], ht[u][:, m * P:(m + 1) * P],
                                                    w2[:, bass.ds(ex * HT + m, 1), :], start=(m == 0), stop=(m == HT - 1)))
        exv = v.engine.value_load(r["expert"][0:1, j:j + 1], min_val=0, max_val=EXPERTS - 1)
        y_read[j] = v.run(lambda e: e.tensor_tensor(y[u][:, :], y_bank[u][:, 0:D],
                                                    b2[:, bass.ds(exv, 1), :].rearrange("p a n -> p (a n)"), ALU.add),
                          fc2_done[j], bias, s_y[u].last())
        s_y[u].dma(sp, lambda e: e.dma_start(result_d[j * P:(j + 1) * P, :], y[u][:, :]), y_read[j])

    fetch(0)
    fetch(1)
    turn_in(0)
    for j in range(SLOTS + 1):
        if j + 2 <= last:
            fetch(j + 2)
        if j >= 1:
            turn_h(j - 1)
        if j <= last:
            first(j)
        if j + 1 <= last:
            turn_in(j + 1)
        if j >= 1:
            second(j - 1)


def combine_stage(c, r, result_d, x1, out):
    nc = c.nc
    A = nc.alloc_sbuf_tensor
    NB = 3
    ys = [A(f"c_y{b}", [P, 2, ST, D], F32) for b in range(NB)]
    s_y, s_o = [c.slot(f"c_y{b}") for b in range(NB)], c.slot("c_o")
    v = c.dve
    used, here = [None] * NB, [None] * NB

    def fetch(k):
        s, n = SUPERS[k]
        b = k % NB
        for i in range(n):
            for j in range(2):
                here[b] = s_y[b].dma(c.pool, lambda e: e.indirect_dma_start(
                    out=ys[b][:, j, i, :], out_offset=None, in_=result_d[:, :],
                    in_offset=bass.IndirectOffsetOnAxis(ap=r["result"][:, j, s + i:s + i + 1], axis=0)), used[b])

    fetch(0)
    fetch(1)
    for k, (s, n) in enumerate(SUPERS):
        b = k % NB
        if k + 2 < len(SUPERS):
            fetch(k + 2)
        t = here[b]
        for j in range(2):
            for i in range(n):
                x = v.run(lambda e: e.scalar_tensor_tensor(
                    out=x1[:, s + i, :], in0=ys[b][:, j, i, :], scalar=r["weight"][:, j, s + i:s + i + 1],
                    in1=x1[:, s + i, :], op0=ALU.mult, op1=ALU.add), t)
            t = x
        used[b] = t
        lo, hi = s * P, min((s + n) * P, N_NODES)
        full = (hi - lo) // P
        s_o.dma(c.sp, lambda e: e.dma_start(out[lo:lo + full * P].rearrange("(t p) d -> p t d", p=P), x1[:, s:s + full, :]), t)
        if hi - lo > full * P:
            s_o.dma(c.sp, lambda e: e.dma_start(out[lo + full * P:hi], x1[0:hi - lo - full * P, s + full, :]), t)


def build(nc, a, out, stop=None):
    c = Core(nc)
    dram = lambda name, shape: nc.dram_tensor(name, shape, F32, kind="Internal").ap()
    table = dram("table", [N_PAD, ROW])
    xn_d = dram("xn_d", [N_PAD, D])
    xnt_d = dram("xnt_d", [D, N_PAD])
    xm_d = dram("xm_d", [N_PAD, D])
    frag = dram("frag", [FRAGS, ROW])
    rows_d = dram("rows_d", [2, CHUNKS])
    sorted_d = dram("sorted_d", [EXPERTS * REGION + P, D])
    result_d = dram("result_d", [SLOTS * P, D])
    sdst_d = dram("sdst_d", [2, CHUNKS, GH])
    A = nc.alloc_sbuf_tensor
    constants(c)
    nodeix = A("nodeix", [P, TILES], I32)
    keep = nc.sbuf_base
    gram = A("gram", [P, KD, D + 1], F32)
    wqa, bqa = A("wqa", [P, KD, D], F32), A("bqa", [1, D], F32)
    g = {"dfb": A("dfb", [P, CHUNKS], F32), "dlb": A("dlb", [P, CHUNKS], F32), "loc": A("loc", [P, CHUNKS], F32),
         "srcix": A("srcix", [P, CHUNKS], I32), "sdedge": A("sdedge", [P, 2, GROUPS], F32),
         "lastix": A("lastix", [P, BLOCKS], I32), "nodeix": nodeix,
         "far": A("far", [1, CHUNKS], I32), "anyfar": A("anyfar", [1, GROUPS], I32)}
    c.fence()
    src, dst = (a[n].rearrange("(c e) -> c e", e=P) for n in ("src", "dst"))
    mark = nc.sbuf_base
    nodes_stage(c, a["x"], frag, table, xn_d, xnt_d, a["L0_gnn_W"], a["L0_gnn_a_src"], a["L0_gnn_a_dst"], gram)
    c.fence()
    nc.sbuf_base = mark
    mix_weights_stage(c, gram, a["L0_mix_w_qkv"], a["L0_mix_b_qkv"], wqa, bqa)
    index_stage(c, dst, src, table, rows_d, sdst_d, g)
    c.fence()
    nc.sbuf_base = mark
    edges = edges_stage(c, dst, src, table, frag, g)
    mlp = mlp_stage(c, a["x"], xn_d, xnt_d, xm_d, wqa, bqa, *(a[f"L0_mix_{n}"] for n in (
        "w_fc1", "b_fc1", "w_fc2", "b_fc2", "norm_g", "norm_b")))
    for _ in edges:
        next(mlp, None)
    for _ in mlp:
        pass
    c.fence()
    nc.sbuf_base = mark
    merge_stage(c, frag, g)
    c.fence()
    nc.sbuf_base = keep
    ffn = {n: a[f"L0_ffn_{n}"] for n in ("gate_w", "gate_b", "W1", "b1", "W2", "b2")}
    x1 = A("x1", [P, TILES, D], F32)
    w1 = A("e_w1", [P, EXPERTS * KD, HID], F32)
    w2 = A("e_w2", [P, EXPERTS * HT, D], F32)
    r = {"row": A("r_row", [P, 2, TILES], I32), "rev": A("r_rev", [P, 2, TILES], F32),
         "weight": A("r_weight", [P, 2, TILES], F32), "result": A("r_result", [P, 2, TILES], I32),
         "count": A("r_count", [P, EXPERTS], F32), "expert": A("r_expert", [1, SLOTS], I32),
         "tile_row": A("r_tile_row", [1, SLOTS], I32)}
    s_w = c.slot("expert_w")
    s_w.dma(c.sp, lambda e: e.dma_start(w1[:, :, :], ffn["W1"].rearrange("e (k p) n -> p (e k) n", p=P)))
    weights = s_w.dma(c.sp, lambda e: e.dma_start(w2[:, :, :], ffn["W2"].rearrange("e (k p) n -> p (e k) n", p=P)))
    mark = nc.sbuf_base
    route_stage(c, xm_d, frag, g, sorted_d, x1, ffn["gate_w"], ffn["gate_b"], r)
    c.fence()
    nc.sbuf_base = mark
    plan_stage(c, r, sorted_d)
    c.fence()
    nc.sbuf_base = mark
    experts_stage(c, r, sorted_d, result_d, w1, w2, ffn["b1"], ffn["b2"], weights)
    c.fence()
    nc.sbuf_base = mark
    combine_stage(c, r, result_d, x1, out)
    c.fence()


_INS = ["x", "src", "dst", "L0_gnn_W", "L0_gnn_a_src", "L0_gnn_a_dst", "L0_mix_w_qkv", "L0_mix_b_qkv",
        "L0_mix_norm_g", "L0_mix_norm_b", "L0_mix_w_fc1", "L0_mix_b_fc1", "L0_mix_w_fc2", "L0_mix_b_fc2",
        "L0_ffn_gate_w", "L0_ffn_gate_b", "L0_ffn_W1", "L0_ffn_b1", "L0_ffn_W2", "L0_ffn_b2"]


def kernel(**inputs):
    import concourse.bacc as _bacc
    from concourse.bass_utils import run_bass_kernel_spmd as _run

    nc = _bacc.Bacc("TRN2", target_bir_lowering=False, num_devices=1)
    arrays, aps = {}, {}
    pads = {"x": (N_PAD - N_NODES, 0), "src": (CHUNKS * P - N_EDGES, N_NODES), "dst": (CHUNKS * P - N_EDGES, N_NODES)}
    for name in _INS:
        v = np.ascontiguousarray(inputs[name])
        if name in pads:
            more, fill = pads[name]
            v = np.concatenate([v, np.full((more,) + v.shape[1:], fill, v.dtype)])
        arrays[f"in_{name}"] = v
        aps[name] = nc.dram_tensor(f"in_{name}", v.shape, mybir.dt.from_np(v.dtype), kind="ExternalInput").ap()
    out = nc.dram_tensor("out_0", (N_NODES, D), F32, kind="ExternalOutput").ap()
    with nc.allow_non_contiguous_dma(reason="small strided loads, once"):
        build(nc, aps, out)
    r = _run(nc, [arrays], core_ids=[0])
    return r.results[0]["out_0"]
```

```python
import numpy as np

import concourse.bass as bass
from concourse import mybir

F32 = mybir.dt.float32
I32 = mybir.dt.int32
ALU = mybir.AluOpType
ACT = mybir.ActivationFunctionType
AX = mybir.AxisListType.X

P = 128
BIG = 1.0e30
LN_EPS = 1e-5
SEG_EPS = 1e-8
SLOPE = 0.2

N_NODES = 12500
N_EDGES = 212500
D = 256
KD = D // P
TILES = -(-N_NODES // P)
N_PAD = TILES * P
ST = 4
SUPERS = [(s, min(ST, TILES - s)) for s in range(0, TILES, ST)]
GH, GF = 8, 32
ROW = D + 2 * GH
CB = 16
GROUPS = -(-N_EDGES // (P * CB))
BLOCKS = -(-GROUPS * CB // P)
CHUNKS = BLOCKS * P
NEAR = 32
FAR = CHUNKS * NEAR
FRAGS = FAR + N_NODES + 1 + P
NOT_WIDE = FRAGS - (P - NEAR)
MIX_HEADS, MIX_HD = 4, 64
MLP = 768
MT = MLP // P
MLP_STEPS = 15 * len(SUPERS) + 30
EXPERTS, HID = 8, 512
HT = HID // P
SENT = D + 4
SUB = 2
ET = SUB * P
HALF = -(-len(SUPERS) // 2) + 1
PARTS = []
for _lo, _hi in ((0, HALF), (HALF, len(SUPERS))):
    _tokens = P * sum(n for _, n in SUPERS[_lo:_hi])
    _base = PARTS[-1]["end"] if PARTS else 0
    PARTS.append({"supers": range(_lo, _hi), "region": _tokens + ET, "base": _base, "zeros": _base + EXPERTS * (_tokens + ET),
                  "end": _base + EXPERTS * (_tokens + ET) + ET, "slots": (2 * _tokens + EXPERTS * (ET - 1)) // ET})
NOUT = 3
ROUTE_STEPS = 3
SLOTS = sum(p["slots"] for p in PARTS)


class Lane:

    def __init__(self, nc, engine, name):
        self.engine, self.sem, self.count, self.seen = engine, nc.alloc_semaphore(name), 0, {}

    def wait(self, *tokens):
        for t in tokens:
            if t is None:
                continue
            if isinstance(t, list):
                self.wait(*t)
                continue
            sem, value, key = t
            if self.seen.get(key, 0) < value:
                self.engine.wait_ge(sem, value)
                self.seen[key] = value

    def run(self, issue, *tokens):
        self.wait(*tokens)
        issue(self.engine).then_inc(self.sem, 1)
        self.count += 1
        return (self.sem, self.count, id(self))

    def last(self):
        return (self.sem, self.count, id(self)) if self.count else None


class Slot:

    def __init__(self, nc, name):
        self.sem, self.count = nc.alloc_semaphore(name), 0

    def dma(self, lane, issue, *tokens):
        lane.wait(*tokens)
        issue(lane.engine).then_inc(self.sem, 16)
        self.count += 16
        return (self.sem, self.count, id(self))

    def last(self):
        return (self.sem, self.count, id(self)) if self.count else None


class Core:
    def __init__(self, nc):
        self.nc = nc
        self.pe = Lane(nc, nc.tensor, "pe_done")
        self.dve = Lane(nc, nc.vector, "dve_done")
        self.act = Lane(nc, nc.scalar, "act_done")
        self.pool = Lane(nc, nc.gpsimd, "pool_done")
        self.sp = Lane(nc, nc.sync, "sp_done")
        self.slots = []
        self.banks = [nc.alloc_psum_tensor(f"bank{i}", [P, 512], F32) for i in range(8)]

    def slot(self, name):
        self.slots.append(Slot(self.nc, name))
        return self.slots[-1]

    def fence(self, but=()):
        done = [l.last() for l in (self.pe, self.dve, self.act, self.pool)]
        done += [s.last() for s in self.slots if s not in but]
        for lane in (self.pe, self.dve, self.act, self.pool, self.sp):
            lane.wait(*done)


def finish(steps):
    while True:
        try:
            next(steps)
        except StopIteration as end:
            return end.value


def every(some, steps):
    n = 0
    while True:
        try:
            next(steps)
        except StopIteration as end:
            return end.value
        n += 1
        if n % some == 0:
            yield


def alternate(steps, between, every):
    n = 0
    while True:
        try:
            next(steps)
        except StopIteration as end:
            return end.value
        n += 1
        if n % every == 0:
            next(between, None)


def rsqrt_steps(c, var, out, tmp, ready):
    v = c.dve
    t = v.run(lambda e: e.tensor_single_scalar(tmp.bitcast(I32), var.bitcast(I32), 1, ALU.logical_shift_right), ready)
    yield
    t = v.run(lambda e: e.tensor_scalar(out.bitcast(I32), tmp.bitcast(I32), -1.0, float(0x5F3759DF), ALU.mult, ALU.add), t)
    yield
    for _ in range(3):
        t = v.run(lambda e: e.tensor_tensor(tmp, out, out, ALU.mult), t)
        yield
        t = v.run(lambda e: e.tensor_tensor(tmp, tmp, var, ALU.mult), t)
        yield
        t = v.run(lambda e: e.tensor_scalar(tmp, tmp, -0.5, 1.5, ALU.mult, ALU.add), t)
        yield
        t = v.run(lambda e: e.tensor_tensor(out, out, tmp, ALU.mult), t)
        yield
    return t


def layernorm_steps(c, x, out, stats, n, ready, free):
    v = c.dve
    v.wait(*ready)
    t = None
    for i in range(n):
        t = v.run(lambda e, i=i: e.bn_stats(stats[:, i, 0:6], x[:, i, :]))
    yield
    for i in range(n):
        t = v.run(lambda e, i=i: e.bn_aggr(stats[:, i, 6:8], stats[:, i, 0:6]), t)
    yield
    var = stats[:, 0:n, 8]
    t = v.run(lambda e: e.tensor_scalar(var, stats[:, 0:n, 7], LN_EPS, None, ALU.add), t)
    yield
    t = yield from rsqrt_steps(c, var, stats[:, 0:n, 9], stats[:, 0:n, 10], t)
    v.wait(*free)
    for i in range(n):
        t = v.run(lambda e, i=i: e.tensor_scalar(out[:, i, 0:D], x[:, i, :], stats[:, i, 6:7], stats[:, i, 9:10],
                                                 ALU.subtract, ALU.mult), t)
    return t


def layernorm(*args):
    return finish(layernorm_steps(*args))


def turn(c, src, dst, n, banks, ready, bank_free, dst_free):
    outs = []
    for k in range(KD):
        c.pe.wait(ready, bank_free[k])
        for i in range(n):
            t = c.pe.run(lambda e, i=i: e.transpose(banks[k][:, i * P:(i + 1) * P], src[:, i, k * P:(k + 1) * P],
                                                    c.ident[:, :]))
        o = c.act.run(lambda e: e.activation(dst[:, k, 0:n * P], banks[k][:, 0:n * P], ACT.Copy), t, dst_free)
        bank_free[k] = o
        outs.append(o)
    return outs


def constants(c):
    nc = c.nc
    c.ident = nc.alloc_sbuf_tensor("ident", [P, P], F32)
    c.ramp = nc.alloc_sbuf_tensor("ramp", [P, P], F32)
    c.ones = nc.alloc_sbuf_tensor("ones", [P, P], F32)
    c.headsel = nc.alloc_sbuf_tensor("headsel", [GH, D], F32)
    p = c.pool
    t = p.run(lambda e: e.memset(c.ident[:, :], 0.0))
    t = p.run(lambda e: e.affine_select(out=c.ident[:, :], in_=c.ident[:, :], compare_op=ALU.not_equal, fill=1.0,
                                        base=0, pattern=[[-1, P]], channel_multiplier=1), t)
    p.run(lambda e: e.iota(c.ramp[:, :], pattern=[[1, P]], base=0, channel_multiplier=0,
                           allow_small_or_imprecise_dtypes=True))
    p.run(lambda e: e.memset(c.ones[:, :], 1.0))
    t = p.run(lambda e: e.memset(c.headsel[:, :], 0.0))
    v = c.headsel[:, :].rearrange("p (h f) -> p h f", f=GF)
    p.run(lambda e: e.affine_select(out=v, in_=v, compare_op=ALU.not_equal, fill=1.0, base=0,
                                    pattern=[[-1, GH], [0, GF]], channel_multiplier=1), t)


def nodes_stage(c, x, frag, table, xnt_d, gnn_w, a_src, a_dst, gram, between):
    nc = c.nc
    A = nc.alloc_sbuf_tensor
    wcat = A("wcat", [P, KD, ROW], F32)
    avec = A("avec", [P, 2, D], F32)
    wtmp = A("wtmp", [P, D], F32)
    xs = [A(f"xs{b}", [P, ST, D], F32) for b in range(2)]
    xn = [A(f"xn{b}", [P, ST, D + 1], F32) for b in range(2)]
    xt = [A(f"xt{b}", [P, KD, ST * P], F32) for b in range(2)]
    hr = [A(f"hr{b}", [P, ST, ROW], F32) for b in range(2)]
    st = A("st_a", [P, ST, 16], F32)
    s_w, s_x = c.slot("a_w"), [c.slot(f"a_x{b}") for b in range(2)]
    s_xt, s_h = ([c.slot(f"a_{n}{b}") for b in range(2)] for n in ("xt", "h"))

    for k in range(KD):
        w = s_w.dma(c.sp, lambda e: e.dma_start(wcat[:, k, 0:D].rearrange("p (h f) -> p h f", f=GF),
                                                gnn_w[:, k * P:(k + 1) * P, :].rearrange("h i f -> i h f")))
    for j, a in enumerate((a_src, a_dst)):
        w = s_w.dma(c.sp, lambda e: e.dma_start(avec[:, j, :], a.rearrange("h f -> (h f)").partition_broadcast(P)))
    t = w
    for k in range(KD):
        for j in range(2):
            t = c.dve.run(lambda e: e.tensor_tensor(wtmp[:, :], wcat[:, k, 0:D], avec[:, j, :], ALU.mult), t)
            t = c.dve.run(lambda e: e.tensor_reduce(wcat[:, k, D + GH * j:D + GH * (j + 1)],
                                                    wtmp[:, :].rearrange("p (h f) -> p h f", f=GF), AX, ALU.add), t)
    scores_ready = t
    for b in range(2):
        c.dve.run(lambda e: e.memset(xn[b][:, :, D:D + 1], 1.0))
    zero = A("zero", [P, ROW], F32)
    zeroed = c.dve.run(lambda e: e.memset(zero[:, :], 0.0))
    s_z = c.slot("a_zero")
    empty = [(r, min(P, FRAGS - r)) for r in range(FAR, FRAGS, P)]
    share = -(-len(empty) // len(SUPERS))

    load, xs_free = [None, None], [None, None]
    tp_free, h_free = [None, None], [None, None]
    xn_used, xt_used, h_out = [None, None], [None, None], [None, None]
    gram_banks = (c.banks[4], c.banks[5])
    g_done = None

    def fetch(k):
        s, n = SUPERS[k]
        b = k % 2
        load[b] = s_x[b].dma(c.sp, lambda e: e.dma_start(
            xs[b][:, 0:n, :], x[s * P:(s + n) * P, :].rearrange("(t p) d -> p t d", p=P)), xs_free[b])

    fetch(0)
    hcount = 0
    for k, (s, n) in enumerate(SUPERS):
        b = k % 2
        if k + 1 < len(SUPERS):
            fetch(k + 1)
        normed = alternate(layernorm_steps(c, xs[b], xn[b], st, n, [load[b]], [xn_used[b]]), between, 2)
        xs_free[b] = normed
        turned = turn(c, xn[b], xt[b], n, c.banks[0:2], normed, tp_free, [xt_used[b], s_xt[b].last()])
        s_xt[b].dma(c.sp, lambda e: e.dma_start(
            xnt_d.rearrange("(k p) n -> p k n", p=P)[:, :, s * P:(s + n) * P], xt[b][:, :, 0:n * P]), turned)
        for i in range(n):
            hb = hcount % 2
            bank = c.banks[2 + hb]
            c.pe.wait(turned, scores_ready, h_free[hb])
            for kk in range(KD):
                t = c.pe.run(lambda e: e.matmul(bank[:, 0:ROW], xt[b][:, kk, i * P:(i + 1) * P], wcat[:, kk, :],
                                                start=(kk == 0), stop=(kk == KD - 1)))
            h_free[hb] = c.act.run(lambda e: e.activation(hr[b][:, i, :], bank[:, 0:ROW], ACT.Copy), t, s_h[b].last())
            hcount += 1
        xt_used[b] = t
        s_h[b].dma(c.sp, lambda e: e.dma_start(
            table[s * P:(s + n) * P, :].rearrange("(t p) d -> p t d", p=P), hr[b][:, 0:n, :]), h_free[hb])
        for i in range(n):
            for m in range(KD):
                g_done = c.pe.run(lambda e: e.matmul(
                    gram_banks[m][:, m * P:D + 1], xn[b][:, i, m * P:(m + 1) * P], xn[b][:, i, m * P:],
                    start=(s + i == 0), stop=(s + i == TILES - 1)))
        xn_used[b] = g_done
        for r, m in empty[k * share:(k + 1) * share]:
            s_z.dma(c.act, lambda e: e.dma_start(frag[r:r + m, :], zero[0:m, :]), zeroed)
    for _ in between:
        pass
    for m in range(KD):
        t = c.dve.run(lambda e: e.tensor_copy(gram[:, m, m * P:], gram_banks[m][:, m * P:D + 1]), g_done)
    t = c.pe.run(lambda e: e.transpose(gram_banks[0][:, 0:P], gram[:, 0, P:D], c.ident[:, :]), t)
    c.dve.run(lambda e: e.tensor_copy(gram[:, 1, 0:P], gram_banks[0][:, 0:P]), t)


def mix_weights_stage(c, gram, wqkv, bqkv, wqa, bqa):
    nc = c.nc
    A = nc.alloc_sbuf_tensor
    w = A("wqkv_s", [P, KD, 3 * D], F32)
    brow = A("bqkv_row", [1, 3 * D], F32)
    bqc = A("bq_col", [P, KD], F32)
    u = A("mix_u", [P, KD, D], F32)
    srow = A("mix_srow", [1, D], F32)
    rrow = A("mix_rrow", [1, D], F32)
    att = A("mix_att", [P, KD, P], F32)
    attt = A("mix_attt", [P, KD, P], F32)
    wqt = A("mix_wqt", [P, KD, D], F32)
    red = A("mix_red", [P, 8], F32)
    s = c.slot("mix_in")
    s.dma(c.sp, lambda e: e.dma_start(w[:, :, :], wqkv.rearrange("(k p) n -> p k n", p=P)))
    s.dma(c.sp, lambda e: e.dma_start(brow[:, :], bqkv.unsqueeze(0)))
    ready = s.dma(c.sp, lambda e: e.dma_start(bqc[:, :], bqkv[0:D].rearrange("(k p) -> p k", p=P)))
    pe, v, bk = c.pe, c.dve, c.banks
    pe.wait(ready)
    for m in range(KD):
        t = pe.run(lambda e: e.transpose(bk[0][0:1, m * P:(m + 1) * P], gram[:, m, D:D + 1], c.ident[:, :]))
    t = v.run(lambda e: e.tensor_copy(srow[:, :], bk[0][0:1, 0:D]), t)
    for m in range(KD):
        pe.wait(t)
        for k in range(KD):
            pe.run(lambda e: e.matmul(bk[1 + m][:, 0:D], gram[:, k, m * P:(m + 1) * P], w[:, k, 2 * D:3 * D],
                                      start=(k == 0), stop=False))
        q = pe.run(lambda e: e.matmul(bk[1 + m][:, 0:D], srow[0:1, m * P:(m + 1) * P], brow[0:1, 2 * D:3 * D],
                                      start=False, stop=True))
        v.run(lambda e: e.tensor_copy(u[:, m, :], bk[1 + m][:, 0:D]), q)
    for k in range(KD):
        q = pe.run(lambda e: e.matmul(bk[3][0:1, 0:D], gram[:, k, D:D + 1], w[:, k, 2 * D:3 * D],
                                      start=(k == 0), stop=(k == KD - 1)))
    t = v.run(lambda e: e.scalar_tensor_tensor(out=rrow[:, :], in0=brow[0:1, 2 * D:3 * D], scalar=float(N_NODES),
                                               in1=bk[3][0:1, 0:D], op0=ALU.mult, op1=ALU.add), q)
    t0 = v.run(lambda e: e.memset(att[:, :, :], 0.0))
    for m in range(KD):
        pe.wait(t)
        for k in range(KD):
            pe.run(lambda e: e.matmul(bk[4 + m][:, 0:D], w[:, k, D + m * P:D + (m + 1) * P], u[:, k, :],
                                      start=(k == 0), stop=False))
        q = pe.run(lambda e: e.matmul(bk[4 + m][:, 0:D], brow[0:1, D + m * P:D + (m + 1) * P], rrow[:, :],
                                      start=False, stop=True))
        scale = float(MIX_HD) ** -0.5
        for hh in range(2):
            r = slice(hh * MIX_HD, (hh + 1) * MIX_HD)
            col = (2 * m + hh) * MIX_HD
            sc = bk[4 + m][r, col:col + MIX_HD]
            o = att[r, m, hh * MIX_HD:(hh + 1) * MIX_HD]
            x = v.run(lambda e: e.tensor_reduce(red[r, 0:1], sc, AX, ALU.max), q, t0)
            x = v.run(lambda e: e.tensor_scalar(red[r, 1:2], red[r, 0:1], -scale, None, ALU.mult), x)
            x = c.act.run(lambda e: e.activation(o, sc, ACT.Exp, bias=red[r, 1:2], scale=scale), x)
            x = v.run(lambda e: e.tensor_reduce(red[r, 2:3], o, AX, ALU.add), x)
            x = v.run(lambda e: e.reciprocal(red[r, 3:4], red[r, 2:3]), x)
            x = v.run(lambda e: e.tensor_scalar(o, o, red[r, 3:4], None, ALU.mult), x)
    for m in range(KD):
        q = pe.run(lambda e: e.transpose(bk[6][:, m * P:(m + 1) * P], att[:, m, :], c.ident[:, :]), x)
    x = v.run(lambda e: e.tensor_copy(attt[:, :, :], bk[6][:, 0:D].rearrange("p (m e) -> p m e", m=KD)), q)
    for m in range(KD):
        for i in range(KD):
            q = pe.run(lambda e: e.transpose(bk[7][:, m * D + i * P:m * D + (i + 1) * P], w[:, i, m * P:(m + 1) * P],
                                             c.ident[:, :]))
    x = v.run(lambda e: e.tensor_copy(wqt[:, :, :], bk[7][:, :].rearrange("p (m i) -> p m i", m=KD)), q)
    pe.wait(x)
    for i in range(KD):
        for m in range(KD):
            q = pe.run(lambda e: e.matmul(bk[i][:, m * P:(m + 1) * P], wqt[:, m, i * P:(i + 1) * P], attt[:, m, :],
                                          start=True, stop=True))
        x = v.run(lambda e: e.tensor_copy(wqa[:, i, :], bk[i][:, 0:D]), q)
        own = wqa[:, i, i * P:(i + 1) * P]
        v.run(lambda e: e.tensor_tensor(own, own, c.ident[:, :], ALU.add), x)
    for m in range(KD):
        q = pe.run(lambda e: e.matmul(bk[2][0:1, m * P:(m + 1) * P], bqc[:, m:m + 1], attt[:, m, :],
                                      start=True, stop=True))
    q = v.run(lambda e: e.tensor_copy(srow[:, :], bk[2][0:1, 0:D]), q)
    q = pe.run(lambda e: e.matmul(bk[3][:, 0:D], c.ones[0:1, :], srow[:, :], start=True, stop=True), q)
    v.run(lambda e: e.tensor_copy(bqa[:, :], bk[3][:, 0:D]), q)


def fragment_rows(c, q, node, out, n, ready):
    A = c.nc.alloc_sbuf_tensor
    qi, loc, ch, far, sel = (A(f"fr{n}_{i}", [P, n], dt) for i, dt in enumerate((I32, I32, I32, F32, F32)))
    v = c.dve
    t = v.run(lambda e: e.tensor_copy(qi[:, :], q[:, 0:n]), ready)
    t1 = v.run(lambda e: e.tensor_scalar(loc[:, :], qi[:, :], P - 1, None, ALU.bitwise_and), t)
    t = v.run(lambda e: e.tensor_scalar(ch[:, :], qi[:, :], 7, 5, ALU.logical_shift_right, ALU.logical_shift_left), t)
    t = v.run(lambda e: e.tensor_tensor(q[:, 0:n], ch[:, :], loc[:, :], ALU.add), t, t1)
    t2 = v.run(lambda e: e.tensor_scalar(sel[:, :], loc[:, :], float(NEAR), None, ALU.is_ge), t1)
    t = v.run(lambda e: e.scalar_tensor_tensor(out=far[:, :], in0=node, scalar=float(FAR), in1=q[:, 0:n], op0=ALU.add,
                                               op1=ALU.subtract), t)
    t = v.run(lambda e: e.tensor_tensor(far[:, :], far[:, :], sel[:, :], ALU.mult), t, t2)
    return v.run(lambda e: e.tensor_tensor(out[:, :], far[:, :], q[:, 0:n], ALU.add), t)


def index_buffers(nc):
    A = nc.alloc_sbuf_tensor
    return A("dfl_i", [P, 2, BLOCKS], I32)


def index_steps(c, dst, src, rows_d, keys_d, fli, g):
    nc = c.nc
    A = nc.alloc_sbuf_tensor
    di = A("dst_i", [P, BLOCKS, P], I32)
    si = A("src_i", [P, BLOCKS, P], I32)
    fl = A("dfl_f", [P, 2, BLOCKS], F32)
    tmp = [A(f"ix_tmp{b}", [P, P], F32) for b in range(2)]
    dkey = A("ix_key", [P, CHUNKS], F32)
    cnum = A("ix_cnum", [P, CHUNKS], F32)
    wide = A("ix_cmp", [P, CHUNKS], F32)
    nid = A("ix_nid", [P, TILES], F32)
    nf = A("ix_nf", [P, TILES], F32)
    below = A("ix_below", [P, TILES, BLOCKS], F32)
    blk = A("ix_blk", [P, TILES], F32)
    blki = A("ix_blki", [P, TILES], I32)
    NK = 8
    keys = [A(f"ix_keys{b}", [P, 2 * P], F32) for b in range(NK)]
    s_k = [c.slot(f"ix_k{b}") for b in range(NK)]
    cn = A("ix_cn", [P, BLOCKS], F32)
    s1, s2, s3 = (c.slot(f"ix_{i}") for i in range(3))
    v, pe, banks = c.dve, c.pe, c.banks[6:8]
    s1.dma(c.act, lambda e: e.dma_start(di[:, :, :], dst.rearrange("(b c) e -> c b e", c=P)))
    t = s1.dma(c.act, lambda e: e.dma_start(si[:, :, :], src.rearrange("(b c) e -> c b e", c=P)))
    for j, col in ((0, 0), (1, P - 1)):
        v.run(lambda e: e.tensor_copy(fl[:, j, :], di[:, :, col]), t)
        f = v.run(lambda e: e.tensor_copy(fli[:, j, :], di[:, :, col]), t)
    w = s2.dma(c.sp, lambda e: e.dma_start(rows_d.rearrange("j (b c) -> c j b", c=P), fl[:, :, :]), f)
    for j, to in ((0, g["dfb"]), (1, g["dlb"])):
        w2 = s3.dma(c.sp, lambda e: e.dma_start(to[:, :], rows_d[j].partition_broadcast(P)), w)
    yield
    free = [None, None]
    n = 0
    for b in range(BLOCKS):
        for what in range(2):
            u = n % 2
            if what == 0:
                t = v.run(lambda e: e.tensor_scalar(tmp[u][:, :], di[:, b, :], fl[:, 0, b:b + 1], None, ALU.subtract),
                          f, free[u])
            else:
                t = v.run(lambda e: e.tensor_copy(tmp[u][:, :], si[:, b, :]), free[u])
            t = pe.run(lambda e: e.transpose(banks[u][:, 0:P], tmp[u][:, :], c.ident[:, :]), t)
            to = (g["loc"], g["srcix"])[what]
            free[u] = c.act.run(lambda e: e.activation(to[:, b * P:(b + 1) * P], banks[u][:, 0:P], ACT.Copy), t)
            n += 1
        yield
    t = c.pool.run(lambda e: e.iota(cn[:, :], pattern=[[P * P, BLOCKS]], base=0, channel_multiplier=P,
                                    allow_small_or_imprecise_dtypes=True))
    t = v.run(lambda e: e.tensor_tensor(cn[:, :], cn[:, :], fl[:, 1, :], ALU.add), t)
    t = v.run(lambda e: e.tensor_tensor(cn[:, :], cn[:, :], fl[:, 0, :], ALU.subtract), t)
    fragment_rows(c, cn, fl[:, 1, :], g["lastix"], BLOCKS, t)
    yield
    t = c.pool.run(lambda e: e.iota(cnum[:, :], pattern=[[P, CHUNKS]], base=0, channel_multiplier=0,
                                    allow_small_or_imprecise_dtypes=True))
    t = v.run(lambda e: e.tensor_tensor(cnum[:, :], cnum[:, :], g["dfb"][:, :], ALU.subtract), t, w2)
    key = v.run(lambda e: e.tensor_tensor(dkey[0:1, 1:], cnum[0:1, 1:], cnum[0:1, 0:CHUNKS - 1], ALU.subtract), t)
    key = v.run(lambda e: e.tensor_copy(dkey[0:1, ::P], cnum[0:1, ::P]), key)
    s2.dma(c.sp, lambda e: e.dma_start(keys_d[:, 0:P].unsqueeze(0), g["dfb"][0:1, :].rearrange("p (b c) -> p b c", c=P)), w2)
    key = s2.dma(c.sp, lambda e: e.dma_start(keys_d[:, P:2 * P].unsqueeze(0), dkey[0:1, :].rearrange("p (b c) -> p b c", c=P)), key)
    nidr = c.pool.run(lambda e: e.iota(nid[:, :], pattern=[[P, TILES]], base=0, channel_multiplier=1,
                                       allow_small_or_imprecise_dtypes=True))
    yield
    shape = [P, TILES, BLOCKS]
    t = v.run(lambda e: e.tensor_tensor(below[:, :, :], nid[:, :].unsqueeze(2).to_broadcast(shape),
                                        g["dfb"][:, ::P].unsqueeze(1).to_broadcast(shape), ALU.is_ge), nidr)
    t = v.run(lambda e: e.tensor_reduce(blk[:, :], below[:, :, :], AX, ALU.add), t)
    blkr = v.run(lambda e: e.tensor_scalar(blki[:, :], blk[:, :], -1.0, None, ALU.add), t)
    here, used = [None] * NK, [None] * NK

    def fetch(i):
        here[i % NK] = s_k[i % NK].dma(c.pool, lambda e: e.indirect_dma_start(
            out=keys[i % NK][:, :], out_offset=None, in_=keys_d[:, :],
            in_offset=bass.IndirectOffsetOnAxis(ap=blki[:, i:i + 1], axis=0)), blkr, key, used[i % NK])

    for i in range(NK - 1):
        fetch(i)
    yield
    for i in range(TILES):
        b = i % NK
        if i + NK - 1 < TILES:
            fetch(i + NK - 1)
        t = used[b] = v.run(lambda e: e.scalar_tensor_tensor(
            out=wide[:, 0:P], in0=keys[b][:, 0:P], scalar=nid[:, i:i + 1], in1=keys[b][:, P:2 * P], op0=ALU.is_le,
            op1=ALU.mult, accum_out=nf[:, i:i + 1]), t, here[b])
        yield
    t = v.run(lambda e: e.tensor_tensor(nf[:, :], nf[:, :], nid[:, :], ALU.add), t)
    fragment_rows(c, nf, nid[:, :], g["nodeix"], TILES, t)
    t = v.run(lambda e: e.tensor_tensor(wide[0:1, :], g["dlb"][0:1, :], g["dfb"][0:1, :], ALU.subtract), t)
    t = v.run(lambda e: e.tensor_scalar(wide[0:1, :], wide[0:1, :], float(NEAR), float(FRAGS), ALU.is_lt, ALU.mult), t)
    t = v.run(lambda e: e.tensor_tensor(wide[0:1, :], wide[0:1, :], g["dfb"][0:1, :], ALU.add), t)
    v.run(lambda e: e.tensor_scalar(g["far"][0:1, :], wide[0:1, :], float(N_NODES + 1), float(FAR + NEAR), ALU.min,
                                    ALU.add), t)
    t = v.run(lambda e: e.tensor_reduce(cnum[0:1, 0:GROUPS], wide[0:1, :].rearrange("p (g c) -> p g c", c=CB), AX,
                                        ALU.min), t)
    v.run(lambda e: e.tensor_scalar(g["anyfar"][0:1, :], cnum[0:1, 0:GROUPS], float(N_NODES + 1), None, ALU.is_lt), t)


def edge_scores_stage(c, table, sdst_d, fli, g):
    nc = c.nc
    A = nc.alloc_sbuf_tensor
    ends = A("ix_rows", [P, 2 * BLOCKS, ROW], F32)
    sd = A("ix_sd", [P, 2, BLOCKS, GH], F32)
    sdg = A("ix_sdg", [GROUPS, 2, P], F32)
    s1, s2, s3 = (c.slot(f"es_{i}") for i in range(3))
    v, pe = c.dve, c.pe
    for j in range(2):
        for b in range(BLOCKS):
            t = s1.dma(c.pool, lambda e: e.indirect_dma_start(
                out=ends[:, j * BLOCKS + b, :], out_offset=None, in_=table[:, :],
                in_offset=bass.IndirectOffsetOnAxis(ap=fli[:, j, b:b + 1], axis=0)))
    yield
    t = v.run(lambda e: e.tensor_copy(sd[:, :, :, :], ends[:, :, D + GH:ROW].rearrange("p (j b) h -> p j b h", j=2)), t)
    for j in range(2):
        t2 = s2.dma(c.sp, lambda e: e.dma_start(sdst_d[j].rearrange("(b c) h -> c b h", c=P), sd[:, j, :, :]), t)
    t = s3.dma(c.sp, lambda e: e.dma_start(sdg[:, :, :], sdst_d.rearrange("j (g c) h -> g j (c h)", c=CB)), t2)
    for j in range(2):
        q = pe.run(lambda e: e.transpose(c.banks[6 + j][:, 0:GROUPS], sdg[:, j, :], c.ident[0:GROUPS, 0:GROUPS]), t)
        v.run(lambda e: e.tensor_copy(g["sdedge"][:, j, :], c.banks[6 + j][:, 0:GROUPS]), q)


def edges_stage(c, dst, src, table, frag, g):
    nc = c.nc
    A = nc.alloc_sbuf_tensor
    NB = 3
    rows = [A(f"rows{b}", [P, CB, ROW], F32) for b in range(NB)]
    onehot = [A(f"onehot{b}", [P, CB, P], F32) for b in range(2)]
    fout = [A(f"fout{b}", [P, CB, ROW], F32) for b in range(2)]
    dsr = [A(f"dsr{b}", [P, 2, P], I32) for b in range(NB)]
    sc_e = [A(f"sc_e{b}", [P, 2, P], F32) for b in range(2)]
    brk = A("brk", [P, P + 1], F32)
    neq = A("neq", [P, P + 1], F32)
    notself = A("notself", [P, P], F32)
    sdm, d1, d2, ea, fm = (A(f"g_{n}", [P, P], F32) for n in ("sdm", "d1", "d2", "ea", "fm"))
    mx1, mx = d1, d2
    wgt = A("g_w", [P, P], F32)
    we = [A(f"g_we{b}", [P, 2, P], F32) for b in range(2)]
    s_row = [c.slot(f"rows_in{b}") for b in range(NB)]
    s_ds = [c.slot(f"ds_in{b}") for b in range(NB)]
    s_near = [c.slot(f"near_out{b}") for b in range(2)]
    s_far = [c.slot(f"far_out{b}") for b in range(2)]
    v, pe, act, pool, sp = c.dve, c.pe, c.act, c.pool, c.sp
    in_bank, out_bank, o_banks = c.banks[0], c.banks[1], c.banks[2:5]
    ends = v.run(lambda e: e.memset(neq[:, :], 1.0))
    gathered, rows_free = [None] * NB, [[None] * CB for _ in range(NB)]
    ds_ready, ds_free = [None] * NB, [None] * NB
    scaled = in_free = out_free = turned = flags = weighed = fm_done = fm_free = None
    o_free, oh_free, sce_free, we_free = [None] * 3, [None] * 2, [None] * 2, [None] * 2
    oh, weights, tail = [None] * 2, [None] * 2, [None] * 2
    nmm = 0

    def gather(k):
        b = k % NB
        for j in range(CB):
            col = k * CB + j
            gathered[b] = s_row[b].dma(pool, lambda e: e.indirect_dma_start(
                out=rows[b][:, j, :], out_offset=None, in_=table[:, :],
                in_offset=bass.IndirectOffsetOnAxis(ap=g["srcix"][:, col:col + 1], axis=0)), rows_free[b][j])

    def edge_rows(k):
        b = k % NB
        for j, of in enumerate((dst, src)):
            rep = bass.AP(of.tensor, k * CB * P, [[P, CB], [0, GH], [1, P]])
            ds_ready[b] = s_ds[b].dma(sp, lambda e: e.dma_start(dsr[b][:, j, :], rep), ds_free[b])

    def back(a):
        return a[:, ::-1]

    def turn_scores(k):
        nonlocal turned
        r, b = k % NB, k % 2
        t = act.run(lambda e: e.activation(sc_e[b][:, :, :].rearrange("p j (c h) -> p j c h", h=GH),
                                           rows[r][:, :, D:ROW].rearrange("p c (j h) -> p j c h", h=GH), ACT.Copy),
                    gathered[r], sce_free[b])
        pe.wait(t, in_free)
        for j in range(2):
            turned = pe.run(lambda e: e.transpose(in_bank[:, j * P:(j + 1) * P], sc_e[b][:, j, :], c.ident[:, :]))
        sce_free[b] = turned

    def breaks(k):
        nonlocal flags, oh
        b = k % 2
        ds, d = dsr[k % NB], k % NB
        t = v.run(lambda e: e.tensor_tensor(neq[:, 1:P], ds[:, 0, 1:P], ds[:, 0, 0:P - 1], ALU.not_equal),
                  ds_ready[d], ends, fm_free)
        v.run(lambda e: e.tensor_scalar(brk[:, :], neq[:, :], -BIG, None, ALU.mult), t)
        ds_free[d] = flags = v.run(lambda e: e.tensor_tensor(notself[:, :], ds[:, 0, :], ds[:, 1, :], ALU.not_equal))
        oh[b] = v.run(lambda e: e.tensor_tensor(onehot[b][:, :, :], c.ramp[:, :].unsqueeze(1).to_broadcast([P, CB, P]),
                                                g["loc"][:, k * CB:(k + 1) * CB].unsqueeze(2).to_broadcast([P, CB, P]),
                                                ALU.is_equal), oh_free[b])

    def edge_scores(k):
        nonlocal in_free, weighed, fm_done
        t = v.run(lambda e: e.scalar_tensor_tensor(out=sdm[:, :], in0=notself[:, :], scalar=-BIG,
                                                   in1=in_bank[:, P:2 * P], op0=ALU.mult, op1=ALU.add), flags, turned)
        v.run(lambda e: e.tensor_copy(sdm[:, 0:1], g["sdedge"][:, 0, k:k + 1]), t)
        t = v.run(lambda e: e.tensor_copy(sdm[:, P - 1:P], g["sdedge"][:, 1, k:k + 1]), t)
        t = v.run(lambda e: e.tensor_tensor_scan(out=d1[:, :], data0=brk[:, 0:P], data1=sdm[:, :], initial=-BIG,
                                                 op0=ALU.add, op1=ALU.max), t)
        t = v.run(lambda e: e.tensor_tensor_scan(out=back(d2), data0=back(brk[:, 1:P + 1]), data1=back(d1),
                                                 initial=-BIG, op0=ALU.add, op1=ALU.max), t)
        t = v.run(lambda e: e.tensor_tensor(ea[:, :], d2[:, :], in_bank[:, 0:P], ALU.add), t, weighed)
        in_free = t
        t = v.run(lambda e: e.scalar_tensor_tensor(out=ea[:, :], in0=ea[:, :], scalar=SLOPE, in1=ea[:, :],
                                                   op0=ALU.mult, op1=ALU.max), t)
        t = v.run(lambda e: e.tensor_tensor_scan(out=mx1[:, :], data0=brk[:, 0:P], data1=ea[:, :], initial=-BIG,
                                                 op0=ALU.add, op1=ALU.max), t)
        t = v.run(lambda e: e.tensor_tensor_scan(out=back(mx), data0=back(brk[:, 1:P + 1]), data1=back(mx1),
                                                 initial=-BIG, op0=ALU.add, op1=ALU.max), t)
        t1 = v.run(lambda e: e.tensor_tensor(ea[:, :], ea[:, :], mx[:, :], ALU.subtract), t)
        fm_done = v.run(lambda e: e.tensor_tensor(fm[:, :], mx[:, :], neq[:, 0:P], ALU.mult), t, fm_free)
        weighed = act.run(lambda e: e.activation(wgt[:, :], ea[:, :], ACT.Exp), t1, fm_free)

    def turn_weights(k):
        nonlocal fm_free, out_free
        r, b = k % NB, k % 2
        pe.wait(weighed, fm_done, out_free)
        for j, a in enumerate((wgt, fm)):
            fm_free = pe.run(lambda e: e.transpose(out_bank[:, j * P:(j + 1) * P], a[:, :], c.ident[:, :]))
        out_free = weights[b] = act.run(lambda e: e.activation(
            we[b][:, :, :], out_bank[:, 0:2 * P].rearrange("p (j x) -> p j x", j=2), ACT.Copy), fm_free, we_free[b])
        tail[b] = act.run(lambda e: e.activation(rows[r][:, :, D:ROW].rearrange("p c (j h) -> p j c h", h=GH),
                                                 we[b][:, :, :].rearrange("p j (c h) -> p j c h", h=GH), ACT.Copy),
                          weights[b])

    def weigh(k, q):
        nonlocal scaled
        r, b = k % NB, k % 2
        n = CB // 4
        q *= n
        hv = rows[r][:, q:q + n, 0:D].rearrange("p c (h f) -> p c h f", f=GF)
        wv = we[b][:, 0, q * GH:(q + n) * GH].rearrange("p (c h) -> p c h", h=GH)
        scaled = v.run(lambda e: e.tensor_tensor(hv, hv, wv.unsqueeze(3).to_broadcast([P, n, GH, GF]), ALU.mult),
                       weights[b])

    def sums(k, q):
        nonlocal nmm
        r, b = k % NB, k % 2
        R, n = rows[r], CB // 4
        q *= n
        t = scaled
        pe.wait(t, tail[b], oh[b])
        for j in range(q, q + n):
            ob = nmm % 3
            rows_free[r][j] = pe.run(lambda e: e.matmul(o_banks[ob][:, 0:ROW], onehot[b][:, j, :], R[:, j, :],
                                                        start=True, stop=True), o_free[ob])
            o_free[ob] = act.run(lambda e: e.activation(fout[b][:, j, :], o_banks[ob][:, 0:ROW], ACT.Copy),
                                 rows_free[r][j], s_near[b].last(), s_far[b].last())
            nmm += 1
        we_free[b] = [t, tail[b]]
        oh_free[b] = rows_free[r][j]

    def store(k):
        b = k % 2
        ready = act.last()
        near = frag[k * CB * NEAR:(k + 1) * CB * NEAR, :].rearrange("(c l) f -> l c f", l=NEAR)
        s_near[b].dma(act, lambda e: e.dma_start(near, fout[b][0:NEAR, :, :]), ready)
        eng, far = sp.engine, s_far[b]
        is_wide = eng.value_load(g["anyfar"][0:1, k:k + 1], min_val=0, max_val=1)
        with eng.If(is_wide > 0):
            eng.wait_ge(ready[0], ready[1])
            for j in range(CB):
                at = eng.value_load(g["far"][0:1, k * CB + j:k * CB + j + 1], min_val=FAR + NEAR, max_val=NOT_WIDE)
                eng.dma_start(frag[bass.ds(at, P - NEAR), :], fout[b][NEAR:P, j, :], cond=at < NOT_WIDE,
                              bounds_check="skip_entire_dma").then_inc(far.sem, 16)
                eng.wait_ge(far.sem, far.count + 16 * (j + 1))
        with eng.Else():
            eng.sem_inc(far.sem, 16 * CB)
        far.count += 16 * CB

    yield
    for k in range(NB):
        gather(k)
        edge_rows(k)
    yield
    turn_scores(0)
    breaks(0)
    edge_scores(0)
    turn_weights(0)
    weigh(0, 0)
    for k in range(GROUPS):
        more = k + 1 < GROUPS
        if NB <= k + 2 < GROUPS:
            gather(k + 2)
            edge_rows(k + 2)
        sums(k, 0)
        if more:
            turn_scores(k + 1)
        weigh(k, 1)
        if more:
            breaks(k + 1)
        yield
        sums(k, 1)
        weigh(k, 2)
        if more:
            edge_scores(k + 1)
        yield
        sums(k, 2)
        weigh(k, 3)
        yield
        if more:
            turn_weights(k + 1)
        sums(k, 3)
        if more:
            weigh(k + 1, 0)
        store(k)
        yield


def merge_stage(c, frag, g):
    nc = c.nc
    A = nc.alloc_sbuf_tensor
    B4 = 4
    windows = [(b, min(B4, BLOCKS - b)) for b in range(0, BLOCKS, B4)]
    first = A("mg_first", [P, BLOCKS, ROW], F32)
    last = A("mg_last", [P, BLOCKS, ROW], F32)
    wide = [A(f"mg_wide{h}", [P, B4 * P], F32) for h in range(KD)]
    part = [A(f"mg_part{u}", [P, B4, P], F32) for u in range(2)]
    cont, alone, mL, alpha, Cm = (A(f"mg_{n}", [GH, CHUNKS], F32) for n in ("cont", "alone", "mL", "alpha", "Cm"))
    gp = A("mg_gp", [GH, CHUNKS + 1], F32)
    run = [A(f"mg_run{h}", [P, CHUNKS + 1], F32) for h in range(KD)] + [A("mg_runs", [GH, CHUNKS + 1], F32)]
    G, C, top, beta, gamma, delta = (A(f"mg_c{n}", [P, BLOCKS, GH], F32) for n in ("G", "C", "top", "beta", "gamma", "delta"))
    s_f, s_l, s_o = c.slot("mg_f"), c.slot("mg_l"), c.slot("mg_o")
    v, pe, act = c.dve, c.pe, c.act
    fl = s_f.dma(c.sp, lambda e: e.dma_start(first[:, :, :], frag[0:FAR].rearrange("(b c l) f -> l c b f", c=P, l=NEAR)[0]))
    for b in range(BLOCKS):
        ll = s_l.dma(c.pool, lambda e: e.indirect_dma_start(
            out=last[:, b, :], out_offset=None, in_=frag[:, :],
            in_offset=bass.IndirectOffsetOnAxis(ap=g["lastix"][:, b:b + 1], axis=0)))
    tt = lambda o, a, b, op, *w: v.run(lambda e: e.tensor_tensor(o, a, b, op), *w)
    ts = lambda o, a, s1, s2, o1, o2, *w: v.run(lambda e: e.tensor_scalar(o, a, s1, s2, o1, o2), *w)
    df, dl = g["dfb"][0:GH, :], g["dlb"][0:GH, :]
    t = v.run(lambda e: e.memset(cont[:, 0:1], 0.0))
    t = tt(cont[:, 1:], df[:, 1:], dl[:, 0:CHUNKS - 1], ALU.is_equal, t)
    t = tt(alone[:, :], df, dl, ALU.is_equal, t)
    t = tt(alone[:, :], alone[:, :], cont[:, :], ALU.mult, t)
    t = ts(alone[:, :], alone[:, :], BIG, -BIG, ALU.mult, ALU.add, t)
    t = ts(cont[:, :], cont[:, :], BIG, -BIG, ALU.mult, ALU.add, t)
    for r in run:
        v.run(lambda e: e.memset(r[:, 0:1], 0.0))
    flags = v.run(lambda e: e.memset(gp[:, 0:1], -BIG), t)
    bank_free = [None] * 8
    n = 0

    def bank():
        nonlocal n
        n += 1
        return (n - 1) % 8

    for b0, m in windows:
        q = bank()
        for b in range(m):
            t = pe.run(lambda e: e.transpose(c.banks[q][0:GH, b * P:(b + 1) * P], last[:, b0 + b, D + GH:ROW], c.ident[:, :]),
                       ll, bank_free[q])
        rows_in = bank_free[q] = v.run(lambda e: e.tensor_copy(mL[:, b0 * P:(b0 + m) * P], c.banks[q][0:GH, 0:m * P]), t)
    t = v.run(lambda e: e.tensor_tensor_scan(out=gp[:, 1:], data0=alone[:, :], data1=mL[:, :], initial=-BIG,
                                             op0=ALU.add, op1=ALU.max), rows_in, flags)
    x = tt(Cm[:, :], gp[:, 0:CHUNKS], cont[:, :], ALU.add, t)
    t1 = tt(alpha[:, :], gp[:, 0:CHUNKS], gp[:, 1:], ALU.subtract, t)
    t1 = tt(alpha[:, :], alpha[:, :], alone[:, :], ALU.add, t1)
    rescale = act.run(lambda e: e.activation(alpha[:, :], alpha[:, :], ACT.Exp), t1)
    for of, to, ready in ((gp[:, 1:], G, t), (Cm[:, :], C, x)):
        q = bank()
        for b in range(BLOCKS):
            y = pe.run(lambda e: e.transpose(c.banks[q][:, b * GH:(b + 1) * GH], of[:, b * P:(b + 1) * P], c.ident[0:GH, 0:GH]),
                       ready, bank_free[q])
        bank_free[q] = v.run(lambda e: e.tensor_copy(to[:, :, :].rearrange("p b h -> p (b h)"), c.banks[q][:, 0:BLOCKS * GH]), y)
    t = bank_free[q]
    y = tt(beta[:, :, :], last[:, :, D + GH:ROW], G[:, :, :], ALU.subtract, t)
    weigh_last = act.run(lambda e: e.activation(beta[:, :, :], beta[:, :, :], ACT.Exp), y)
    t = tt(top[:, :, :], C[:, :, :], first[:, :, D + GH:ROW], ALU.max, t, fl)
    x = tt(gamma[:, :, :], C[:, :, :], top[:, :, :], ALU.subtract, t)
    act.run(lambda e: e.activation(gamma[:, :, :], gamma[:, :, :], ACT.Exp), x)
    x = tt(delta[:, :, :], first[:, :, D + GH:ROW], top[:, :, :], ALU.subtract, t)
    weigh_first = act.run(lambda e: e.activation(delta[:, :, :], delta[:, :, :], ACT.Exp), x)

    def scaled(of, by, ready):
        h = of[:, :, 0:D].rearrange("p b (h f) -> p b h f", f=GF)
        tt(h, h, by[:, :, :].unsqueeze(3).to_broadcast([P, BLOCKS, GH, GF]), ALU.mult, ready)
        return tt(of[:, :, D:D + GH], of[:, :, D:D + GH], by[:, :, :], ALU.mult)

    lasts = scaled(last, beta, weigh_last)
    parts = [(h * P, (h + 1) * P) for h in range(KD)] + [(D, D + GH)]
    carried = [None] * 3
    for b0, m in windows:
        for h, (lo, hi) in enumerate(parts):
            w, sl = hi - lo, slice(b0 * P, (b0 + m) * P)
            q = bank()
            pe.wait(lasts, rescale, bank_free[q])
            for b in range(m):
                t = pe.run(lambda e: e.transpose(c.banks[q][0:w, b * P:(b + 1) * P], last[:, b0 + b, lo:hi], c.ident[:, :]))
            al = alpha[:, sl]
            if h < KD:
                qa = bank()
                t = pe.run(lambda e: e.matmul(c.banks[qa][:, 0:m * P], c.headsel[:, lo:hi], alpha[:, sl], start=True, stop=True),
                           bank_free[qa])
                al = wide[h][:, 0:m * P]
                bank_free[qa] = act.run(lambda e: e.activation(al, c.banks[qa][:, 0:m * P], ACT.Copy), pe.last(), carried[h])
            carried[h] = bank_free[q] = v.run(lambda e: e.tensor_tensor_scan(
                out=run[h][:, b0 * P + 1:(b0 + m) * P + 1], data0=al, data1=c.banks[q][0:w, 0:m * P],
                initial=run[h][:, b0 * P:b0 * P + 1], op0=ALU.mult, op1=ALU.add), t, carried[h], rescale, bank_free[qa] if h < KD else None)
    firsts = scaled(first, delta, weigh_first)
    used = [None, None]
    for b0, m in windows:
        for h, (lo, hi) in enumerate(parts):
            w = hi - lo
            q = bank()
            u = n % 2
            pe.wait(carried[h], bank_free[q])
            for b in range(m):
                t = pe.run(lambda e: e.transpose(c.banks[q][:, b * w:(b + 1) * w], run[h][:, (b0 + b) * P:(b0 + b + 1) * P],
                                                 c.ident[0:w, 0:w]))
            back = c.banks[q][:, 0:m * w].rearrange("p (b f) -> p b f", b=m)
            heads = slice(h * GH // KD, (h + 1) * GH // KD) if h < KD else slice(0, GH)
            k = heads.stop - heads.start
            by = gamma[:, b0:b0 + m, heads].unsqueeze(3).to_broadcast([P, m, k, w // k])
            o = part[u][:, 0:m, 0:w]
            t = bank_free[q] = tt(o.rearrange("p b (h f) -> p b h f", h=k), back.rearrange("p b (h f) -> p b h f", h=k), by,
                                  ALU.mult, t, used[u])
            to = first[:, b0:b0 + m, lo:hi]
            used[u] = tt(to, to, o, ALU.add, t, firsts)
    s_o.dma(c.sp, lambda e: e.dma_start(frag[0:FAR].rearrange("(b c l) f -> l c b f", c=P, l=NEAR)[0], first[:, :, :]),
            v.last())


def mlp_stage(c, x, xnt_d, xm_d, wqa, bqa, w_fc1, b_fc1, w_fc2, b_fc2, norm_g, norm_b):
    nc = c.nc
    A = nc.alloc_sbuf_tensor
    w1 = A("fc1_w", [P, KD, MLP], F32)
    w2 = A("fc2_w", [P, MT, D], F32)
    gcol = A("fc_gcol", [P, 2, KD], F32)
    b1 = A("fc1_b", [P, MT], F32)
    b2 = A("fc2_b", [P, D], F32)
    xts = [A(f"m_xt{b}", [P, KD, ST * P], F32) for b in range(2)]
    hn = A("m_hn", [P, ST, D], F32)
    xs = A("m_xs", [P, ST, D], F32)
    x2 = A("m_x2", [P, ST, D], F32)
    hnt = A("m_hnt", [P, KD, ST * P], F32)
    hid = A("m_hid", [P, MT, ST * P], F32)
    st = A("m_st", [P, ST, 16], F32)
    s_w, s_xs, s_o = (c.slot(f"m_{n}") for n in ("w", "xs", "o"))
    s_xt = [c.slot(f"m_xt{b}") for b in range(2)]
    v, pe, act, sp = c.dve, c.pe, c.act, c.sp
    s_w.dma(sp, lambda e: e.dma_start(w1[:, :, :], w_fc1.rearrange("(k p) n -> p k n", p=P)))
    s_w.dma(sp, lambda e: e.dma_start(w2[:, :, :], w_fc2.rearrange("(k p) n -> p k n", p=P)))
    s_w.dma(sp, lambda e: e.dma_start(gcol[:, 0, :], norm_g.rearrange("(k p) -> p k", p=P)))
    s_w.dma(sp, lambda e: e.dma_start(gcol[:, 1, :], norm_b.rearrange("(k p) -> p k", p=P)))
    s_w.dma(sp, lambda e: e.dma_start(b1[:, :], b_fc1.rearrange("(k p) -> p k", p=P)))
    w = s_w.dma(sp, lambda e: e.dma_start(b2[:, :], b_fc2.partition_broadcast(P)))
    bank_y, bank_h = (c.banks[7], c.banks[5]), (c.banks[6], c.banks[5])
    pe.wait(w)
    for m in range(MT):
        for k in range(KD):
            t = pe.run(lambda e: e.matmul(bank_y[0][:, m:m + 1], w1[:, k, m * P:(m + 1) * P], gcol[:, 1, k:k + 1],
                                          start=(k == 0), stop=(k == KD - 1)))
    t = v.run(lambda e: e.tensor_tensor(b1[:, :], b1[:, :], bank_y[0][:, 0:MT], ALU.add), t)
    for k in range(KD):
        t = v.run(lambda e: e.tensor_scalar(w1[:, k, :], w1[:, k, :], gcol[:, 0, k:k + 1], None, ALU.mult), t)
    wready = t
    free = {id(c.banks[5]): None, id(c.banks[6]): None, id(c.banks[7]): t}
    xs_used = hnt_used = hid_used = None
    xt_in, xt_used = [None] * 2, [None] * 2
    hn_used = None

    def fetch(k):
        s, n = SUPERS[k]
        b = k % 2
        rows = slice(s * P, (s + n) * P)
        xt_in[b] = s_xt[b].dma(sp, lambda e: e.dma_start(
            xts[b][:, :, 0:n * P], xnt_d.rearrange("(k p) n -> p k n", p=P)[:, :, rows]), xt_used[b])

    fetch(0)
    for si, (s, n) in enumerate(SUPERS):
        u = si % 2
        rows = slice(s * P, (s + n) * P)
        d = s_xs.dma(sp, lambda e: e.dma_start(xs[:, 0:n, :], x[rows].rearrange("(t p) d -> p t d", p=P)), xs_used)
        if si + 1 < len(SUPERS):
            fetch(si + 1)
        v.run(lambda e: e.tensor_tensor(xs[:, 0:n, :], xs[:, 0:n, :], b2[:, :].unsqueeze(1).to_broadcast([P, n, D]),
                                        ALU.add), d, w)
        xt, a = xts[u], xt_in[u]
        for i in range(0, n, 2):
            bank = bank_y[i // 2 % 2]
            pe.wait(a, free[id(bank)])
            for j in range(2):
                for k in range(KD):
                    t = pe.run(lambda e: e.matmul(bank[:, j * D:(j + 1) * D], xt[:, k, (i + j) * P:(i + j + 1) * P], wqa[:, k, :],
                                                  start=(k == 0), stop=(k == KD - 1)))
            yield
            y = free[id(bank)] = v.run(lambda e: e.tensor_tensor(
                x2[:, i:i + 2, :], bank[:, :].rearrange("p (t d) -> p t d", t=2),
                bqa[:, :].unsqueeze(1).to_broadcast([P, 2, D]), ALU.add), t, s_o.last())
        xt_used[u] = t
        normed = yield from every(8, layernorm_steps(c, x2, hn, st, n, [y], [hn_used]))
        yield
        tp_free = [free[id(b)] for b in bank_y]
        turned = turn(c, hn, hnt, n, bank_y, normed, tp_free, hnt_used)
        for b, t in zip(bank_y, tp_free):
            free[id(b)] = t
        hn_used = pe.last()
        yield
        for m in range(MT):
            bank = bank_h[m % 2]
            pe.wait(turned, wready, free[id(bank)])
            for k in range(KD):
                t = pe.run(lambda e: e.matmul(bank[:, 0:n * P], w1[:, k, m * P:(m + 1) * P], hnt[:, k, 0:n * P],
                                              start=(k == 0), stop=(k == KD - 1)))
            hidden = free[id(bank)] = act.run(lambda e: e.activation(
                hid[:, m, 0:n * P], bank[:, 0:n * P], ACT.Gelu, bias=b1[:, m:m + 1]), t, hid_used)
            yield
        hnt_used = t
        for i in range(0, n, 2):
            bank = bank_y[i // 2 % 2]
            pe.wait(hidden, free[id(bank)])
            for j in range(2):
                for m in range(MT):
                    t = pe.run(lambda e: e.matmul(bank[:, j * D:(j + 1) * D], hid[:, m, (i + j) * P:(i + j + 1) * P], w2[:, m, :],
                                                  start=(m == 0), stop=(m == MT - 1)))
            yield
            y = free[id(bank)] = v.run(lambda e: e.tensor_tensor(
                x2[:, i:i + 2, :], bank[:, :].rearrange("p (t d) -> p t d", t=2), x2[:, i:i + 2, :], ALU.add), t)
        hid_used = t
        t = v.run(lambda e: e.tensor_tensor(x2[:, 0:n, :], x2[:, 0:n, :], xs[:, 0:n, :], ALU.add), y, d)
        xs_used = t
        s_o.dma(sp, lambda e: e.dma_start(xm_d[rows].rearrange("(t p) d -> p t d", p=P), x2[:, 0:n, :]), t)
        yield


def pause(steps):
    for _ in range(steps):
        yield


def route_stage(c, xm_d, x1_d, frag, g, sorted_d, gate_w, gate_b, plans, weights, loads):
    nc = c.nc
    A = nc.alloc_sbuf_tensor
    gw = A("e_gw", [P, KD, EXPERTS], F32)
    gb = A("e_gb", [1, EXPERTS], F32)
    NF, NH, W = 3, 4, 2 * ST
    xs = [A(f"e_x{b}", [P, ST, D], F32) for b in range(NF)]
    fr = [A(f"e_fr{b}", [P, ST, ROW], F32) for b in range(NF)]
    rs = A("e_rs", [P, ST, GH], F32)
    hn = [A(f"e_hn{b}", [P, ST, SENT], F32) for b in range(NH)]
    hnt = A("e_hnt", [P, KD, ST * P], F32)
    st = A("e_st", [P, ST, 16], F32)
    lg, pr, key, pos, both = (A(f"e_{n}", [P, W, EXPERTS], F32) for n in ("lg", "pr", "key", "pos", "both"))
    sel = A("e_sel", [P, 2, W, EXPERTS], F32)
    s1 = A("e_s1", [P, W, 3], F32)
    posf = A("e_posf", [P, 2, W], F32)
    before = A("e_before", [P, P], F32)
    rev = A("e_rev", [P, EXPERTS], F32)
    plan_region = [A(f"e_region{i}", [P, EXPERTS], F32) for i in range(len(PARTS))]
    nid = A("e_nid", [P, TILES], F32)
    top, rank, row = A("e_top", [P, 2, W], F32), A("e_rank", [P, 2, W], F32), A("e_row", [P, 2, TILES], I32)
    zero = A("pl_zero", [P, SUB, SENT], F32)
    s_w, s_x, s_x1 = c.slot("e_w"), [c.slot(f"e_x{b}") for b in range(NF)], [c.slot(f"e_x1{b}") for b in range(NF)]
    s_f, s_g = [c.slot(f"e_f{b}") for b in range(NF)], [c.slot(f"e_g{b}") for b in range(NH)]
    v, pe, act, sp, pool = c.dve, c.pe, c.act, c.sp, c.pool
    for to, of in ((gw[:, :, :], gate_w.rearrange("(k p) n -> p k n", p=P)), (gb[:, :], gate_b.unsqueeze(0))):
        w = s_w.dma(sp, lambda e: e.dma_start(to, of))
    t = pool.run(lambda e: e.memset(before[:, :], 1.0))
    pool.run(lambda e: e.affine_select(out=before[:, :], in_=before[:, :], compare_op=ALU.is_gt, fill=0.0, base=0,
                                       pattern=[[1, P]], channel_multiplier=-1), t)
    pool.run(lambda e: e.iota(rev[:, :], pattern=[[-1, EXPERTS]], base=EXPERTS, channel_multiplier=0,
                              allow_small_or_imprecise_dtypes=True))
    pool.run(lambda e: e.iota(nid[:, :], pattern=[[P, TILES]], base=0, channel_multiplier=1,
                              allow_small_or_imprecise_dtypes=True))
    for of, to, r in zip(PARTS, plan_region, plans):
        pool.run(lambda e: e.iota(r["num"][:, :], pattern=[[1, of["slots"]]], base=0, channel_multiplier=0,
                                  allow_small_or_imprecise_dtypes=True))
        pool.run(lambda e: e.iota(to[:, :], pattern=[[of["region"], EXPERTS]], base=of["base"], channel_multiplier=0,
                                  allow_small_or_imprecise_dtypes=True))
    consts = pool.last()
    z = v.run(lambda e: e.memset(zero[:, :, :], 0.0))
    z = pool.run(lambda e: e.iota(zero[:, :, D], pattern=[[1, SUB]], base=2 * N_PAD, channel_multiplier=SUB,
                                  allow_small_or_imprecise_dtypes=True), z)
    zeroed = v.run(lambda e: e.tensor_scalar(zero[:, :, D], zero[:, :, D], -float(N_PAD), None, ALU.add), z)
    carry = carried = None
    bank_t, bank_g, bank_p = c.banks[0:2], c.banks[2], c.banks[3]
    tp_free, g_free, p_free = [None] * 2, None, None
    xin, fin, fr_used, hn_turned = [None] * NF, [None] * NF, [None] * NF, [None] * NH
    hnt_used = None
    x_used = [None] * NF
    logits = {}

    def fetch(k):
        s, n = SUPERS[k]
        b = k % NF
        xin[b] = s_x[b].dma(sp, lambda e: e.dma_start(
            xs[b][:, 0:n, :], xm_d[s * P:(s + n) * P].rearrange("(t p) d -> p t d", p=P)), s_x1[b].last(), x_used[b])
        for i in range(n):
            fin[b] = s_f[b].dma(pool, lambda e: e.indirect_dma_start(
                out=fr[b][:, i, :], out_offset=None, in_=frag[:, :],
                in_offset=bass.IndirectOffsetOnAxis(ap=g["nodeix"][:, s + i:s + i + 1], axis=0)), fr_used[b])

    def front(k, first):
        nonlocal hnt_used
        s, n = SUPERS[k]
        b, h = k % NF, k % NH
        Fr, X = fr[b], xs[b][:, 0:n, :]
        t = v.run(lambda e: e.tensor_scalar(rs[:, 0:n, :], Fr[:, 0:n, D:D + GH], SEG_EPS, None, ALU.add), fin[b])
        yield
        t = v.run(lambda e: e.reciprocal(rs[:, 0:n, :], rs[:, 0:n, :]), t)
        yield
        fv = Fr[:, 0:n, 0:D].rearrange("p t (h f) -> p t h f", f=GF)
        t = v.run(lambda e: e.tensor_tensor(fv, fv, rs[:, 0:n, :].unsqueeze(3).to_broadcast([P, n, GH, GF]), ALU.mult), t)
        yield
        t = v.run(lambda e: e.tensor_tensor(X, X, Fr[:, 0:n, 0:D], ALU.add), t, xin[b])
        fr_used[b] = t
        s_x1[b].dma(act, lambda e: e.dma_start(x1_d[s * P:(s + n) * P].rearrange("(t p) d -> p t d", p=P), X), t)
        yield
        normed = yield from layernorm_steps(c, X, hn[h], st, n, [t], [hn_turned[h], s_g[h].last()])
        x_used[b] = normed
        if k + NF < len(SUPERS):
            fetch(k + NF)
        yield
        turned = turn(c, hn[h], hnt, n, bank_t, normed, tp_free, hnt_used)
        hn_turned[h] = pe.last()
        yield from pause(3)
        pe.wait(w, turned, g_free)
        first *= ST
        for i in range(n):
            o = bank_g[:, (first + i) * EXPERTS:(first + i + 1) * EXPERTS]
            for kk in range(KD):
                pe.run(lambda e: e.matmul(o, hnt[:, kk, i * P:(i + 1) * P], gw[:, kk, :], start=(kk == 0), stop=False))
            logits[k] = hnt_used = pe.run(lambda e: e.matmul(o, c.ones[0:1, :], gb[:, :], start=False, stop=True))

    def back(part, ks):
        nonlocal carried, p_free, g_free
        s, n = SUPERS[ks[0]][0], sum(SUPERS[k][1] for k in ks)
        yield from pause(8)
        L, Pr, K, B = (a[:, 0:n, :] for a in (lg, pr, key, both))
        t = v.run(lambda e: e.tensor_copy(L, bank_g[:, 0:n * EXPERTS].rearrange("p (t e) -> p t e", t=n)), logits[ks[-1]])
        g_free = t
        yield
        wide = lambda a: a.to_broadcast([P, n, EXPERTS])
        over_tiles = lambda a: a.unsqueeze(1).to_broadcast([P, n, EXPERTS])
        t = v.run(lambda e: e.tensor_reduce(s1[:, 0:n, 0], L, AX, ALU.max), t)
        yield
        t = v.run(lambda e: e.tensor_tensor(L, L, wide(s1[:, 0:n, 0:1]), ALU.subtract), t)
        yield
        t = act.run(lambda e: e.activation(Pr, L, ACT.Exp), t)
        yield from pause(6)
        t = v.run(lambda e: e.tensor_reduce(s1[:, 0:n, 1], Pr, AX, ALU.add), t)
        yield
        t = v.run(lambda e: e.reciprocal(s1[:, 0:n, 2], s1[:, 0:n, 1]), t)
        yield
        t = v.run(lambda e: e.tensor_tensor(Pr, Pr, wide(s1[:, 0:n, 2:3]), ALU.mult), t)
        yield
        for j in range(2):
            T, R = top[:, j, 0:n], rank[:, j, 0:n]
            S = sel[:, j, 0:n, :]
            t = v.run(lambda e: e.tensor_reduce(T, Pr, AX, ALU.max), t)
            yield
            t = v.run(lambda e: e.tensor_tensor(K, Pr, wide(T.unsqueeze(2)), ALU.is_equal), t)
            yield
            t = v.run(lambda e: e.tensor_tensor(K, K, over_tiles(rev[:, :]), ALU.mult), t, consts)
            yield
            t = v.run(lambda e: e.tensor_reduce(R, K, AX, ALU.max), t)
            yield
            t = v.run(lambda e: e.tensor_tensor(S, K, wide(R.unsqueeze(2)), ALU.is_equal), t)
            yield
            if j == 0:
                t = v.run(lambda e: e.scalar_tensor_tensor(out=Pr, in0=S, scalar=-2.0, in1=Pr, op0=ALU.mult, op1=ALU.add), t)
                yield
        t = v.run(lambda e: e.tensor_tensor(B, sel[:, 0, 0:n, :], sel[:, 1, 0:n, :], ALU.add), t)
        Bf = B.rearrange("p t e -> p (t e)")
        pe.wait(t, p_free)
        pe.run(lambda e: e.matmul(bank_p[:, 0:n * EXPERTS], before[:, :], Bf, start=True, stop=True))
        t = pe.run(lambda e: e.matmul(bank_p[:, P:P + n * EXPERTS], c.ones[:, :], Bf, start=True, stop=True))
        yield from pause(8)
        for i in range(n):
            v.run(lambda e: e.tensor_tensor(pos[:, i, :], bank_p[:, i * EXPERTS:(i + 1) * EXPERTS], carry[:, :],
                                            ALU.add), t, carried)
            t = carried = v.run(lambda e: e.tensor_tensor(carry[:, :], carry[:, :],
                                                          bank_p[:, P + i * EXPERTS:P + (i + 1) * EXPERTS], ALU.add), t)
            yield
        p_free = t
        t = v.run(lambda e: e.tensor_tensor(pos[:, 0:n, :], pos[:, 0:n, :], over_tiles(plan_region[part][:, :]), ALU.add), t)
        yield
        for j in range(2):
            x = v.run(lambda e: e.tensor_tensor(K, pos[:, 0:n, :], sel[:, j, 0:n, :], ALU.mult), t)
            yield
            t = v.run(lambda e: e.tensor_reduce(posf[:, j, 0:n], K, AX, ALU.add), x)
            yield
        t = v.run(lambda e: e.tensor_copy(row[:, :, s:s + n], posf[:, :, 0:n]), t)
        for k in ks:
            ks_, kn = SUPERS[k]
            o, to = ks_ - s, hn[k % NH]
            for col, of in ((0, nid[:, ks_:ks_ + kn]), (1, top[:, 0, o:o + kn]), (2, top[:, 1, o:o + kn]), (3, rank[:, 0, o:o + kn])):
                t = v.run(lambda e: e.tensor_copy(to[:, 0:kn, D + col], of), t, s_g[k % NH].last(), consts)
        for k in ks:
            s, n = SUPERS[k]
            for i in range(n):
                for j in range(2):
                    s_g[k % NH].dma(pool, lambda e: e.indirect_dma_start(
                        out=sorted_d[:, :], out_offset=bass.IndirectOffsetOnAxis(ap=row[:, j, s + i:s + i + 1], axis=0),
                        in_=hn[k % NH][:, i, :], in_offset=None), t)
                yield

    for k in range(NF):
        fetch(k)
    loads = iter(loads)
    for part, of in enumerate(PARTS):
        r = plans[part]
        carry = r["count"]
        carried = v.run(lambda e: e.memset(carry[:, :], 0.0))
        pairs = [of["supers"][i:i + 2] for i in range(0, len(of["supers"]), 2)]
        for q in range(len(pairs) + 1):
            behind = back(part, pairs[q - 1]) if q else iter(())
            for i, k in enumerate(pairs[q] if q < len(pairs) else ()):
                for load in (next(loads, None), next(loads, None)):
                    if load:
                        weights.dma(sp, lambda e: e.dma_start(*load))
                for _ in front(k, i):
                    next(behind, None)
                    yield
            for _ in behind:
                yield
        r["x1"] = [x.last() for x in s_x1]
        yield from plan_steps(c, r, of, plan_region[part], zero, zeroed, consts, carried, sorted_d, [x.last() for x in s_g])
        yield r


def plan_buffers(c, n):
    A, slots = c.nc.alloc_sbuf_tensor, PARTS[n]["slots"]
    b = {"count": A(f"r{n}_count", [P, EXPERTS], F32), "rev": A(f"r{n}_rev", [P, slots], F32),
         "expert": A(f"r{n}_expert", [1, slots], I32), "tile_row": A(f"r{n}_tile_row", [1, slots], I32),
         "ci": A(f"pl{n}_ci", [P, EXPERTS], I32), "endrow": A(f"pl{n}_endrow", [1, EXPERTS], I32), "part": n}
    b.update({k: A(f"pl{n}_{k}", [P, EXPERTS], F32) for k in ("tiles", "ends", "starts", "shift", "step")})
    b.update({k: A(f"pl{n}_{k}", [P, slots], F32) for k in ("num", "ge", "row", "ex")})
    return b


def plan_steps(c, r, of, region, zero, zeroed, numbered, counted, sorted_d, sent):
    v, sp = c.dve, c.sp
    ci, endrow, tiles, ends, starts, shift, step, num, ge, row, ex = (
        r[k] for k in ("ci", "endrow", "tiles", "ends", "starts", "shift", "step", "num", "ge", "row", "ex"))
    s_z = c.slot(f"pl_z{r['part']}")
    rows = lambda a: a.rearrange("(p t) d -> p t d", t=SUB)
    s_z.dma(sp, lambda e: e.dma_start(rows(sorted_d[of["zeros"]:of["zeros"] + ET, :]), zero[:, :, :]), zeroed)
    t = v.run(lambda e: e.tensor_tensor(endrow[:, :], region[0:1, :], r["count"][0:1, :], ALU.add), counted)
    yield
    sp.wait(t)
    for k in range(EXPERTS):
        lo = of["base"] + k * of["region"]
        at = sp.engine.value_load(endrow[0:1, k:k + 1], min_val=lo, max_val=lo + of["region"] - ET)
        s_z.dma(sp, lambda e: e.dma_start(rows(sorted_d[bass.ds(at, ET), :]), zero[:, :, :]))
    t = v.run(lambda e: e.tensor_scalar(ci[:, :], r["count"][:, :], float(ET - 1), None, ALU.add), counted)
    yield
    t = v.run(lambda e: e.tensor_single_scalar(ci[:, :], ci[:, :], ET.bit_length() - 1, ALU.logical_shift_right), t)
    yield
    t = v.run(lambda e: e.tensor_copy(tiles[:, :], ci[:, :]), t)
    yield
    t = v.run(lambda e: e.tensor_tensor_scan(out=ends[:, :], data0=c.ones[:, 0:EXPERTS], data1=tiles[:, :], initial=0.0,
                                             op0=ALU.mult, op1=ALU.add), t)
    t = v.run(lambda e: e.tensor_tensor(starts[:, :], ends[:, :], tiles[:, :], ALU.subtract), t)
    yield
    t = v.run(lambda e: e.scalar_tensor_tensor(out=shift[:, :], in0=starts[:, :], scalar=float(ET), in1=region[:, :],
                                               op0=ALU.mult, op1=ALU.subtract), t, numbered)
    v.run(lambda e: e.tensor_copy(step[:, 0:1], shift[:, 0:1]), t)
    yield
    t = v.run(lambda e: e.tensor_tensor(step[:, 1:], shift[:, 1:], shift[:, 0:EXPERTS - 1], ALU.subtract), t)
    yield
    e1 = v.run(lambda e: e.memset(ex[:, :], 0.0))
    yield
    t = v.run(lambda e: e.tensor_scalar(row[:, :], num[:, :], float(ET), float(of["base"]), ALU.mult, ALU.add), t)
    yield
    for k in range(1, EXPERTS):
        q = v.run(lambda e: e.tensor_scalar(ge[:, :], num[:, :], starts[:, k:k + 1], None, ALU.is_ge), t, e1)
        yield
        e1 = v.run(lambda e: e.tensor_tensor(ex[:, :], ex[:, :], ge[:, :], ALU.add), q)
        yield
        q = v.run(lambda e: e.tensor_scalar(ge[:, :], ge[:, :], step[:, k:k + 1], None, ALU.mult), e1)
        yield
        t = v.run(lambda e: e.tensor_tensor(row[:, :], row[:, :], ge[:, :], ALU.subtract), q)
        yield
    v.run(lambda e: e.tensor_copy(r["expert"][:, :], ex[0:1, :]), e1)
    yield
    v.run(lambda e: e.tensor_scalar(r["rev"][:, :], ex[:, :], -1.0, float(EXPERTS), ALU.mult, ALU.add), e1)
    yield
    zrow = float(of["zeros"])
    q = v.run(lambda e: e.tensor_scalar(ge[:, :], num[:, :], ends[:, EXPERTS - 1:EXPERTS], None, ALU.is_lt), t)
    yield
    t = v.run(lambda e: e.tensor_scalar(row[:, :], row[:, :], -zrow, None, ALU.add), t)
    yield
    t = v.run(lambda e: e.tensor_tensor(row[:, :], row[:, :], ge[:, :], ALU.mult), t, q)
    yield
    t = v.run(lambda e: e.tensor_scalar(r["tile_row"][:, :], row[0:1, :], zrow, None, ALU.add), t)
    yield
    r["planned"], r["filled"] = v.last(), [s_z.last()] + sent


def expert_buffers(c, eb1, eb2):
    A = c.nc.alloc_sbuf_tensor
    pair = lambda name, shape, n=2, dt=F32: [A(f"x_{name}{b}", shape, dt) for b in range(n)]
    b = {"b1": A("x_b1", [P, EXPERTS, HT], F32), "b2": A("x_b2", [P, EXPERTS, D], F32), "gin": pair("in", [P, SUB, SENT]),
         "gt": pair("int", [P, KD, ET]), "w1c": pair("w1c", [P, KD, HID]), "b1c": pair("b1c", [P, HT]),
         "ht": pair("ht", [P, HT, ET]), "dest": pair("dest", [P, SUB], NOUT + 1, I32), "scale": pair("scale", [P, SUB], NOUT + 1),
         "isf": A("x_isf", [P, SUB], F32), "df": A("x_df", [P, SUB], F32), "pad": A("x_pad", [P, SUB], F32),
         "y": pair("y", [P, SUB, D], NOUT), "s_in": [c.slot(f"x_in{b}") for b in range(2)], "s_y": [c.slot(f"x_y{b}") for b in range(NOUT)]}
    s_b = c.slot("x_b")
    s_b.dma(c.sp, lambda e: e.dma_start(b["b1"][:, :, :], eb1.rearrange("e (k p) -> p e k", p=P)))
    b["bias"] = s_b.dma(c.sp, lambda e: e.dma_start(b["b2"][:, :, :].rearrange("p e n -> p (e n)"),
                                                    eb2.rearrange("e n -> (e n)").partition_broadcast(P)))
    b["done"] = [{} for _ in range(9)]
    return b


def experts_stage(c, bufs, plans, sorted_d, result_d, w1, w2, weights):
    b1, b2, gin, gt, w1c, b1c, ht, dest, scale, isf, df, pad, y, s_in, s_y, bias = (bufs[k] for k in (
        "b1", "b2", "gin", "gt", "w1c", "b1c", "ht", "dest", "scale", "isf", "df", "pad", "y", "s_in", "s_y", "bias"))
    v, pe, act, sp = c.dve, c.pe, c.act, c.sp
    in_bank, h_bank, y_bank = c.banks[4], c.banks[5:7], c.banks[7]
    loaded, in_turned, in_ready, fc1_done, fc2_done, hidden, y_read, copied, aimed = bufs["done"]
    tiles = [(p, i) for p, of in enumerate(PARTS) for i in range(of["slots"])]
    rows = lambda a: a.rearrange("(t p) d -> p t d", p=P)

    def expert(lane, j):
        p, i = tiles[j]
        lane.wait(plans[p]["planned"])
        return lane.engine.value_load(plans[p]["expert"][0:1, i:i + 1], min_val=0, max_val=EXPERTS - 1)

    def fetch(j):
        p, i = tiles[j]
        sp.wait(plans[p]["planned"], plans[p]["filled"])
        at = sp.engine.value_load(plans[p]["tile_row"][0:1, i:i + 1], min_val=PARTS[p]["base"], max_val=PARTS[p]["zeros"])
        loaded[j] = s_in[j % 2].dma(sp, lambda e: e.dma_start(gin[j % 2][:, :, :], rows(sorted_d[bass.ds(at, ET), :])),
                                    in_turned.get(j - 2), aimed.get(j - 2))

    def copy_first(j):
        u = j % 2
        ex = expert(v, j)
        v.wait(weights, bias, fc1_done.get(j - 2), hidden.get(j - 2))
        v.run(lambda e: e.tensor_copy(w1c[u][:, :, :], w1[:, bass.ds(ex * KD, KD), :]))
        copied[j] = v.run(lambda e: e.tensor_copy(b1c[u][:, :], b1[:, bass.ds(ex, 1), :].rearrange("p a k -> p (a k)")))

    def aim(j):
        u = j % 2
        tail = lambda col: gin[u][:, :, D + col]
        t = v.run(lambda e: e.tensor_scalar(isf[:, :], tail(3), plans[tiles[j][0]]["rev"][:, tiles[j][1]:tiles[j][1] + 1], None, ALU.is_equal), loaded[j], aimed.get(j - 1))
        x = v.run(lambda e: e.tensor_scalar(df[:, :], isf[:, :], -float(N_PAD), float(N_PAD), ALU.mult, ALU.add), t)
        p = v.run(lambda e: e.tensor_scalar(pad[:, :], tail(3), 0.0, float(j * ET), ALU.is_equal, ALU.mult), v.last())
        x = v.run(lambda e: e.tensor_tensor(df[:, :], df[:, :], pad[:, :], ALU.add), p)
        v.run(lambda e: e.tensor_tensor(dest[j % (NOUT + 1)][:, :], df[:, :], tail(0), ALU.add), x, s_y[(j - NOUT - 1) % NOUT].last())
        x = v.run(lambda e: e.tensor_tensor(df[:, :], tail(1), tail(2), ALU.subtract), v.last())
        x = v.run(lambda e: e.tensor_tensor(df[:, :], df[:, :], isf[:, :], ALU.mult), x)
        aimed[j] = v.run(lambda e: e.tensor_tensor(scale[j % (NOUT + 1)][:, :], df[:, :], tail(2), ALU.add), x)

    def turn_in(j):
        u = j % 2
        pe.wait(loaded[j], in_ready.get(j - 1))
        for k in range(KD):
            for i in range(SUB):
                in_turned[j] = pe.run(lambda e: e.transpose(in_bank[:, k * ET + i * P:k * ET + (i + 1) * P],
                                                            gin[u][:, i, k * P:(k + 1) * P], c.ident[:, :]))
        in_ready[j] = act.run(lambda e: e.activation(gt[u][:, :, :], in_bank[:, :].rearrange("p (k n) -> p k n", k=KD),
                                                     ACT.Copy), in_turned[j], fc1_done.get(j - 2))

    def first(j):
        u = j % 2
        pe.wait(in_ready[j], copied[j], hidden.get(j - 1))
        for m in range(HT):
            out = h_bank[m * 2 // HT][:, m % 2 * ET:(m % 2 + 1) * ET]
            for k in range(KD):
                fc1_done[j] = pe.run(lambda e: e.matmul(out, w1c[u][:, k, m * P:(m + 1) * P], gt[u][:, k, :],
                                                        start=(k == 0), stop=(k == KD - 1)))
            if m % 2:
                for mm in (m - 1, m):
                    out = h_bank[mm * 2 // HT][:, mm % 2 * ET:(mm % 2 + 1) * ET]
                    hidden[j] = act.run(lambda e: e.activation(ht[u][:, mm, :], out, ACT.Gelu, bias=b1c[u][:, mm:mm + 1]),
                                        fc1_done[j], fc2_done.get(j - 2))

    def second(j):
        u = j % 2
        ex = expert(pe, j)
        pe.wait(hidden[j], weights, y_read.get(j - 1))
        for i in range(SUB):
            for m in range(HT):
                fc2_done[j] = pe.run(lambda e: e.matmul(y_bank[:, i * D:(i + 1) * D], ht[u][:, m, i * P:(i + 1) * P],
                                                        w2[:, bass.ds(ex * HT + m, 1), :], start=(m == 0), stop=(m == HT - 1)))

    def store(j):
        u = j % NOUT
        ex = expert(v, j)
        y_read[j] = v.run(lambda e: e.tensor_tensor(y[u][:, :, :], y_bank[:, :].rearrange("p (t d) -> p t d", t=SUB),
                                                    b2[:, bass.ds(ex, 1), :].to_broadcast([P, SUB, D]), ALU.add),
                          fc2_done[j], bias, s_y[u].last())
        t = v.run(lambda e: e.tensor_tensor(y[u][:, :, :], y[u][:, :, :],
                                            scale[j % (NOUT + 1)][:, :].unsqueeze(2).to_broadcast([P, SUB, D]), ALU.mult), y_read[j], aimed[j])
        for i in range(SUB):
            s_y[u].dma(c.pool, lambda e: e.indirect_dma_start(
                out=result_d[:, :], out_offset=bass.IndirectOffsetOnAxis(ap=dest[j % (NOUT + 1)][:, i:i + 1], axis=0),
                in_=y[u][:, i, :], in_offset=None), t)

    def start(j):
        copy_first(j)
        turn_in(j)
        aim(j)

    last = 0
    for p, of in enumerate(PARTS):
        lo, last = last, last + of["slots"]
        fetch(lo)
        fetch(lo + 1)
        start(lo)
        for j in range(lo, last + 1):
            if j < last:
                first(j)
                yield p
            if j + 1 < last:
                start(j + 1)
                yield p
            if j + 2 < last:
                fetch(j + 2)
            if j > lo:
                second(j - 1)
                yield p
                store(j - 1)
        bufs["stored", p] = [x.last() for x in s_y]
        yield None


def combine_steps(c, p, ys, xs, slots, result_d, x1_d, out, ready):
    s_y, s_o = slots
    v, NB = c.dve, len(ys)
    used, here = [None] * NB, [None] * NB
    supers = [SUPERS[k] for k in PARTS[p]["supers"]]

    def fetch(k):
        s, n = supers[k]
        b = k % NB
        c.sp.wait(ready)
        rows = lambda a, lo: a[lo:lo + n * P].rearrange("(t p) d -> p t d", p=P)
        for j in range(2):
            s_y[b].dma(c.sp, lambda e: e.dma_start(ys[b][:, j, 0:n, :], rows(result_d, j * N_PAD + s * P)), used[b])
        here[b] = s_y[b].dma(c.sp, lambda e: e.dma_start(xs[b][:, 0:n, :], rows(x1_d, s * P)), s_o[b].last())

    for k in range(NB - 1):
        fetch(k)
    yield
    for k, (s, n) in enumerate(supers):
        b = k % NB
        if k + NB - 1 < len(supers):
            fetch(k + NB - 1)
        yield
        t = here[b]
        X = xs[b][:, 0:n, :]
        for j in range(2):
            t = v.run(lambda e: e.tensor_tensor(X, X, ys[b][:, j, 0:n, :], ALU.add), t)
            yield
        used[b] = t
        lo, hi = s * P, min((s + n) * P, N_NODES)
        full = (hi - lo) // P
        s_o[b].dma(c.sp, lambda e: e.dma_start(out[lo:lo + full * P].rearrange("(t p) d -> p t d", p=P), xs[b][:, 0:full, :]), t)
        if hi - lo > full * P:
            s_o[b].dma(c.sp, lambda e: e.dma_start(out[lo + full * P:hi], xs[b][0:hi - lo - full * P, full, :]), t)
        yield


def build(nc, a, out, stop=None):
    c = Core(nc)
    dram = lambda name, shape: nc.dram_tensor(name, shape, F32, kind="Internal").ap()
    table = dram("table", [N_PAD, ROW])
    xnt_d = dram("xnt_d", [D, N_PAD])
    xm_d = dram("xm_d", [N_PAD, D])
    frag = dram("frag", [FRAGS, ROW])
    rows_d = dram("rows_d", [2, CHUNKS])
    x1_d = dram("x1_d", [N_PAD, D])
    keys_d = dram("keys_d", [BLOCKS, 2 * P])
    sorted_d = dram("sorted_d", [PARTS[-1]["end"], SENT])
    result_d = dram("result_d", [2 * N_PAD + SLOTS * ET, D])
    sdst_d = dram("sdst_d", [2, CHUNKS, GH])
    A = nc.alloc_sbuf_tensor
    constants(c)
    nodeix = A("nodeix", [P, TILES], I32)
    keep = nc.sbuf_base
    gram = A("gram", [P, KD, D + 1], F32)
    wqa, bqa = A("wqa", [P, KD, D], F32), A("bqa", [P, D], F32)
    g = {"dfb": A("dfb", [P, CHUNKS], F32), "dlb": A("dlb", [P, CHUNKS], F32), "loc": A("loc", [P, CHUNKS], F32),
         "srcix": A("srcix", [P, CHUNKS], I32), "sdedge": A("sdedge", [P, 2, GROUPS], F32),
         "lastix": A("lastix", [P, BLOCKS], I32), "nodeix": nodeix,
         "far": A("far", [1, CHUNKS], I32), "anyfar": A("anyfar", [1, GROUPS], I32)}
    c.fence()
    src, dst = (a[n].rearrange("(c e) -> c e", e=P) for n in ("src", "dst"))
    mark = nc.sbuf_base
    fli = index_buffers(nc)
    mark_ix = nc.sbuf_base
    index = index_steps(c, dst, src, rows_d, keys_d, fli, g)
    nodes_stage(c, a["x"], frag, table, xnt_d, a["L0_gnn_W"], a["L0_gnn_a_src"], a["L0_gnn_a_dst"], gram, index)
    c.fence()
    nc.sbuf_base = mark_ix
    edges = edges_stage(c, dst, src, table, frag, g)
    slots = len(c.slots)
    next(edges)
    group_slots = c.slots[slots:]
    mark_mlp = nc.sbuf_base
    ends = edge_scores_stage(c, table, sdst_d, fli, g)
    next(ends)
    next(edges)
    mix_weights_stage(c, gram, a["L0_mix_w_qkv"], a["L0_mix_b_qkv"], wqa, bqa)
    for _ in ends:
        pass
    c.fence(but=group_slots)
    nc.sbuf_base = mark_mlp
    mlp = mlp_stage(c, a["x"], xnt_d, xm_d, wqa, bqa, *(a[f"L0_mix_{n}"] for n in (
        "w_fc1", "b_fc1", "w_fc2", "b_fc2", "norm_g", "norm_b")))
    done = 0
    for step, _ in enumerate(edges, 1):
        while done * 4 * GROUPS < step * MLP_STEPS:
            next(mlp, None)
            done += 1
    for _ in mlp:
        pass
    c.fence()
    nc.sbuf_base = mark
    merge_stage(c, frag, g)
    c.fence()
    nc.sbuf_base = keep
    ffn = {n: a[f"L0_ffn_{n}"] for n in ("gate_w", "gate_b", "W1", "b1", "W2", "b2")}
    w1 = A("e_w1", [P, EXPERTS * KD, HID], F32)
    w2 = A("e_w2", [P, EXPERTS * HT, D], F32)
    weights = c.slot("expert_w")
    loads = [(to[:, e * n:(e + 1) * n, :], ffn[name][e].rearrange("(k p) n -> p k n", p=P))
             for to, name, n in ((w1, "W1", KD), (w2, "W2", HT)) for e in range(EXPERTS)]
    plans = [plan_buffers(c, n) for n in range(len(PARTS))]
    route = route_stage(c, xm_d, x1_d, frag, g, sorted_d, ffn["gate_w"], ffn["gate_b"], plans, weights, loads)
    next(route)
    bufs = expert_buffers(c, ffn["b1"], ffn["b2"])
    NY = 3
    ys = [A(f"c_y{b}", [P, 2, ST, D], F32) for b in range(NY)]
    xs = [A(f"c_x{b}", [P, ST, D], F32) for b in range(NY)]
    combine_slots = [c.slot(f"c_y{b}") for b in range(NY)], [c.slot(f"c_o{b}") for b in range(NY)]
    for step in route:
        if step:
            break
    tiles = experts_stage(c, bufs, plans, sorted_d, result_d, w1, w2, weights.last())
    combine = lambda p: combine_steps(c, p, ys, xs, combine_slots, result_d, x1_d, out,
                                      bufs["stored", p] + plans[p]["x1"])
    for part in tiles:
        if part is None:
            break
        for _ in range(ROUTE_STEPS):
            next(route, None)
    for _ in route:
        pass
    sums = combine(0)
    for n, part in enumerate(tiles):
        if n % 2:
            next(sums, None)
    for _ in sums:
        pass
    for _ in combine(1):
        pass
    c.fence()


_INS = ["x", "src", "dst", "L0_gnn_W", "L0_gnn_a_src", "L0_gnn_a_dst", "L0_mix_w_qkv", "L0_mix_b_qkv",
        "L0_mix_norm_g", "L0_mix_norm_b", "L0_mix_w_fc1", "L0_mix_b_fc1", "L0_mix_w_fc2", "L0_mix_b_fc2",
        "L0_ffn_gate_w", "L0_ffn_gate_b", "L0_ffn_W1", "L0_ffn_b1", "L0_ffn_W2", "L0_ffn_b2"]


def kernel(**inputs):
    import concourse.bacc as _bacc
    from concourse.bass_utils import run_bass_kernel_spmd as _run

    nc = _bacc.Bacc("TRN2", target_bir_lowering=False, num_devices=1)
    arrays, aps = {}, {}
    pads = {"x": (N_PAD - N_NODES, 0), "src": (CHUNKS * P - N_EDGES, N_NODES), "dst": (CHUNKS * P - N_EDGES, N_NODES)}
    for name in _INS:
        v = np.ascontiguousarray(inputs[name])
        if name in pads:
            more, fill = pads[name]
            v = np.concatenate([v, np.full((more,) + v.shape[1:], fill, v.dtype)])
        arrays[f"in_{name}"] = v
        aps[name] = nc.dram_tensor(f"in_{name}", v.shape, mybir.dt.from_np(v.dtype), kind="ExternalInput").ap()
    out = nc.dram_tensor("out_0", (N_NODES, D), F32, kind="ExternalOutput").ap()
    with nc.allow_non_contiguous_dma(reason="small strided loads, once"):
        build(nc, aps, out)
    r = _run(nc, [arrays], core_ids=[0])
    return r.results[0]["out_0"]
```
